# Optimizing a Trainium2 kernel written in Bass

```python
import numpy as np
import jax
import jax.numpy as jnp

def _softmax(x, axis=-1):
    return jax.nn.softmax(x, axis=axis)

def _gelu(x):
    return jax.nn.gelu(x, approximate=True)

def _silu(x):
    return jax.nn.silu(x)

def _sigmoid(x):
    return jax.nn.sigmoid(x)

def _layernorm(x, axis=-1, eps=1e-05):
    m = jnp.mean(x, axis=axis, keepdims=True)
    v = jnp.var(x, axis=axis, keepdims=True)
    return (x - m) / jnp.sqrt(v + eps)

def _scatter_add(tgt, idx, src, axis=0):
    return tgt.at[idx].add(src)

def _segment_sum(src, seg, n):
    return jax.ops.segment_sum(src, seg, n)
kernel_name = 'mk_adj_resnorm_d4_adj_r2_ca3f7f'

def setup_inputs(seed: int=0):
    np.random.seed(seed)
    _w = jnp.asarray

    def _rec_inputs():
        import jax
        import jax.numpy as jnp
        _gk = jax.random.key(seed)
        x = 7.22e-05 + 1 * jax.random.normal(jax.random.fold_in(_gk, 1), (8, 2048, 64), jnp.float32)
        _a = jax.random.bernoulli(jax.random.fold_in(_gk, 2), 0.00390625, (2048, 2048))
        adj = _a.astype(jnp.int32)
        return (x, adj)
    x, adj = _rec_inputs()

    def _L0_gnn_setup():
        import jax, jax.numpy as jnp
        import numpy as np
        B, N, F_IN, F_OUT = (32, 2048, 64, 64)
        ALPHA = 0.2

        def _xavier(key, shape, gain=1.414):
            fan_in, fan_out = (shape[0], shape[1])
            bound = gain * np.sqrt(6.0 / (fan_in + fan_out))
            return jax.random.uniform(key, shape, jnp.float32, -bound, bound)
        key = jax.random.key(seed)
        k1, k2, k3, k4 = jax.random.split(key, 4)
        inp = jax.random.normal(k1, (B, N, F_IN), jnp.float32)
        W = _xavier(k2, (F_IN, F_OUT))
        a = _xavier(k3, (2 * F_OUT, N))
        adj = jax.random.randint(k4, (N, N), 0, 2, jnp.int32)
        return {'inp': inp, 'W': W, 'a': a, 'adj': adj}
    _L0_gnn_all = _L0_gnn_setup()
    _L0_gnn_in = {k: v for k, v in _L0_gnn_all.items() if k in ('W', 'a')}
    del _L0_gnn_all

    def _L1_gnn_setup():
        import jax, jax.numpy as jnp
        import numpy as np
        import math
        INPUT_SIZE = 64
        key = jax.random.key(seed)
        k1, k2 = jax.random.split(key)
        B, N, D = (32, 1024, INPUT_SIZE)
        x = jax.random.normal(k1, (B, N, D), dtype=jnp.float32)
        adj = jax.random.randint(k2, (N, N), 0, 2, dtype=jnp.int32)
        return {'input': x, 'adj': adj}
    _L1_gnn_all = _L1_gnn_setup()
    _L1_gnn_in = {k: v for k, v in _L1_gnn_all.items() if k in ()}
    del _L1_gnn_all

    def _L2_gnn_setup():
        import jax, jax.numpy as jnp
        import numpy as np
        ALPHA = 0.2
        NEG_INF = -1e+30
        key = jax.random.key(seed)
        k1, k2, k3, k4 = jax.random.split(key, 4)
        B, N, Din, Dout = (8, 1024, 64, 64)
        x = jax.random.normal(k1, (B, N, Din), dtype=jnp.float32)
        adj = jax.random.randint(k2, (N, N), 0, 2, dtype=jnp.int32)
        W = jax.random.normal(k3, (Din, Dout), dtype=jnp.float32) * (1.0 / np.sqrt(Din))
        a = jax.random.normal(k4, (2 * Dout,), dtype=jnp.float32) * 0.1
        return {'x': x, 'adj': adj, 'W': W, 'a': a}
    _L2_gnn_all = _L2_gnn_setup()
    _L2_gnn_in = {k: v for k, v in _L2_gnn_all.items() if k in ('W', 'a')}
    del _L2_gnn_all

    def _L3_gnn_setup():
        import jax, jax.numpy as jnp
        import numpy as np
        ALPHA = 0.2
        NEG_INF = -9000000000000000.0
        key = jax.random.key(seed)
        k1, k2, k3, k4 = jax.random.split(key, 4)
        B, N, Fin, Fout = (8, 1024, 64, 64)
        inp = jax.random.normal(k1, (B, N, Fin), dtype=jnp.float32)
        adj = jax.random.randint(k2, (N, N), 0, 2, dtype=jnp.int32)
        W = jax.random.normal(k3, (Fin, Fout), dtype=jnp.float32) * np.sqrt(2.0 / Fout)
        a = jax.random.normal(k4, (2 * Fout, 1), dtype=jnp.float32) * np.sqrt(2.0 / (2 * Fout + 1))
        return {'input': inp, 'adj': adj, 'W': W, 'a': a}
    _L3_gnn_all = _L3_gnn_setup()
    _L3_gnn_in = {k: v for k, v in _L3_gnn_all.items() if k in ('W', 'a')}
    del _L3_gnn_all
    return {'x': x, 'adj': adj, 'L0_gnn_W': _L0_gnn_in['W'], 'L0_gnn_a': _L0_gnn_in['a'], 'L2_gnn_W': _L2_gnn_in['W'], 'L2_gnn_a': _L2_gnn_in['a'], 'L3_gnn_W': _L3_gnn_in['W'], 'L3_gnn_a': _L3_gnn_in['a']}

def reference(x, adj, L0_gnn_W, L0_gnn_a, L2_gnn_W, L2_gnn_a, L3_gnn_W, L3_gnn_a):
    import jax
    import jax.numpy as jnp

    def _L0_gnn_ref(inp, W, a, adj):
        import jax, jax.numpy as jnp
        import numpy as np
        B, N, F_IN, F_OUT = (32, 2048, 64, 64)
        ALPHA = 0.2

        def _xavier(key, shape, gain=1.414):
            fan_in, fan_out = (shape[0], shape[1])
            bound = gain * np.sqrt(6.0 / (fan_in + fan_out))
            return jax.random.uniform(key, shape, jnp.float32, -bound, bound)
        h = jnp.matmul(inp, W)
        h = h.at[:, 0, :].set(0.0)
        Do = W.shape[0] if False else W.shape[1]
        mask = (adj[1:, :] > 0).astype(h.dtype)
        h2 = jnp.einsum('ji,bjd->bid', mask, h[:, :-1, :])
        a1, a2 = (a[:Do, :], a[Do:, :])
        score = jnp.einsum('bid,di->bi', h, a1) + jnp.einsum('bid,di->bi', h2, a2)
        score = score.at[:, 0].set(0.0)
        hsum = jnp.sum(h, axis=1, keepdims=True)
        h_prime = score[:, :, None] * hsum
        return jnp.where(h_prime >= 0, h_prime, ALPHA * h_prime)

    def _L1_gnn_ref(input, adj):
        import jax, jax.numpy as jnp
        import numpy as np
        import math
        INPUT_SIZE = 64
        scale = 1.0 / math.sqrt(INPUT_SIZE)
        scores = jnp.einsum('bnd,bmd->bnm', input, input) * scale
        neg = jnp.float32(-1000000000000.0)
        masked = jnp.where(adj > 0, scores, neg)
        attn = jax.nn.softmax(masked, axis=-1)
        out = jnp.einsum('bnm,bmd->bnd', attn, input)
        return out

    def _L2_gnn_ref(x, adj, W, a):
        import jax, jax.numpy as jnp
        import numpy as np
        ALPHA = 0.2
        NEG_INF = -1e+30
        Dout = W.shape[1]
        h = jnp.einsum('bnd,de->bne', x, W)
        a1, a2 = (a[:Dout], a[Dout:])
        s_i = h @ a1
        s_j = h @ a2
        e = s_i[:, :, None] + s_j[:, None, :]
        e = jnp.where(e >= 0, e, ALPHA * e)
        e = jnp.where(adj[None, :, :] > 0, e, NEG_INF)
        attn = jax.nn.softmax(e, axis=-1)
        return jnp.einsum('bij,bjd->bid', attn, h)

    def _L3_gnn_ref(input, adj, W, a):
        import jax, jax.numpy as jnp
        import numpy as np
        ALPHA = 0.2
        NEG_INF = -9000000000000000.0
        h = jnp.matmul(input, W)
        Fout = W.shape[1]
        a1 = a[:Fout, 0]
        a2 = a[Fout:, 0]
        s1 = jnp.einsum('bnf,f->bn', h, a1)
        s2 = jnp.einsum('bnf,f->bn', h, a2)
        e = s1[:, :, None] + s2[:, None, :]
        e = jnp.where(e > 0, e, ALPHA * e)
        masked = jnp.where(adj[None, :, :] > 0, e, NEG_INF)
        attention = jax.nn.softmax(masked, axis=-1)
        h_prime = jnp.matmul(attention, h)
        return jax.nn.elu(h_prime)
    x = _layernorm(x + _L0_gnn_ref(x, L0_gnn_W, L0_gnn_a, adj), axis=-1)
    x = _layernorm(x + _L1_gnn_ref(x, adj), axis=-1)
    x = _layernorm(x + _L2_gnn_ref(x, adj, L2_gnn_W, L2_gnn_a), axis=-1)
    x = _layernorm(x + _L3_gnn_ref(x, adj, L3_gnn_W, L3_gnn_a), axis=-1)
    return x

_drawn_inputs = setup_inputs


def setup_inputs(seed=0):
    import zlib

    import numpy as np

    out = dict(_drawn_inputs(seed))
    spreads = {}
    factors = {}
    for name, (base, spread) in spreads.items():
        noise = np.random.default_rng([zlib.crc32(name.encode()), seed]).standard_normal(out[name].shape)
        drawn = base * np.exp(spread * noise) if base else spread * noise
        out[name] = jnp.asarray(drawn.astype(out[name].dtype))
    for name, factor in factors.items():
        out[name] = (out[name] * factor).astype(out[name].dtype)
    return out
```

```python
from contextlib import ExitStack

import concourse.bass as bass
from concourse import mybir

F32 = mybir.dt.float32
F16 = mybir.dt.float16
BF16 = mybir.dt.bfloat16
I32 = mybir.dt.int32
ALU = mybir.AluOpType
ACT = mybir.ActivationFunctionType
X = mybir.AxisListType.X

P = 128
B, N, D = 8, 2048, 64
T = N // P
QT = 4
NQ = T // QT
EPS = 1e-5
SX = 256.0
SH = 64.0


class Count:

    def __init__(self, sem):
        self.sem, self.n = sem, 0

    def inc(self, ins):
        ins.then_inc(self.sem, 1)
        self.n += 1
        return ins

    def now(self):
        return self.n


def over(ap, shape, axis):
    return ap.unsqueeze(axis).to_broadcast(shape)


def rows(ap):
    return ap.rearrange("(t p) c -> p t c", p=P)


class Kept:

    def __init__(self, nc, ctx):
        def sb(name, shape, dt):
            return ctx.enter_context(nc.sbuf_tensor(name, shape, dt))

        self.x = sb("x_rows", [P, B, T, D], F32)
        self.maskT = sb("mask_t", [P, T, N], BF16)
        self.w_raw = sb("w_raw", [P, 3, D + 2], F32)
        self.w_hi = sb("w_hi", [P, 3, D + 2], F16)
        self.w_lo = sb("w_lo", [P, 3, D + 2], F16)
        self.id16 = sb("id16", [P, P], F16)
        self.idb = sb("idb", [P, P], BF16)
        self.id32 = sb("id32", [P, P], F32)
        self.eye2 = sb("eye2", [P, D], F32)
        self.neg_half = sb("neg_half", [P, T], F32)


def prepare(nc, kept, l0, sems, A, psum):
    x, id16, id32, idb = kept.x, kept.id16, kept.id32, kept.idb
    x_in, w_in, av_in, a0_in = sems("x_in0"), sems("w_in"), sems("av_in"), sems("a0_in")
    x_in = [x_in, sems("x_in1")]
    pool_order, vec_order = Count(sems("prep_pool")), Count(sems("prep_vec"))
    ident_ready, w_ready, a0T, a0_kept = sems("ident_ready"), sems("w_ready"), sems("a0T"), sems("a0_kept")
    x_hi, x_lo, x_t, x_tk = sems("p_x_hi"), sems("p_x_lo"), sems("p_x_t"), sems("p_x_tk")
    h_done, h_hi, h_used = sems("p_h_done"), sems("p_h_hi"), sems("p_h_used")
    stage_clear = sems("stage_clear")
    adj_in = [sems(f"adj_in{r}") for r in range(NQ)]
    row0_in = sems("row0_in")
    l0.adj_in, l0.row0_in = adj_in, row0_in

    with ExitStack() as ctx:
        def sb(name, shape, dt):
            return ctx.enter_context(nc.sbuf_tensor(name, shape, dt))

        a0 = sb("a0", [P, N], F32)
        av = sb("av", [P, 2, 2, D], F32)
        wa = sb("wa", [P, 2, 2, D], F32)
        w256 = sb("w256", [P, 3, D + 2], F32)
        xs = sb("xs", [P, 2, QT, P], F16)
        xt = sb("xt", [P, 2, QT, P], F16)
        prod = sb("prod", [P, QT, D], F32)
        ps_t = [psum[:, 512 * r:512 * r + 256].bitcast(F16).rearrange("p (t n) -> p t n", t=QT) for r in (0, 1)]
        ps_h = [psum[:, 512 * r:512 * r + QT * D].rearrange("p (t d) -> p t d", t=QT) for r in (2, 3)]
        block = ctx.enter_context(nc.Block())

        @block.sync
        def _(sp):
            for b in range(B):
                if b >= 2:
                    sp.wait_ge(x_in[b % 2], 16 * (b // 2))
                sp.dma_start(x[:, b, :, :], rows(A["x"][b])).then_inc(x_in[b % 2], 16)
            sp.wait_ge(stage_clear, 1)
            for r in range(NQ):
                load_adj(sp, A["adj"], l0.stage, r, 0, adj_in[r])
            sp.dma_start(l0.row0[:, :], A["adj"][0:1, :].rearrange("o (t p) -> p (o t)", p=P),
                         allow_slow_non_contiguous=True).then_inc(row0_in, 16)

        @block.gpsimd
        def _(pool):
            pool_order.inc(nc.gpsimd.memset(id32[:, :], 0.0))
            pool_order.inc(nc.gpsimd.memset(kept.eye2[:, :], 0.0))
            pool_order.inc(nc.gpsimd.memset(kept.neg_half[:, :], -0.5))
            nc.gpsimd.memset(l0.stage[:, NQ - 1, QT - 1, :], 0).then_inc(stage_clear, 1)
            pool.wait_ge(pool_order.sem, pool_order.now())
            pool_order.inc(nc.gpsimd.affine_select(out=id32[:, :], in_=id32[:, :], compare_op=ALU.not_equal, fill=1.0,
                                                   base=0, pattern=[[-1, P]], channel_multiplier=1))
            pool_order.inc(nc.gpsimd.affine_select(out=kept.eye2[:, :], in_=kept.eye2[:, :], compare_op=ALU.not_equal,
                                                   fill=1.0, base=0, pattern=[[-1, D]], channel_multiplier=1))
            pool.wait_ge(pool_order.sem, pool_order.now())
            pool_order.inc(nc.gpsimd.affine_select(out=kept.eye2[:, :], in_=kept.eye2[:, :], compare_op=ALU.not_equal,
                                                   fill=1.0, base=-D, pattern=[[-1, D]], channel_multiplier=1))
            nc.gpsimd.tensor_copy(id16[:, :], id32[:, :]).then_inc(ident_ready, 1)
            nc.gpsimd.tensor_copy(idb[:, :], id32[:, :]).then_inc(ident_ready, 1)

        @block.scalar
        def _(act):
            act.dma_start(a0[:, :], A["a0"]).then_inc(a0_in, 16)
            for l, w in enumerate(("w0", "w2", "w3")):
                for half in (0, D):
                    act.dma_start(kept.w_raw[half:half + D, l, 0:D], A[w]).then_inc(w_in, 16)
            act.dma_start(av[:, 0, :, :].rearrange("p i d -> p (i d)"), A["a2"].unsqueeze(0).to_broadcast([P, 2 * D])
                          ).then_inc(av_in, 16)
            act.dma_start(av[:, 1, :, :].rearrange("p i d -> p (i d)"), A["a3"].rearrange("d o -> o d").to_broadcast([P, 2 * D])
                          ).then_inc(av_in, 16)
            for r in range(NQ):
                act.wait_ge(a0T, r + 1)
                nc.scalar.copy(l0.a12[:, QT * r:QT * r + QT, :],
                               psum[:, 2048 + 512 * r:2560 + 512 * r].rearrange("p (t d) -> p t d", t=QT)
                               ).then_inc(a0_kept, 1)

            def quarter(b, q, first):
                r, Q = q % 2, NQ * b + q
                if not first:
                    act.wait_ge(x_t, Q - 1)
                nc.scalar.activation(xs[:, r, :, 0:D], x[:, b, QT * q:QT * q + QT, :], ACT.Copy, scale=SX
                                     ).then_inc(x_hi, 1)
                act.wait_ge(x_t, Q + 1)
                if not first:
                    act.wait_ge(h_done, Q - 1)
                nc.scalar.copy(xt[:, r, :, :], ps_t[r]).then_inc(x_tk, 1)
                act.wait_ge(h_done, Q + 1)
                nc.scalar.activation(l0.h_hi[:, QT * q:QT * q + QT, b, :], ps_h[r], ACT.Copy, scale=SH / SX / SX
                                     ).then_inc(h_hi, 1)

            def pair(bp):
                for par in (0, 1):
                    act.wait_ge(x_in[par], 16 * bp + 16)
                    for q in range(NQ):
                        quarter(2 * bp + par, q, isinstance(bp, int) and par == 0 and q < 2)

            pair(0)
            with act.Fori(1, B // 2) as bp:
                pair(bp)

        @block.vector
        def _(dve):
            def link(ins):
                vec_order.inc(ins)
                dve.wait_ge(vec_order.sem, vec_order.now())

            link(nc.vector.memset(kept.w_raw[:, 0, D:D + 2], 0.0))
            dve.wait_ge(w_in, 96)
            dve.wait_ge(av_in, 32)
            for i in (0, 1):
                link(nc.vector.tensor_tensor(wa[:, :, i, :], kept.w_raw[:, 1:3, 0:D], av[:, :, i, :], ALU.mult))
            for l in (0, 1):
                link(nc.vector.tensor_reduce(kept.w_raw[:, 1 + l, D:D + 2], wa[:, l, :, :], X, ALU.add))
            link(nc.vector.tensor_scalar(w256[:, :, :], kept.w_raw[:, :, :], SX, None, ALU.mult))
            link(nc.vector.tensor_copy(kept.w_hi[:, :, :], w256[:, :, :]))
            nc.vector.tensor_tensor(kept.w_lo[:, :, :], w256[:, :, :], kept.w_hi[:, :, :], ALU.subtract
                                    ).then_inc(w_ready, 1)
            dve.wait_ge(a0_kept, NQ)

            def quarter(b, q, first):
                r, Q = q % 2, NQ * b + q
                xq = x[:, b, QT * q:QT * q + QT, :]
                dve.wait_ge(x_hi, Q + 1)
                nc.vector.scalar_tensor_tensor(out=xs[:, r, :, D:P], in0=xq, scalar=SX, in1=xs[:, r, :, 0:D],
                                               op0=ALU.mult, op1=ALU.subtract).then_inc(x_lo, 1)
                dve.wait_ge(h_hi, Q + 1)
                if not first:
                    dve.wait_ge(sc_done, Q)
                nc.vector.tensor_tensor(prod[:, :, :], ps_h[r], l0.a12[:, QT * q:QT * q + QT, 0:D], ALU.mult
                                        ).then_inc(pr_done, 1)
                nc.vector.scalar_tensor_tensor(out=l0.h_lo[:, QT * q:QT * q + QT, b, :], in0=ps_h[r], scalar=SH / SX / SX,
                                               in1=l0.h_hi[:, QT * q:QT * q + QT, b, :],
                                               op0=ALU.mult, op1=ALU.subtract).then_inc(h_used, 1)
                dve.wait_ge(pr_done, Q + 1)
                nc.vector.tensor_reduce(l0.sc1[:, b, QT * q:QT * q + QT], prod[:, :, :], X, ALU.add
                                        ).then_inc(sc_done, 1)

            sc_done, pr_done = sems("p_sc_done"), sems("p_pr_done")
            for bp_ in (0,):
                for par in (0, 1):
                    dve.wait_ge(x_in[par], 16)
                    for q in range(NQ):
                        quarter(par, q, par == 0 and q == 0)
            with dve.Fori(1, B // 2) as bp:
                for par in (0, 1):
                    dve.wait_ge(x_in[par], 16 * bp + 16)
                    for q in range(NQ):
                        quarter(2 * bp + par, q, False)
            dve.wait_ge(sc_done, B * NQ)
            link(nc.vector.tensor_scalar(l0.sc1[:, :, :], l0.sc1[:, :, :], 1.0 / SX / SX, None, ALU.mult))
            link(nc.vector.memset(l0.sc1[0:1, :, 0], 0.0))
            link(nc.vector.memset(l0.c6[:, :], 1.0 / SH))
            link(nc.vector.memset(l0.c6[0:1, 0:1], 0.0))
            dve.wait_ge(h_used, B * NQ)
            dve.wait_ge(h_hi, B * NQ)
            link(nc.vector.memset(l0.h_hi[0:1, 0, :, :], 0.0))
            link(nc.vector.memset(l0.h_lo[0:1, 0, :, :], 0.0))
            dve.wait_ge(ident_ready, 1)
            link(nc.vector.tensor_scalar(l0.not_last[:, :], id16[:, P - 1:P], -1.0, 1.0, ALU.mult, ALU.add))
            link(nc.vector.memset(l0.ones[:, :], 1.0))

        @block.tensor
        def _(pe):
            pe.wait_ge(a0_in, 16)
            pe.wait_ge(ident_ready, 2)
            for t in range(T):
                tr = nc.tensor.transpose(psum[:, 2048 + P * t:2048 + P * t + P], a0[:, P * t:P * t + P], id32[:, :])
                if t % QT == QT - 1:
                    tr.then_inc(a0T, 1)
            pe.wait_ge(w_ready, 1)

            def quarter(b, q, first):
                r, Q = q % 2, NQ * b + q
                pe.wait_ge(x_hi, Q + 1)
                pe.wait_ge(x_lo, Q + 1)
                if not first:
                    pe.wait_ge(x_tk, Q - 1)
                for k in range(QT):
                    mm = nc.tensor.transpose(ps_t[r][:, k, :], xs[:, r, k, :], id16[:, :])
                mm.then_inc(x_t, 1)
                pe.wait_ge(x_tk, Q + 1)
                if not first:
                    pe.wait_ge(h_used, Q - 1)
                    pe.wait_ge(h_hi, Q - 1)
                for k in range(QT):
                    for w in (kept.w_hi, kept.w_lo):
                        mm = nc.tensor.matmul(ps_h[r][:, k, :], xt[:, r, k, :], w[:, 0, 0:D],
                                              start=(w is kept.w_hi), stop=(w is kept.w_lo))
                mm.then_inc(h_done, 1)

            for par in (0, 1):
                for q in range(NQ):
                    quarter(par, q, par == 0 and q < 2)
            with pe.Fori(1, B // 2) as bp:
                for par in (0, 1):
                    for q in range(NQ):
                        quarter(2 * bp + par, q, False)


def load_adj(sp, adj, stage, r, cq, sem):
    cols = slice(512 * cq, 512 * cq + 512)
    lo = 1 + 512 * r
    if r < NQ - 1:
        sp.dma_start(stage[:, r, :, :], adj[lo:lo + 512, cols].rearrange("(t p) c -> p t c", p=P)).then_inc(sem, 16)
    else:
        sp.dma_start(stage[:, r, 0:3, :], adj[lo:lo + 384, cols].rearrange("(t p) c -> p t c", p=P)).then_inc(sem, 16)
        sp.dma_start(stage[0:112, r, 3, :], adj[lo + 384:lo + 496, cols]).then_inc(sem, 16)
        sp.dma_start(stage[112:127, r, 3, :], adj[lo + 496:lo + 511, cols]).then_inc(sem, 16)


def layer_0(nc, kept, l0, sems, A, psum):
    x, maskT = kept.x, kept.maskT
    cast, turned, mask_kept, tile_used = sems("m_cast"), sems("m_turned"), sems("m_kept"), sems("m_tile_used")
    acc_done, acc_read = sems("l0_acc_done"), sems("l0_acc_read")
    hs_ready, hs_done = sems("hs_ready"), sems("hs_done")
    yc_ready, sq_done, var_ready, rstd_ready = (sems("l0_yc"), sems("l0_sq"), sems("l0_var"), sems("l0_rstd"))
    order = Count(sems("l0_vec"))

    with ExitStack() as ctx:
        def sb(name, shape, dt):
            return ctx.enter_context(nc.sbuf_tensor(name, shape, dt))

        RING = 8
        tile = sb("mask_tiles", [P, RING, 512], BF16)
        hsum = sb("hsum", [P, B, D], F32)
        m1 = sb("m1", [P, QT, B, D], F32)
        v = sb("v0", [P, 2, B, D], F32)
        y = sb("y0", [P, 2, B, D], F32)
        yc = sb("yc0", [P, 2, B, D], F32)
        sq = sb("sq0", [P, 2, B, D], F32)
        st = sb("st0", [P, 2, 8, B], F32)
        acc = [psum[:, 512 * i:512 * i + 512] for i in range(QT)]
        ps_m = [psum[:, 512 * i:512 * i + 256].bitcast(BF16).rearrange("p (c n) -> p c n", c=QT) for i in (4, 5)]
        ps_s = psum[:, 512 * 6:512 * 7]
        block = ctx.enter_context(nc.Block())

        @block.sync
        def _(sp):
            for cq in range(1, NQ):
                for r in range(NQ):
                    sp.wait_ge(cast, T * cq - T + QT * r + QT)
                    load_adj(sp, A["adj"], l0.stage, r, cq, l0.adj_in[r])

        @block.gpsimd
        def _(pool):
            def rstd(first_tile):
                for i in range(QT):
                    s = st[:, i % 2, :, :]
                    pool.wait_ge(var_ready, first_tile + i + 1)
                    nc.gpsimd.tensor_tensor(s[:, 4, :], s[:, 3, :], kept.neg_half[:, 0:B], ALU.pow
                                            ).then_inc(rstd_ready, 1)

            with pool.Fori(0, NQ) as cq:
                rstd(cq * QT)

        @block.scalar
        def _(act):
            def square(J, i):
                act.wait_ge(yc_ready, J + 1)
                nc.scalar.activation(sq[:, i % 2, :, :], yc[:, i % 2, :, :], ACT.Square).then_inc(sq_done, 1)

            def sweep(cq, first):
                for t in range(T):
                    m = T * cq + t
                    act.wait_ge(turned, m + 1)
                    n = P if t < T - 1 else P - 1
                    nc.scalar.copy(maskT[:, bass.ds(QT * cq, QT), 1 + P * t:1 + P * t + n], ps_m[t % 2][:, :, 0:n]
                                   ).then_inc(mask_kept, 1)
                    if not first and t % 4 == 3:
                        square(QT * cq - QT + t // 4, t // 4)

            sweep(0, True)
            with act.Fori(1, NQ) as cq:
                sweep(cq, False)
            for i in range(QT):
                square(T - QT + i, i)

        @block.tensor
        def _(pe):
            pe.wait_ge(hs_ready, 1)
            for half in (l0.h_hi, l0.h_lo):
                for t in range(T):
                    mm = nc.tensor.matmul(ps_s, l0.ones[:, :], half[:, t, :, :].rearrange("p b d -> p (b d)"),
                                          start=(half is l0.h_hi and t == 0), stop=(half is l0.h_lo and t == T - 1))
            mm.then_inc(hs_done, 1)
            pe.wait_ge(hs_ready, 2)

            def sweep(cq, first):
                for t in range(T):
                    m = T * cq + t
                    pe.wait_ge(cast, m + 1)
                    if not (first and t < 2):
                        pe.wait_ge(mask_kept, m - 1)
                    for c in range(QT):
                        tr = nc.tensor.transpose(ps_m[t % 2][:, c, :], tile[:, t % RING, P * c:P * c + P], kept.idb[:, :])
                    tr.then_inc(turned, 1)
                    for c in range(QT):
                        if t == 0 and not first:
                            pe.wait_ge(acc_read, QT * cq - QT + c + 1)
                        for half in (l0.h_hi, l0.h_lo):
                            mm = nc.tensor.matmul(acc[c], tile[:, t % RING, P * c:P * c + P],
                                                  half[:, t, :, :].rearrange("p b d -> p (b d)"),
                                                  start=(t == 0 and half is l0.h_hi),
                                                  stop=(t == T - 1 and half is l0.h_lo))
                        if t == T - 1:
                            mm.then_inc(acc_done, 1)
                    if t < T - 1:
                        mm.then_inc(tile_used, 1)
                    else:
                        nc.tensor.matmul(ps_s[:, 0:1], l0.ones[:, :], l0.ones[:, 0:1], start=True, stop=True
                                         ).then_inc(tile_used, 1)

            sweep(0, True)
            with pe.Fori(1, NQ) as cq:
                sweep(cq, False)

        @block.vector
        def _(dve):
            def link(ins):
                order.inc(ins)
                dve.wait_ge(order.sem, order.now())

            dve.wait_ge(l0.row0_in, 16)
            nc.vector.tensor_scalar(maskT[:, :, 0], l0.row0[:, :], 0, None, ALU.is_gt).then_inc(hs_ready, 1)
            dve.wait_ge(hs_done, 1)
            link(nc.vector.tensor_scalar(hsum[:, :, :].rearrange("p b d -> p (b d)"), ps_s, 1.0 / SH, None, ALU.mult))
            link(nc.vector.tensor_scalar(l0.h_lo[:, T - 1, :, :], l0.h_lo[:, T - 1, :, :], l0.not_last[:, :], None,
                                         ALU.mult))
            nc.vector.tensor_scalar(l0.h_hi[:, T - 1, :, :], l0.h_hi[:, T - 1, :, :], l0.not_last[:, :], None,
                                    ALU.mult).then_inc(hs_ready, 1)

            def post_read(cq):
                for c in range(QT):
                    J = QT * cq + c
                    dve.wait_ge(acc_done, J + 1)
                    a2 = l0.a12[:, bass.ds(J, 1), D:P].to_broadcast([P, B, D])
                    nc.vector.tensor_tensor(m1[:, c, :, :], acc[c].rearrange("p (b d) -> p b d", b=B), a2, ALU.mult
                                            ).then_inc(acc_read, 1)

            def post(cq, c):
                J, r = QT * cq + c, c % 2
                s = st[:, r, :, :]
                k = [0]

                def lk(ins):
                    k[0] += 1
                    ins.then_inc(post_order, 1)
                    dve.wait_ge(post_order, POST * J + k[0])

                xj = x[:, :, bass.ds(J, 1), :].rearrange("p b o d -> p b (o d)")
                dve.wait_ge(acc_read, J + 1)
                lk(nc.vector.tensor_reduce(s[:, 0, :], m1[:, c, :, :], X, ALU.add))
                lk(nc.vector.scalar_tensor_tensor(out=s[:, 1, :], in0=s[:, 0, :], scalar=l0.c6[:, bass.ds(J, 1)],
                                                  in1=l0.sc1[:, :, bass.ds(J, 1)].rearrange("p b o -> p (b o)"),
                                                  op0=ALU.mult, op1=ALU.add))
                lk(nc.vector.tensor_tensor(v[:, r, :, :], hsum[:, :, :], over(s[:, 1, :], [P, B, D], 2), ALU.mult))
                lk(nc.vector.scalar_tensor_tensor(out=y[:, r, :, :], in0=v[:, r, :, :], scalar=0.2, in1=v[:, r, :, :],
                                                  op0=ALU.mult, op1=ALU.max))
                lk(nc.vector.tensor_tensor(v[:, r, :, :], y[:, r, :, :], xj, ALU.add))
                lk(nc.vector.tensor_reduce(s[:, 2, :], v[:, r, :, :], X, ALU.add))
                nc.vector.scalar_tensor_tensor(out=yc[:, r, :, :], in0=over(s[:, 2, :], [P, B, D], 2), scalar=-1.0 / D,
                                               in1=v[:, r, :, :], op0=ALU.mult, op1=ALU.add).then_inc(yc_ready, 1)
                dve.wait_ge(sq_done, J + 1)
                lk(nc.vector.tensor_reduce(s[:, 5, :], sq[:, r, :, :], X, ALU.add))
                nc.vector.tensor_scalar(s[:, 3, :], s[:, 5, :], 1.0 / D, EPS, ALU.mult, ALU.add).then_inc(var_ready, 1)
                dve.wait_ge(rstd_ready, J + 1)
                lk(nc.vector.tensor_tensor(xj, yc[:, r, :, :], over(s[:, 4, :], [P, B, D], 2), ALU.mult))
                assert k[0] == POST

            POST = 8
            post_order = sems("l0_post")

            def sweep(cq, first):
                if not first:
                    post_read(cq - 1)
                for t in range(T):
                    m = T * cq + t
                    if t % QT == 0:
                        dve.wait_ge(l0.adj_in[t // QT], (48 if t // QT == NQ - 1 else 16) * (cq + 1))
                    if not (first and t < RING):
                        dve.wait_ge(tile_used, m - RING + 1)
                    nc.vector.tensor_scalar(tile[:, t % RING, :], l0.stage[:, t // QT, t % QT, :], 0, None, ALU.is_gt
                                            ).then_inc(cast, 1)
                    if not first and t % QT == 3:
                        post(cq - 1, t // QT)

            sweep(0, True)
            with dve.Fori(1, NQ) as cq:
                sweep(cq, False)
            post_read(NQ - 1)
            for c in range(QT):
                post(NQ - 1, c)
            dve.wait_ge(post_order, POST * T)


def layer_1(nc, kept, sems, psum):
    x, maskT = kept.x, kept.maskT
    qk_done, exp_done, mul_done, pv_done = sems("qk_done"), sems("exp_done"), sems("mul_done"), sems("pv_done")
    hi_done, lo_done, turned, ab_ready = sems("a_hi"), sems("a_lo"), sems("a_turned"), sems("a_ready")
    xv_ready = sems("xv_ready")
    o_out, o_turned, o_rows = sems("o_out"), sems("o_turned"), sems("o_rows")
    sum_wide, mean_ps, mean_kept = sems("sum_wide"), sems("mean_ps"), sems("mean_kept")
    q_summed, mean_spread, filled = sems("q_summed"), sems("mean_spread"), sems("filled")
    yc_ready, sq_done, var_ready, rstd_ready = sems("l1_yc"), sems("l1_sq"), sems("l1_var"), sems("l1_rstd")
    post_order, x_done = sems("l1_post"), sems("l1_x_done")
    CH = 2 * T
    POST = 8

    with ExitStack() as ctx:
        def sb(name, shape, dt):
            return ctx.enter_context(nc.sbuf_tensor(name, shape, dt))

        xa = sb("xa", [P, 2, N], F16)
        xb = sb("xb", [P, 2, N], F16)
        xs = sb("xs1", [P, QT, 3, D], F16)
        xv = sb("xv", [P, 2, T, D], F32)
        e = sb("e", [P, 4, 1024], F32)
        pm = sb("pm", [P, 4, 1024], F32)
        oT = sb("oT", [P, 1024], F32)
        o = sb("o", [P, T, D], F32)
        y = sb("y1", [P, T, D], F32)
        yc = sb("yc1", [P, T, D], F32)
        sq = sb("sq1", [P, T, D], F32)
        st = sb("st1", [P, 8, T], F32)
        none = sb("none1", [P, T], F32)
        fill = sb("fill1", [P, T, D], F32)
        qsum = sb("qsum1", [P, 2, NQ], F32)
        wide = sb("wide1", [P, P], F32)
        mean = sb("mean1", [P, 2, D], F32)
        S = [psum[:, 1024 * h:1024 * h + 1024] for h in (0, 1)]
        acc = [psum[:, 2048 + 512 * j:2560 + 512 * j] for j in (0, 1)]
        ps_x = psum[:, 3072:3584].bitcast(F16).rearrange("p (u t n) -> p u t n", u=2, t=QT)
        ps_o = psum[:, 3584:3840]
        ps_mean = psum[:, 3840:3840 + D]
        block = ctx.enter_context(nc.Block())

        def everywhere(body, eng):
            body(0, 0, True)
            body(1, 1, False)
            with eng.Fori(1, B // 2) as bp:
                body(2 * bp, 0, False)
                body(2 * bp + 1, 1, False)

        @block.gpsimd
        def _(pool):
            nc.gpsimd.memset(xv[:, :, :, D - 1:D], 1.0).then_inc(xv_ready, 1)
            nc.gpsimd.tensor_copy(xv[:, 0, :, 0:D - 1], x[:, 0, :, 0:D - 1]).then_inc(xv_ready, 1)

            def fill_of(g, par):
                pool.wait_ge(mean_kept, g + 1)
                pool.wait_ge(post_order, POST * g + 1)
                nc.gpsimd.tensor_tensor(fill[:, :, :], over(none[:, :], [P, T, D], 2), over(mean[:, par, :], [P, T, D], 1),
                                        ALU.mult).then_inc(mean_spread, 1)
                pool.wait_ge(mean_spread, g + 1)
                nc.gpsimd.tensor_tensor(fill[:, :, :], fill[:, :, :], x[:, g, :, :], ALU.add).then_inc(filled, 1)

            def rstd(g):
                pool.wait_ge(var_ready, g + 1)
                nc.gpsimd.tensor_tensor(st[:, 5, :], st[:, 4, :], kept.neg_half[:, :], ALU.pow).then_inc(rstd_ready, 1)

            def body(b, par, first):
                if not first:
                    pool.wait_ge(pv_done, T * b)
                nc.gpsimd.tensor_copy(xv[:, 1 - par, :, 0:D - 1], x[:, after(b), :, 0:D - 1]).then_inc(xv_ready, 1)
                if not first:
                    fill_of(b - 1, 1 - par)
                    rstd(b - 1)

            def after(b):
                return b + 1

            body(0, 0, True)
            body(1, 1, False)
            with pool.Fori(1, B // 2 - 1) as bp:
                body(2 * bp, 0, False)
                body(2 * bp + 1, 1, False)
            body(B - 2, 0, False)
            fill_of(B - 2, 0)
            rstd(B - 2)
            fill_of(B - 1, 1)
            rstd(B - 1)

        @block.tensor
        def _(pe):
            def pv(b, par, mt, s):
                pe.wait_ge(mul_done, 2 * s + 2)
                if mt == 0:
                    pe.wait_ge(xv_ready, b + 2)
                for j in (0, 1):
                    for h in (0, 1):
                        mm = nc.tensor.matmul(acc[j][D * h:D * h + D, :], xv[:, par, mt, :],
                                              pm[:, (2 * mt + h) % 4, 512 * j:512 * j + 512],
                                              start=(mt == 0), stop=(mt == T - 1))
                mm.then_inc(pv_done, 1)

            def turn_x(par, q, Q):
                pe.wait_ge(hi_done, Q + 1)
                pe.wait_ge(lo_done, Q + 1)
                if not (isinstance(Q, int) and Q == 0):
                    pe.wait_ge(ab_ready, Q)
                for u in (0, 1):
                    for k in range(QT):
                        tr = nc.tensor.transpose(ps_x[:, u, k, :], xs[:, k, u:u + 2, :].rearrange("p u d -> p (u d)"),
                                                 kept.id16[:, :])
                tr.then_inc(turned, 1)

            def turn_o(g, i):
                pe.wait_ge(o_out, g + 1)
                if not (isinstance(g, int) and g == 0 and i == 0):
                    pe.wait_ge(o_rows, 4 * g + i)
                if i == 0 and not (isinstance(g, int) and g == 0):
                    pe.wait_ge(mean_kept, g + 1)
                for k in (0, 1):
                    tr = nc.tensor.transpose(ps_o[:, P * k:P * k + P], oT[:, P * (2 * i + k):P * (2 * i + k) + P],
                                             kept.id32[:, :])
                tr.then_inc(o_turned, 1)

            def mean_of(g):
                pe.wait_ge(sum_wide, g + 1)
                if not (isinstance(g, int) and g == 0):
                    pe.wait_ge(o_rows, 4 * g)
                nc.tensor.matmul(ps_mean, wide[:, :], kept.eye2[:, :], start=True, stop=True).then_inc(mean_ps, 1)

            def body(b, par, first, last=False):
                for mt in range(T):
                    s = T * b + mt
                    if mt == 0:
                        pe.wait_ge(ab_ready, NQ * b + NQ)
                    for h in (0, 1):
                        if not (first and mt == 0):
                            pe.wait_ge(exp_done, 2 * s + h - 1)
                        for nb in (0, 1):
                            for xm in (xa, xb):
                                mm = nc.tensor.matmul(S[h][:, 512 * nb:512 * nb + 512],
                                                      xa[:, par, P * mt:P * mt + P],
                                                      xm[:, par, 1024 * h + 512 * nb:1024 * h + 512 * nb + 512],
                                                      start=(xm is xa), stop=(xm is xb))
                        mm.then_inc(qk_done, 1)
                    if mt > 0:
                        if mt == 1 and not first:
                            pe.wait_ge(o_out, b)
                        pv(b, par, mt - 1, s - 1)
                    elif not first:
                        pv(b - 1, 1 - par, T - 1, s - 1)
                    if mt % 3 == 2 and mt < 12 and not last:
                        turn_x(1 - par, mt // 3, NQ * b + NQ + mt // 3)
                    if mt in (2, 4, 6, 8) and not first:
                        turn_o(b - 1, mt // 2 - 1)
                    if mt == 10:
                        mean_of(b)

            for q in range(NQ):
                turn_x(0, q, q)
            body(0, 0, True)
            body(1, 1, False)
            with pe.Fori(1, B // 2 - 1) as bp:
                body(2 * bp, 0, False)
                body(2 * bp + 1, 1, False)
            body(B - 2, 0, False)
            body(B - 1, 1, False, last=True)
            pv(B - 1, 1, T - 1, T * B - 1)
            for i in range(4):
                turn_o(B - 1, i)

        @block.scalar
        def _(act):
            def split_hi(b, q, Q, first):
                if not first:
                    act.wait_ge(turned, Q)
                nc.scalar.activation(xs[:, :, 0:3:2, :], over(x[:, b, QT * q:QT * q + QT, :], [P, QT, 2, D], 2),
                                     ACT.Copy, scale=SX).then_inc(hi_done, 1)

            def keep_x(par, q, Q):
                act.wait_ge(turned, Q + 1)
                nc.scalar.activation(xa[:, par, 512 * q:512 * q + 512], ps_x[:, 0, :, :].rearrange("p t n -> p (t n)"),
                                     ACT.Copy, accum_out=qsum[:, par, q:q + 1])
                nc.scalar.copy(xb[:, par, 512 * q:512 * q + 512], ps_x[:, 1, :, :].rearrange("p t n -> p (t n)")
                               ).then_inc(ab_ready, 1)

            def keep_o(g, i):
                act.wait_ge(o_turned, 4 * g + i + 1)
                if i == 0 and not (isinstance(g, int) and g == 0):
                    act.wait_ge(x_done, g)
                nc.scalar.copy(o[:, :, :].rearrange("p (h t) d -> p t h d", h=2)[:, 2 * i:2 * i + 2, :, :],
                               ps_o.rearrange("p (t h d) -> p t h d", t=2, h=2)).then_inc(o_rows, 1)

            def out_sums(g):
                act.wait_ge(pv_done, T * g + T)
                if not (isinstance(g, int) and g == 0):
                    act.wait_ge(o_turned, 4 * g)
                nc.scalar.copy(oT[:, :], psum[:, 2048:3072]).then_inc(o_out, 1)

            def square(g):
                act.wait_ge(yc_ready, g + 1)
                nc.scalar.activation(sq[:, :, :], yc[:, :, :], ACT.Square).then_inc(sq_done, 1)

            def body(b, par, first, last=False):
                for mt in range(T):
                    s = T * b + mt
                    for h in (0, 1):
                        act.wait_ge(qk_done, 2 * s + h + 1)
                        if not (first and mt < 2):
                            act.wait_ge(mul_done, 2 * s + h - 3)
                        nc.scalar.activation(e[:, (2 * mt + h) % 4, :], S[h], ACT.Exp, scale=1.0 / SX / SX / 8.0
                                             ).then_inc(exp_done, 1)
                        if mt == 0 and h == 0 and not first:
                            out_sums(b - 1)
                    if mt < 12 and not last:
                        q = mt // 3
                        if mt % 3 == 0:
                            split_hi(b + 1, q, NQ * b + NQ + q, False)
                        if mt % 3 == 2:
                            keep_x(1 - par, q, NQ * b + NQ + q)
                    if mt in (3, 5, 7, 9) and not first:
                        keep_o(b - 1, (mt - 3) // 2)
                    if mt == 14 and not first:
                        square(b - 1)

            for q in range(NQ):
                split_hi(0, q, q, q == 0)
                keep_x(0, q, q)
            body(0, 0, True)
            body(1, 1, False)
            with act.Fori(1, B // 2 - 1) as bp:
                body(2 * bp, 0, False)
                body(2 * bp + 1, 1, False)
            body(B - 2, 0, False)
            body(B - 1, 1, False, last=True)
            out_sums(B - 1)
            for i in range(4):
                keep_o(B - 1, i)
            square(B - 1)

        @block.vector
        def _(dve):
            def split_lo(b, q, Q):
                dve.wait_ge(hi_done, Q + 1)
                nc.vector.scalar_tensor_tensor(out=xs[:, :, 1, :], in0=x[:, b, QT * q:QT * q + QT, :], scalar=SX,
                                               in1=xs[:, :, 0, :], op0=ALU.mult, op1=ALU.subtract).then_inc(lo_done, 1)

            def widen(par, g):
                dve.wait_ge(ab_ready, NQ * g + NQ)
                link1(g, nc.vector.tensor_reduce(st[:, 7, 0:1], qsum[:, par, :], X, ALU.add))
                nc.vector.tensor_scalar(wide[:, :], st[:, 7, 0:1].to_broadcast([P, P]), 1.0 / SX / N, None, ALU.mult
                                        ).then_inc(sum_wide, 1)

            def link1(g, ins):
                ins.then_inc(q_summed, 1)
                dve.wait_ge(q_summed, g + 1)

            def link(g, k, ins):
                ins.then_inc(post_order, 1)
                dve.wait_ge(post_order, POST * g + k)

            def post(par, g, part):
                xg = x[:, g, :, :]
                if part == 1:
                    dve.wait_ge(o_rows, 4 * g + 4)
                    if not (isinstance(g, int) and g == 0):
                        dve.wait_ge(filled, g)
                    link(g, 1, nc.vector.tensor_scalar(none[:, :], o[:, :, D - 1], 0.0, None, ALU.is_equal))
                    link(g, 2, nc.vector.tensor_tensor(st[:, 0, :], o[:, :, D - 1], none[:, :], ALU.add))
                    link(g, 3, nc.vector.reciprocal(st[:, 1, :], st[:, 0, :]))
                    link(g, 4, nc.vector.tensor_reduce(o[:, :, D - 1:D], o[:, :, 0:D - 1], X, ALU.add, negate=True))
                if part == 2:
                    link(g, 5, nc.vector.tensor_tensor(o[:, :, :], o[:, :, :], over(st[:, 1, :], [P, T, D], 2), ALU.mult))
                if part == 4:
                    dve.wait_ge(filled, g + 1)
                    link(g, 6, nc.vector.tensor_tensor(y[:, :, :], o[:, :, :], fill[:, :, :], ALU.add))
                if part == 5:
                    link(g, 7, nc.vector.tensor_reduce(st[:, 2, :], y[:, :, :], X, ALU.add))
                    nc.vector.scalar_tensor_tensor(out=yc[:, :, :], in0=over(st[:, 2, :], [P, T, D], 2), scalar=-1.0 / D,
                                                   in1=y[:, :, :], op0=ALU.mult, op1=ALU.add).then_inc(yc_ready, 1)
                if part == 6:
                    dve.wait_ge(sq_done, g + 1)
                    link(g, 8, nc.vector.tensor_reduce(st[:, 3, :], sq[:, :, :], X, ALU.add))
                    nc.vector.tensor_scalar(st[:, 4, :], st[:, 3, :], 1.0 / D, EPS, ALU.mult, ALU.add
                                            ).then_inc(var_ready, 1)
                if part == 7:
                    dve.wait_ge(rstd_ready, g + 1)
                    nc.vector.tensor_tensor(xg, yc[:, :, :], over(st[:, 5, :], [P, T, D], 2), ALU.mult).then_inc(x_done, 1)

            def body(b, par, first, last=False):
                for mt in range(T):
                    s = T * b + mt
                    for h in (0, 1):
                        dve.wait_ge(exp_done, 2 * s + h + 1)
                        if not (first and mt < 2):
                            dve.wait_ge(pv_done, s - 1)
                        nc.vector.tensor_tensor(pm[:, (2 * mt + h) % 4, :], e[:, (2 * mt + h) % 4, :],
                                                maskT[:, mt, 1024 * h:1024 * h + 1024], ALU.mult).then_inc(mul_done, 1)
                    if mt < 12 and mt % 3 == 1 and not last:
                        split_lo(b + 1, mt // 3, NQ * b + NQ + mt // 3)
                    if mt == 0:
                        widen(par, b)
                    if mt == 11:
                        dve.wait_ge(mean_ps, b + 1)
                        nc.vector.tensor_copy(mean[:, par, :], ps_mean).then_inc(mean_kept, 1)
                    if not first:
                        if 10 <= mt < 16:
                            post(1 - par, b - 1, mt - 9)
                        if mt == T - 1:
                            post(1 - par, b - 1, 7)

            for q in range(NQ):
                split_lo(0, q, q)
            body(0, 0, True)
            body(1, 1, False)
            with dve.Fori(1, B // 2 - 1) as bp:
                body(2 * bp, 0, False)
                body(2 * bp + 1, 1, False)
            body(B - 2, 0, False)
            body(B - 1, 1, False, last=True)
            for part in range(1, 8):
                post(1, B - 1, part)


def layers_2_3(nc, kept, sems, psum, scratch, out):
    x, maskT = kept.x, kept.maskT
    BIG = 2.0 ** 40
    SV = 256.0
    W1 = D + 1
    LEAD = 4
    G = 2 * B
    relu_done, mp_done, av_done, evac = sems("relu_done"), sems("mp_done"), sems("av_done"), sems("uv_evac")
    hi_done, lo_done, turned, xt_ready, h_ps, h_kept = (sems(n) for n in (
        "g_hi", "g_lo", "g_turned", "g_xt", "g_h_ps", "g_h_kept"))
    top_part, top_all, args_ready, ex_ready, bias_ready = (sems(n) for n in (
        "top_part", "top_all", "args_ready", "ex_ready", "bias_ready"))
    v_done, v_hi, v_lo, v_ready = sems("v_done"), sems("v_hi"), sems("v_lo"), sems("v_ready")
    q_summed, sum_wide, mean_ps, mean_kept = sems("g_q_summed"), sems("g_wide"), sems("g_mean_ps"), sems("g_mean_kept")
    s_out, r_in = sems("s_out"), [sems("r_in0"), sems("r_in1")]
    uv_used, elu_in, elu_out = sems("uv_used"), sems("elu_in"), sems("elu_out")
    filled, mean_spread = sems("g_filled"), sems("g_mean_spread")
    yc_ready, sq_done, var_ready, rstd_ready = sems("g_yc"), sems("g_sq"), sems("g_var"), sems("g_rstd")
    post_order, sc_order, x_done, out_done, ones_set = (sems(n) for n in (
        "g_post", "g_sc", "g_x_done", "out_done", "ones_set"))
    POST, SC = 9, 2

    with ExitStack() as ctx:
        def sb(name, shape, dt):
            return ctx.enter_context(nc.sbuf_tensor(name, shape, dt))

        si = sb("si", [P, 2, N], F32)
        z = sb("z", [P, 2, N], BF16)
        mp = sb("mp", [P, LEAD, N], BF16)
        mn = sb("mn", [P, 2, N], BF16)
        v = sb("v", [P, T, 6, W1], F16)
        vf = sb("vf", [P, 2, QT, W1], F32)
        h = sb("h", [P, 2, T, D + 3], F32)
        xs = sb("xs2", [P, NQ, QT, 2, D], F16)
        xt = sb("xt2", [P, 2, QT * P], F16)
        qsum = sb("qsum", [P, 2, NQ], F32)
        wide = sb("wide", [P, P], F32)
        mean = sb("mean", [P, 2, D], F32)
        args = sb("args", [P, 4, T], F32)
        ex = sb("ex", [P, 2, 4, T], F32)
        bias = sb("bias", [P, 2, T], F32)
        tops = sb("tops", [P, 4], F32)
        tt = sb("tt", [P, T], F32)
        uv = sb("uv", [P, T, 2, W1], F32)
        n2 = sb("n2", [P, T, W1], F32)
        o = sb("o2", [P, T, W1], F32)
        y = sb("y2", [P, T, D], F32)
        yc = sb("yc2", [P, T, D], F32)
        st = sb("st2", [P, 8, T], F32)
        none = sb("none2", [P, T], F32)
        fill = sb("fill2", [P, T, D], F32)
        big = sb("big", [P, T], F32)
        ps_x = psum[:, 3072:3328].bitcast(F16)
        ps_h = psum[:, 3584:3584 + QT * (D + 2)].rearrange("p (t d) -> p t d", t=QT)
        ps_mean = psum[:, 3584 + QT * (D + 2):3584 + QT * (D + 2) + D]

        def tile_sum(it):
            c = 512 * (it // 3) + 2 * W1 * (it % 3)
            return psum[:, c:c + 2 * W1]

        block = ctx.enter_context(nc.Block())

        def drive(eng, body, pair=None):
            for lay in (0, 1):
                body(lay, 0, 0, (lay, 2))
                body(lay, 1, 1, (lay, 3))
                with eng.Fori(1, B // 2 - 1) as bp:
                    if pair is not None:
                        pair[0] = bp
                    for par in (0, 1):
                        body(lay, 2 * bp + par, par, (lay, 2 * bp + par + 2))
                for par in (0, 1):
                    body(lay, B - 2 + par, par, (1, par) if lay == 0 else None)

        def is0(g):
            return isinstance(g, int) and g == 0

        def last_of_all(lay, b):
            return lay == 1 and isinstance(b, int) and b == B - 1

        @block.sync
        def _(sp):
            def load_si(g, par):
                sp.wait_ge(h_kept, NQ * g + NQ)
                sp.dma_start(scratch[par:par + 1, :].rearrange("o (t p) -> p (o t)", p=P), h[:, par, :, D + 1],
                             allow_slow_non_contiguous=True).then_inc(s_out, 16)
                if g >= 2:
                    sp.wait_ge(relu_done, T * g - T)
                sp.wait_ge(s_out, 16 * g + 16)
                sp.dma_start(si[:, par, :], scratch[par:par + 1, :].to_broadcast([P, N])).then_inc(r_in[par], 16)

            def store(b, g):
                sp.wait_ge(x_done, g + 1)
                sp.dma_start(rows(out[b]), x[:, b, :, :]).then_inc(out_done, 16)

            load_si(0, 0)
            for g in range(G):
                if g + 1 < G:
                    load_si(g + 1, (g + 1) % 2)
                if g >= B + 1:
                    store(g - B - 1, g - 1)
            store(B - 1, G - 1)
            sp.wait_ge(out_done, 16 * B)

        @block.gpsimd
        def _(pool):
            nc.gpsimd.memset(big[:, :], BIG).then_inc(ones_set, 1)
            nc.gpsimd.memset(h[:, :, :, 0:1], 1.0).then_inc(ones_set, 1)
            pool.wait_ge(ones_set, 2)

            def top_of(g, par):
                pool.wait_ge(top_part, g + 1)
                nc.gpsimd.tensor_tensor(bias[:, par, :], h[:, par, :, D + 2], big[:, :], ALU.mult).then_inc(bias_ready, 1)
                nc.gpsimd.partition_all_reduce(tops[:, 2:3], tops[:, 0:1], P, bass.bass_isa.ReduceOp.max
                                               ).then_inc(top_all, 1)

            def fill_of(lay, g, b, par):
                pool.wait_ge(mean_kept, g + 1)
                pool.wait_ge(post_order, POST * g + 3)
                if lay == 1:
                    nc.gpsimd.tensor_tensor(fill[:, :, :], over(none[:, :], [P, T, D], 2),
                                            over(mean[:, par, :], [P, T, D], 1), ALU.mult).then_inc(filled, 1)
                    return
                nc.gpsimd.tensor_tensor(fill[:, :, :], over(none[:, :], [P, T, D], 2),
                                        over(mean[:, par, :], [P, T, D], 1), ALU.mult).then_inc(mean_spread, 1)
                pool.wait_ge(mean_spread, g + 1)
                nc.gpsimd.tensor_tensor(fill[:, :, :], fill[:, :, :], x[:, b, :, :], ALU.add).then_inc(filled, 1)

            def rstd(g):
                pool.wait_ge(var_ready, g + 1)
                nc.gpsimd.tensor_tensor(st[:, 5, :], st[:, 4, :], kept.neg_half[:, :], ALU.pow).then_inc(rstd_ready, 1)

            def body(lay, b, par, ahead):
                g = B * lay + b
                if not last_of_all(lay, b):
                    top_of(g + 1, 1 - par)
                if not is0(g):
                    if isinstance(b, int) and b == 0:
                        fill_of(lay - 1, g - 1, B - 1, 1 - par)
                    else:
                        fill_of(lay, g - 1, b - 1, 1 - par)
                    rstd(g - 1)

            top_of(0, 0)
            drive(pool, body)
            fill_of(1, G - 1, B - 1, 1)
            rstd(G - 1)

        @block.tensor
        def _(pe):
            def turn(q, Q):
                pe.wait_ge(hi_done, Q + 1)
                pe.wait_ge(lo_done, Q + 1)
                if not is0(Q):
                    pe.wait_ge(xt_ready, Q)
                for k in range(QT):
                    tr = nc.tensor.transpose(ps_x[:, P * k:P * k + P], xs[:, q, k, :, :].rearrange("p u d -> p (u d)"),
                                             kept.id16[:, :])
                tr.then_inc(turned, 1)

            def times_w(lay, q, Q, g=None):
                pe.wait_ge(xt_ready, Q + 1)
                if not is0(Q):
                    pe.wait_ge(h_kept, Q)
                if q == 0 and g is not None:
                    pe.wait_ge(mean_kept, g + 1)
                for k in range(QT):
                    for w in (kept.w_hi, kept.w_lo):
                        mm = nc.tensor.matmul(ps_h[:, k, :], xt[:, q % 2, P * k:P * k + P], w[:, 1 + lay, :],
                                              start=(w is kept.w_hi), stop=(w is kept.w_lo))
                mm.then_inc(h_ps, 1)

            def mean_of(lay, g, kept_quarters):
                pe.wait_ge(sum_wide, g + 1)
                pe.wait_ge(h_kept, kept_quarters)
                nc.tensor.matmul(ps_mean, wide[:, :], kept.w_raw[:, 1 + lay, 0:D], start=True, stop=True
                                 ).then_inc(mean_ps, 1)

            def step(g, jt):
                s = T * g + jt
                apart = jt % 4 == 0
                pe.wait_ge(mp_done, s + 1)
                if jt % QT == 0:
                    pe.wait_ge(v_ready, NQ * g + jt // QT + 1)
                w = v[:, jt, :, :]
                for it in range(T):
                    if jt == 0 and it % 3 == 0 and not is0(g):
                        pe.wait_ge(evac, 6 * g - 6 + it // 3 + 1)
                    a = mp[:, jt % LEAD, P * it:P * it + P]
                    m = mn[:, jt // 4 % 2, P * it:P * it + P] if apart else maskT[:, jt, P * it:P * it + P]
                    acc = tile_sum(it)
                    for half in (0, 1):
                        lead = w[:, 2 * half:2 * half + (1 if apart else 2), :].rearrange("p u d -> p (u d)")
                        nc.tensor.matmul(acc[:, 0:lead.shape[1]], a, lead,
                                         start=(jt == 0 and half == 0 and it % 3 == 0), stop=False,
                                         skip_group_check=True)
                    for half in (0, 1):
                        mm = nc.tensor.matmul(acc[:, W1:2 * W1], m, w[:, 4 + half, :], start=False,
                                              stop=(jt == T - 1 and half == 1 and (it % 3 == 2 or it == T - 1)),
                                              skip_group_check=True)
                mm.then_inc(av_done, 1)

            def body(lay, b, par, ahead):
                g = B * lay + b
                for jt in range(T):
                    step(g, jt)
                    if ahead:
                        Q = NQ * (g + 2)
                        if jt % 2 == 0 and jt < 8:
                            turn(jt // 2, Q + jt // 2)
                        if jt % 2 == 1 and 3 <= jt < 11:
                            times_w(ahead[0], (jt - 3) // 2, Q + (jt - 3) // 2, g)
                    if jt == 11 and not last_of_all(lay, b):
                        mean_of(1 if lay == 0 and isinstance(b, int) and b == B - 1 else lay, g + 1,
                                NQ * (g + 3) if ahead else NQ * G)

            for Q in range(2 * NQ):
                turn(Q % NQ, Q)
                times_w(0, Q % NQ, Q)
            mean_of(0, 0, 2 * NQ)
            drive(pe, body)

        @block.scalar
        def _(act):
            def split_hi(b, q, Q):
                if not (isinstance(Q, int) and Q < NQ):
                    act.wait_ge(turned, Q - NQ + 1)
                nc.scalar.activation(xs[:, q, :, 0, :], x[:, b, QT * q:QT * q + QT, :], ACT.Copy, scale=SX
                                     ).then_inc(hi_done, 1)

            def keep_x(par, q, Q):
                act.wait_ge(turned, Q + 1)
                if not (isinstance(Q, int) and Q < 2):
                    act.wait_ge(h_ps, Q - 1)
                nc.scalar.activation(xt[:, q % 2, :], ps_x, ACT.Copy, accum_out=qsum[:, par, q:q + 1]
                                     ).then_inc(xt_ready, 1)

            def exps(g, par):
                act.wait_ge(args_ready, g + 1)
                if not (isinstance(g, int) and g < 2):
                    act.wait_ge(uv_used, g - 1)
                nc.scalar.activation(ex[:, par, :, :], args[:, :, :], ACT.Exp).then_inc(ex_ready, 1)

            def values_hi(q, Q):
                act.wait_ge(v_done, Q + 1)
                nc.scalar.copy(v[:, QT * q:QT * q + QT, 0:5:4, :].rearrange("p t u d -> p u t d"), vf[:, :, :, :]
                               ).then_inc(v_hi, 1)

            def values_minus(q, Q):
                act.wait_ge(v_lo, Q + 1)
                nc.scalar.activation(v[:, QT * q:QT * q + QT, 1:4:2, :], v[:, QT * q:QT * q + QT, 4:6, :], ACT.Copy,
                                     scale=-1.0).then_inc(v_ready, 1)

            def copy_sums(g):
                act.wait_ge(av_done, T * g + T)
                if not is0(g):
                    act.wait_ge(uv_used, g)
                for k in range(6):
                    n = 3 if k < 5 else 1
                    nc.scalar.copy(uv[:, 3 * k:3 * k + n, :, :].rearrange("p t u d -> p (t u d)"),
                                   psum[:, 512 * k:512 * k + 2 * W1 * n]).then_inc(evac, 1)

            def square(g):
                act.wait_ge(yc_ready, g + 1)
                nc.scalar.activation(y[:, :, :], yc[:, :, :], ACT.Square).then_inc(sq_done, 1)

            def elu_exp(b1):
                act.wait_ge(elu_in, b1)
                nc.scalar.activation(y[:, :, :], o[:, :, 1:W1], ACT.Exp).then_inc(elu_out, 1)

            def body(lay, b, par, ahead):
                g = B * lay + b
                last = last_of_all(lay, b)
                for jt in range(T):
                    s = T * g + jt
                    if jt == 0:
                        act.wait_ge(r_in[par], 16 * count_pairs(lay, b, par))
                        act.wait_ge(bias_ready, g + 1)
                    if not (is0(g) and jt < 2):
                        act.wait_ge(mp_done, s - 1)
                    nc.scalar.activation(z[:, jt % 2, :], si[:, par, :], ACT.Relu, scale=BIG,
                                         bias=bias[:, par, jt:jt + 1]).then_inc(relu_done, 1)
                    if jt == 4 and not is0(g):
                        copy_sums(g - 1)
                    if ahead and jt % 2 == 0 and jt < 8:
                        q = jt // 2
                        if lay == 0 and ahead[0] == 1 and q == 0:
                            act.wait_ge(x_done, ahead[1] + 1)
                        split_hi(ahead[1], q, NQ * (g + 2) + q)
                    if ahead and jt % 2 == 1 and 5 <= jt < 13:
                        q = (jt - 5) // 2
                        keep_x(par, q, NQ * (g + 2) + q)
                    if jt == 7 and not last:
                        exps(g + 1, 1 - par)
                    Q = NQ * g + jt // QT + 2
                    if not (last and jt >= 8):
                        if jt % QT == 2:
                            values_hi((jt // QT + 2) % NQ, Q)
                        if jt % QT == 3:
                            values_minus((jt // QT + 2) % NQ, Q)
                    if not is0(g):
                        if jt == 9 and elu_here(lay, b):
                            elu_exp(g - B)
                        if jt == 13:
                            square(g - 1)

            def count_pairs(lay, b, par):
                if isinstance(b, int):
                    return (B * lay + b) // 2 + 1
                return B // 2 * lay + pair[0] + 1

            def elu_here(lay, b):
                return lay == 1 and not is0(b)

            pair = [None]

            for Q in range(2 * NQ):
                split_hi(Q // NQ, Q % NQ, Q)
                keep_x(Q // NQ, Q % NQ, Q)
            exps(0, 0)
            for q in (0, 1):
                values_hi(q, q)
                values_minus(q, q)
            drive(act, body, pair)
            copy_sums(G - 1)
            elu_exp(B)
            square(G - 1)

        @block.vector
        def _(dve):
            def split_lo(b, q, Q):
                dve.wait_ge(hi_done, Q + 1)
                nc.vector.scalar_tensor_tensor(out=xs[:, q, :, 1, :], in0=x[:, b, QT * q:QT * q + QT, :], scalar=SX,
                                               in1=xs[:, q, :, 0, :], op0=ALU.mult, op1=ALU.subtract).then_inc(lo_done, 1)

            def keep_h(par, q, Q, stored=None):
                dve.wait_ge(h_ps, Q + 1)
                if stored is not None:
                    dve.wait_ge(s_out, 16 * stored)
                nc.vector.tensor_scalar(h[:, par, QT * q:QT * q + QT, 1:D + 3], ps_h, 1.0 / SX / SX, None, ALU.mult
                                        ).then_inc(h_kept, 1)

            def sc(g, k, ins):
                ins.then_inc(sc_order, 1)
                dve.wait_ge(sc_order, SC * g + k)

            def tops_of(g, par):
                dve.wait_ge(h_kept, NQ * g + NQ)
                nc.vector.tensor_reduce(tops[:, 0:1], h[:, par, :, D + 2], X, ALU.max).then_inc(top_part, 1)
                dve.wait_ge(xt_ready, NQ * g + NQ)
                sc(g, 1, nc.vector.tensor_reduce(tops[:, 1:2], qsum[:, par, :], X, ALU.add))
                nc.vector.tensor_scalar(wide[:, :], tops[:, 1:2].to_broadcast([P, P]), 1.0 / SX / N, None, ALU.mult
                                        ).then_inc(sum_wide, 1)

            def args_of(g, par):
                dve.wait_ge(top_all, g + 1)
                top, s_j = tops[:, 2:3], h[:, par, :, D + 2]
                if not is0(g):
                    dve.wait_ge(ex_ready, g)
                sc(g, 2, nc.vector.tensor_scalar(tt[:, :], h[:, par, :, D + 1], top, 0.8, ALU.add, ALU.mult))
                nc.vector.tensor_scalar(args[:, 0, :], tt[:, :], 0.0, None, ALU.min)
                nc.vector.tensor_scalar(args[:, 1, :], tt[:, :], -1.0, 0.0, ALU.mult, ALU.min)
                nc.vector.tensor_scalar(args[:, 2, :], s_j, top, None, ALU.subtract)
                nc.vector.tensor_scalar(args[:, 3, :], s_j, top, 0.2, ALU.subtract, ALU.mult).then_inc(args_ready, 1)

            def keep_mean(g, par):
                dve.wait_ge(mean_ps, g + 1)
                nc.vector.tensor_copy(mean[:, par, :], ps_mean).then_inc(mean_kept, 1)

            def values(q, Q, g, par):
                dve.wait_ge(ex_ready, g + 1)
                if not is0(Q):
                    dve.wait_ge(v_lo, Q)
                hq = h[:, par, QT * q:QT * q + QT, 0:W1]
                for u in (0, 1):
                    ins = nc.vector.scalar_tensor_tensor(out=vf[:, u, :, :], in0=hq, scalar=SV,
                                                         in1=over(ex[:, par, 2 + u, QT * q:QT * q + QT], [P, QT, W1], 2),
                                                         op0=ALU.mult, op1=ALU.mult)
                ins.then_inc(v_done, 1)

            def values_lo(q, Q):
                dve.wait_ge(v_hi, Q + 1)
                for u in (0, 1):
                    ins = nc.vector.tensor_tensor(v[:, QT * q:QT * q + QT, 2 + 3 * u, :], vf[:, u, :, :],
                                                  v[:, QT * q:QT * q + QT, 4 * u, :], ALU.subtract)
                ins.then_inc(v_lo, 1)

            def post(g, b, lay, par, part):
                def lk(k, ins):
                    ins.then_inc(post_order, 1)
                    dve.wait_ge(post_order, POST * g + k)

                xg = x[:, b, :, :]
                if part == 4:
                    dve.wait_ge(evac, 6 * g + 6)
                    lk(1, nc.vector.tensor_tensor(n2[:, :, :], uv[:, :, 1, :], over(ex[:, par, 1, :], [P, T, W1], 2), ALU.mult))
                    nc.vector.tensor_tensor(o[:, :, :], uv[:, :, 0, :], over(ex[:, par, 0, :], [P, T, W1], 2), ALU.mult
                                            ).then_inc(uv_used, 1)
                if part == 5:
                    dve.wait_ge(uv_used, g + 1)
                    lk(2, nc.vector.tensor_tensor(o[:, :, :], o[:, :, :], n2[:, :, :], ALU.add))
                    if not is0(g):
                        dve.wait_ge(filled, g)
                    lk(3, nc.vector.tensor_scalar(none[:, :], o[:, :, 0], 0.0, None, ALU.is_equal))
                    lk(4, nc.vector.tensor_tensor(st[:, 0, :], o[:, :, 0], none[:, :], ALU.add))
                    lk(5, nc.vector.reciprocal(st[:, 1, :], st[:, 0, :]))
                if part == 6:
                    lk(6, nc.vector.tensor_tensor(o[:, :, 1:W1], o[:, :, 1:W1], over(st[:, 1, :], [P, T, D], 2), ALU.mult))
                if part == 7:
                    dve.wait_ge(filled, g + 1)
                    if lay == 0:
                        nc.vector.tensor_tensor(y[:, :, :], o[:, :, 1:W1], fill[:, :, :], ALU.add
                                                ).then_inc(post_order, 2)
                        dve.wait_ge(post_order, POST * g + 8)
                    else:
                        nc.vector.tensor_tensor(o[:, :, 1:W1], o[:, :, 1:W1], fill[:, :, :], ALU.add).then_inc(elu_in, 1)
                if part == 9 and lay == 1:
                    dve.wait_ge(elu_out, b + 1)
                    lk(7, nc.vector.tensor_scalar(n2[:, :, 0:D], y[:, :, :], 1.0, -1.0, ALU.min, ALU.add))
                    nc.vector.scalar_tensor_tensor(out=o[:, :, 1:W1], in0=o[:, :, 1:W1], scalar=0.0,
                                                   in1=n2[:, :, 0:D], op0=ALU.max, op1=ALU.add).then_inc(elu_sum, 1)
                    dve.wait_ge(elu_sum, b + 1)
                    lk(8, nc.vector.tensor_tensor(y[:, :, :], o[:, :, 1:W1], xg, ALU.add))
                if part == 10:
                    lk(9, nc.vector.tensor_reduce(st[:, 2, :], y[:, :, :], X, ALU.add))
                if part == 11:
                    nc.vector.scalar_tensor_tensor(out=yc[:, :, :], in0=over(st[:, 2, :], [P, T, D], 2), scalar=-1.0 / D,
                                                   in1=y[:, :, :], op0=ALU.mult, op1=ALU.add).then_inc(yc_ready, 1)
                if part == 13:
                    dve.wait_ge(sq_done, g + 1)
                    nc.vector.tensor_reduce(st[:, 3, :], y[:, :, :], X, ALU.add).then_inc(var_sum, 1)
                    dve.wait_ge(var_sum, g + 1)
                    nc.vector.tensor_scalar(st[:, 4, :], st[:, 3, :], 1.0 / D, EPS, ALU.mult, ALU.add
                                            ).then_inc(var_ready, 1)
                if part == 15:
                    dve.wait_ge(rstd_ready, g + 1)
                    nc.vector.tensor_tensor(xg, yc[:, :, :], over(st[:, 5, :], [P, T, D], 2), ALU.mult).then_inc(x_done, 1)

            elu_sum, var_sum = sems("elu_sum"), sems("var_sum")

            def body(lay, b, par, ahead):
                g = B * lay + b
                last = last_of_all(lay, b)
                if isinstance(b, int) and b == 0:
                    lay1, b1 = lay - 1, B - 1
                else:
                    lay1, b1 = lay, b - 1
                for jt in range(T):
                    s = T * g + jt
                    dve.wait_ge(relu_done, s + 1)
                    if not (is0(g) and jt < LEAD):
                        dve.wait_ge(av_done, s - LEAD + 1)
                    nc.vector.tensor_tensor(mp[:, jt % LEAD, :], z[:, jt % 2, :], maskT[:, jt, :], ALU.min
                                            ).then_inc(mp_parts if jt % 4 == 0 else mp_done, 1)
                    if jt % 4 == 0:
                        dve.wait_ge(mp_parts, NQ * g + jt // 4 + 1)
                        nc.vector.tensor_tensor(mn[:, jt // 4 % 2, :], maskT[:, jt, :], mp[:, jt % LEAD, :], ALU.subtract
                                                ).then_inc(mp_done, 1)
                    Q = NQ * g + jt // QT + 2
                    if jt % QT == 0 and not (last and jt >= 8):
                        if jt < 8:
                            values(jt // QT + 2, Q, g, par)
                        else:
                            values(jt // QT - 2, Q, g + 1, 1 - par)
                    if jt % QT == 2 and not (last and jt >= 8):
                        values_lo((jt // QT + 2) % NQ, Q)
                    if not is0(g):
                        post(g - 1, b1, lay1, 1 - par, jt)
                    if ahead and jt % 2 == 0 and jt < 8:
                        split_lo(ahead[1], jt // 2, NQ * (g + 2) + jt // 2)
                    if ahead and jt % 2 == 1 and jt >= 7 and jt < 15:
                        keep_h(par, (jt - 7) // 2, NQ * (g + 2) + (jt - 7) // 2, g + 1)
                    if not last:
                        if jt == 4:
                            tops_of(g + 1, 1 - par)
                        if jt == 5:
                            args_of(g + 1, 1 - par)
                        if jt == T - 1:
                            keep_mean(g + 1, 1 - par)

            mp_parts = sems("mp_parts")
            dve.wait_ge(ones_set, 2)
            for Q in range(2 * NQ):
                split_lo(Q // NQ, Q % NQ, Q)
                keep_h(Q // NQ, Q % NQ, Q)
            tops_of(0, 0)
            args_of(0, 0)
            keep_mean(0, 0)
            for q in (0, 1):
                values(q, q, 0, 0)
                values_lo(q, q)
            drive(dve, body)
            for part in (4, 5, 6, 7, 9, 10, 11, 13, 15):
                post(G - 1, B - 1, 1, 1, part)


class Layer0:

    def __init__(self, nc, ctx):
        def sb(name, shape, dt):
            return ctx.enter_context(nc.sbuf_tensor(name, shape, dt))

        self.a12 = sb("a12", [P, T, P], F32)
        self.h_hi = sb("h_hi", [P, T, B, D], F16)
        self.h_lo = sb("h_lo", [P, T, B, D], F16)
        self.sc1 = sb("sc1", [P, B, T], F32)
        self.c6 = sb("c6", [P, T], F32)
        self.not_last = sb("not_last", [P, 1], F32)
        self.ones = sb("ones16", [P, P], F16)
        self.stage = sb("stage", [P, NQ, QT, 512], I32)
        self.row0 = sb("row0", [P, T], I32)


def build(nc, A, out, stop_after=99):
    with ExitStack() as ctx:
        psum = ctx.enter_context(nc.psum_tensor("banks", [P, 4096], F32))
        names = {}

        def sems(name):
            assert name not in names
            names[name] = ctx.enter_context(nc.semaphore(name))
            return names[name]

        kept = Kept(nc, ctx)
        with ExitStack() as first:
            l0 = Layer0(nc, first)
            prepare(nc, kept, l0, sems, A, psum)
            layer_0(nc, kept, l0, sems, A, psum)
        if stop_after >= 1:
            layer_1(nc, kept, sems, psum)
        if stop_after >= 2:
            scratch = nc.dram_tensor("s_i_rows", (2, N), F32, kind="Internal").ap()
            layers_2_3(nc, kept, sems, psum, scratch, out)
            return
        if stop_after <= 1:
            out_done = sems("out_done")
            with nc.Block() as block:
                @block.sync
                def _(sp):
                    for b in range(B):
                        sp.dma_start(rows(out[b]), kept.x[:, b, :, :]).then_inc(out_done, 16)
                    sp.wait_ge(out_done, 16 * B)
            return


_INS = {"x": "x", "adj": "adj", "L0_gnn_W": "w0", "L0_gnn_a": "a0", "L2_gnn_W": "w2", "L2_gnn_a": "a2",
        "L3_gnn_W": "w3", "L3_gnn_a": "a3"}


def kernel(**inputs):
    import numpy as np
    import concourse.bacc as bacc
    from concourse.bass_utils import run_bass_kernel_spmd

    nc = bacc.Bacc("TRN2", target_bir_lowering=False, num_devices=1)
    arrays, A = {}, {}
    for name, short in _INS.items():
        a = np.ascontiguousarray(inputs[name])
        arrays[f"in_{short}"] = a
        A[short] = nc.dram_tensor(f"in_{short}", a.shape, mybir.dt.from_np(a.dtype), kind="ExternalInput").ap()
    out = nc.dram_tensor("out_x", (B, N, D), F32, kind="ExternalOutput").ap()
    build(nc, A, out)
    r = run_bass_kernel_spmd(nc, [arrays], core_ids=[0])
    return r.results[0]["out_x"]
```

```python
from contextlib import ExitStack

import concourse.bass as bass
from concourse import mybir

F32 = mybir.dt.float32
F16 = mybir.dt.float16
BF16 = mybir.dt.bfloat16
I32 = mybir.dt.int32
ALU = mybir.AluOpType
ACT = mybir.ActivationFunctionType
X = mybir.AxisListType.X

P = 128
B, N, D = 8, 2048, 64
T = N // P
QT = 4
NQ = T // QT
EPS = 1e-5
SX = 256.0
SH = 64.0


class Count:

    def __init__(self, sem):
        self.sem, self.n = sem, 0

    def inc(self, ins):
        ins.then_inc(self.sem, 1)
        self.n += 1
        return ins

    def now(self):
        return self.n


def over(ap, shape, axis):
    return ap.unsqueeze(axis).to_broadcast(shape)


def rows(ap):
    return ap.rearrange("(t p) c -> p t c", p=P)


class Kept:

    def __init__(self, nc, ctx):
        def sb(name, shape, dt):
            return ctx.enter_context(nc.sbuf_tensor(name, shape, dt))

        self.x = sb("x_rows", [P, B, T, D], F32)
        self.maskT = sb("mask_t", [P, T, N], BF16)
        self.w_raw = sb("w_raw", [P, 3, D + 2], F32)
        self.w_hi = sb("w_hi", [P, 3, D + 2], F16)
        self.w_lo = sb("w_lo", [P, 3, D + 2], F16)
        self.id16 = sb("id16", [P, P], F16)
        self.idb = sb("idb", [P, P], BF16)
        self.id32 = sb("id32", [P, P], F32)
        self.eye2 = sb("eye2", [P, D], F32)
        self.neg_half = sb("neg_half", [P, T], F32)


def prepare(nc, kept, l0, sems, A, psum):
    x, id16, id32, idb = kept.x, kept.id16, kept.id32, kept.idb
    x_in, w_in, av_in, a0_in = [sems("x_in0"), sems("x_in1")], sems("w_in"), sems("av_in"), sems("a0_in")
    pool_order, vec_order = Count(sems("prep_pool")), Count(sems("prep_vec"))
    ident_ready, w_ready, a0T, a0_kept = sems("ident_ready"), sems("w_ready"), sems("a0T"), sems("a0_kept")
    x_hi, x_lo, x_t, x_tk = sems("p_x_hi"), sems("p_x_lo"), sems("p_x_t"), sems("p_x_tk")
    h_done, h_hi, h_used = sems("p_h_done"), sems("p_h_hi"), sems("p_h_used")
    stage_clear, ones_set = sems("stage_clear"), sems("ones16_set")
    adj_in = [sems(f"adj_in{r}") for r in range(NQ)]
    row0_in = sems("row0_in")
    l0.adj_in, l0.row0_in = adj_in, row0_in

    with ExitStack() as ctx:
        def sb(name, shape, dt):
            return ctx.enter_context(nc.sbuf_tensor(name, shape, dt))

        a0 = sb("a0", [P, N], F32)
        av = sb("av", [P, 2, 2, D], F32)
        wa = sb("wa", [P, 2, 2, D], F32)
        w256 = sb("w256", [P, 3, D + 2], F32)
        xs = sb("xs", [P, 2, QT, P], F16)
        xt = sb("xt", [P, 2, QT, P], F16)
        prod = sb("prod", [P, 2, QT, D], F32)
        ps_t = [psum[:, 512 * r:512 * r + 256].bitcast(F16).rearrange("p (t n) -> p t n", t=QT) for r in (0, 1)]
        ps_h = [psum[:, 512 * r:512 * r + QT * D].rearrange("p (t d) -> p t d", t=QT) for r in (2, 3)]
        ps_s = psum[:, 512 * 4:512 * 5]
        block = ctx.enter_context(nc.Block())
        sc_done, pr_done, hs_done = sems("p_sc_done"), sems("p_pr_done"), sems("p_hs_done")

        def stages(step, eng):
            def pair(bp):
                for par in (0, 1):
                    for q in range(NQ):
                        step(bp, par, q)

            pair(0)
            with eng.Fori(1, B // 2 - 1) as bp:
                pair(bp)
            pair(B // 2 - 1)

        def after(bp, par, q, n):
            k = NQ * par + q + n
            if k >= 2 * NQ and isinstance(bp, int) and bp == B // 2 - 1:
                return None
            return (bp + 1, 0, k - 2 * NQ) if k >= 2 * NQ else (bp, k // NQ, k % NQ)

        def number(bp, par, q):
            return 2 * NQ * bp + NQ * par + q

        def before(Q, n):
            return isinstance(Q, int) and Q < n

        @block.sync
        def _(sp):
            for b in range(B):
                if b >= 2:
                    sp.wait_ge(x_in[b % 2], 16 * (b // 2))
                sp.dma_start(x[:, b, :, :], rows(A["x"][b])).then_inc(x_in[b % 2], 16)
            sp.wait_ge(stage_clear, 1)
            for r in range(NQ):
                load_adj(sp, A["adj"], l0.stage, r, 0, adj_in[r])
            sp.dma_start(l0.row0[:, :], A["adj"][0:1, :].rearrange("o (t p) -> p (o t)", p=P),
                         allow_slow_non_contiguous=True).then_inc(row0_in, 16)

        @block.gpsimd
        def _(pool):
            pool_order.inc(nc.gpsimd.memset(id32[:, :], 0.0))
            pool_order.inc(nc.gpsimd.memset(kept.eye2[:, :], 0.0))
            pool_order.inc(nc.gpsimd.memset(kept.neg_half[:, :], -0.5))
            nc.gpsimd.memset(l0.stage[:, NQ - 1, QT - 1, :], 0).then_inc(stage_clear, 1)
            pool.wait_ge(pool_order.sem, pool_order.now())
            pool_order.inc(nc.gpsimd.affine_select(out=id32[:, :], in_=id32[:, :], compare_op=ALU.not_equal, fill=1.0,
                                                   base=0, pattern=[[-1, P]], channel_multiplier=1))
            pool_order.inc(nc.gpsimd.affine_select(out=kept.eye2[:, :], in_=kept.eye2[:, :], compare_op=ALU.not_equal,
                                                   fill=1.0, base=0, pattern=[[-1, D]], channel_multiplier=1))
            pool.wait_ge(pool_order.sem, pool_order.now())
            pool_order.inc(nc.gpsimd.affine_select(out=kept.eye2[:, :], in_=kept.eye2[:, :], compare_op=ALU.not_equal,
                                                   fill=1.0, base=-D, pattern=[[-1, D]], channel_multiplier=1))
            nc.gpsimd.tensor_copy(id16[:, :], id32[:, :]).then_inc(ident_ready, 1)
            nc.gpsimd.tensor_copy(idb[:, :], id32[:, :]).then_inc(ident_ready, 1)

        @block.scalar
        def _(act):
            act.dma_start(a0[:, :], A["a0"]).then_inc(a0_in, 16)
            for l, w in enumerate(("w0", "w2", "w3")):
                for half in (0, D):
                    act.dma_start(kept.w_raw[half:half + D, l, 0:D], A[w]).then_inc(w_in, 16)
            act.dma_start(av[:, 0, :, :].rearrange("p i d -> p (i d)"), A["a2"].unsqueeze(0).to_broadcast([P, 2 * D])
                          ).then_inc(av_in, 16)
            act.dma_start(av[:, 1, :, :].rearrange("p i d -> p (i d)"), A["a3"].rearrange("d o -> o d").to_broadcast([P, 2 * D])
                          ).then_inc(av_in, 16)
            def split_hi(bp, par, q):
                b, Q = 2 * bp + par, number(bp, par, q)
                if q == 0:
                    act.wait_ge(x_in[par], 16 * bp + 16)
                if not before(Q, 2):
                    act.wait_ge(x_t, Q - 1)
                nc.scalar.activation(xs[:, q % 2, :, 0:D], x[:, b, QT * q:QT * q + QT, :], ACT.Copy, scale=SX
                                     ).then_inc(x_hi, 1)

            def keep_x(q, Q):
                act.wait_ge(x_t, Q + 1)
                if not before(Q, 2):
                    act.wait_ge(h_done, Q - 1)
                nc.scalar.copy(xt[:, q % 2, :, :], ps_t[q % 2]).then_inc(x_tk, 1)

            def step(bp, par, q):
                b, Q = 2 * bp + par, number(bp, par, q)
                if after(bp, par, q, 2):
                    split_hi(*after(bp, par, q, 2))
                if after(bp, par, q, 1):
                    keep_x(after(bp, par, q, 1)[2], Q + 1)
                act.wait_ge(h_done, Q + 1)
                nc.scalar.activation(l0.h_hi[:, QT * q:QT * q + QT, b, :], ps_h[q % 2], ACT.Copy, scale=SH / SX / SX
                                     ).then_inc(h_hi, 1)

            split_hi(0, 0, 0)
            split_hi(0, 0, 1)
            keep_x(0, 0)
            for r in range(NQ):
                act.wait_ge(a0T, r + 1)
                nc.scalar.copy(l0.a12[:, QT * r:QT * r + QT, :],
                               psum[:, 2048 + 512 * r:2560 + 512 * r].rearrange("p (t d) -> p t d", t=QT)
                               ).then_inc(a0_kept, 1)
            stages(step, act)

        @block.vector
        def _(dve):
            def link(ins):
                vec_order.inc(ins)
                dve.wait_ge(vec_order.sem, vec_order.now())

            def split_lo(bp, par, q):
                b, Q = 2 * bp + par, number(bp, par, q)
                if q == 0:
                    dve.wait_ge(x_in[par], 16 * bp + 16)
                dve.wait_ge(x_hi, Q + 1)
                nc.vector.scalar_tensor_tensor(out=xs[:, q % 2, :, D:P], in0=x[:, b, QT * q:QT * q + QT, :], scalar=SX,
                                               in1=xs[:, q % 2, :, 0:D], op0=ALU.mult, op1=ALU.subtract
                                               ).then_inc(x_lo, 1)

            def step(bp, par, q):
                b, Q = 2 * bp + par, number(bp, par, q)
                if after(bp, par, q, 2):
                    split_lo(*after(bp, par, q, 2))
                dve.wait_ge(h_hi, Q + 1)
                if not before(Q, 2):
                    dve.wait_ge(sc_done, Q - 1)
                nc.vector.tensor_tensor(prod[:, q % 2, :, :], ps_h[q % 2], l0.a12[:, QT * q:QT * q + QT, 0:D], ALU.mult
                                        ).then_inc(pr_done, 1)
                nc.vector.scalar_tensor_tensor(out=l0.h_lo[:, QT * q:QT * q + QT, b, :], in0=ps_h[q % 2],
                                               scalar=SH / SX / SX, in1=l0.h_hi[:, QT * q:QT * q + QT, b, :],
                                               op0=ALU.mult, op1=ALU.subtract).then_inc(h_used, 1)
                dve.wait_ge(pr_done, Q + 1)
                nc.vector.tensor_reduce(l0.sc1[:, b, QT * q:QT * q + QT], prod[:, q % 2, :, :], X, ALU.add
                                        ).then_inc(sc_done, 1)

            split_lo(0, 0, 0)
            split_lo(0, 0, 1)
            link(nc.vector.memset(l0.ones[:, :, :], 1.0))
            nc.vector.memset(l0.ones[0:1, 0, :], 0.0).then_inc(ones_set, 1)
            link(nc.vector.memset(kept.w_raw[:, 0, D:D + 2], 0.0))
            dve.wait_ge(w_in, 96)
            dve.wait_ge(av_in, 32)
            for i in (0, 1):
                link(nc.vector.tensor_tensor(wa[:, :, i, :], kept.w_raw[:, 1:3, 0:D], av[:, :, i, :], ALU.mult))
            for l in (0, 1):
                link(nc.vector.tensor_reduce(kept.w_raw[:, 1 + l, D:D + 2], wa[:, l, :, :], X, ALU.add))
            link(nc.vector.tensor_scalar(w256[:, :, :], kept.w_raw[:, :, :], SX, None, ALU.mult))
            link(nc.vector.tensor_copy(kept.w_hi[:, :, :], w256[:, :, :]))
            nc.vector.tensor_tensor(kept.w_lo[:, :, :], w256[:, :, :], kept.w_hi[:, :, :], ALU.subtract
                                    ).then_inc(w_ready, 1)
            dve.wait_ge(a0_kept, NQ)
            stages(step, dve)
            dve.wait_ge(sc_done, B * NQ)
            link(nc.vector.tensor_scalar(l0.sc1[:, :, :], l0.sc1[:, :, :], 1.0 / SX / SX, None, ALU.mult))
            link(nc.vector.memset(l0.sc1[0:1, :, 0], 0.0))
            link(nc.vector.memset(l0.c6[:, :], 1.0 / SH))
            link(nc.vector.memset(l0.c6[0:1, 0:1], 0.0))
            dve.wait_ge(ident_ready, 1)
            link(nc.vector.tensor_scalar(l0.not_last[:, :], id16[:, P - 1:P], -1.0, 1.0, ALU.mult, ALU.add))
            dve.wait_ge(hs_done, B)
            link(nc.vector.tensor_scalar(l0.hsum[:, :, :].rearrange("p b d -> p (b d)"), ps_s, 1.0 / SH, None, ALU.mult))
            for half in (l0.h_hi, l0.h_lo):
                link(nc.vector.memset(half[0:1, 0, :, :], 0.0))
                link(nc.vector.tensor_scalar(half[:, T - 1, :, :], half[:, T - 1, :, :], l0.not_last[:, :], None,
                                             ALU.mult))

        @block.tensor
        def _(pe):
            def turn(q, Q):
                pe.wait_ge(x_hi, Q + 1)
                pe.wait_ge(x_lo, Q + 1)
                if not before(Q, 2):
                    pe.wait_ge(x_tk, Q - 1)
                for k in range(QT):
                    mm = nc.tensor.transpose(ps_t[q % 2][:, k, :], xs[:, q % 2, k, :], id16[:, :])
                mm.then_inc(x_t, 1)

            def sum_rows(b):
                pe.wait_ge(h_used, NQ * b + NQ)
                for half in (l0.h_hi, l0.h_lo):
                    for t in range(T):
                        mm = nc.tensor.matmul(ps_s[:, D * b:D * b + D] if isinstance(b, int) else ps_s[:, bass.ds(D * b, D)],
                                              l0.ones[:, min(t, 1), :], half[:, t, b, :],
                                              start=(half is l0.h_hi and t == 0), stop=(half is l0.h_lo and t == T - 1))
                mm.then_inc(hs_done, 1)

            def step(bp, par, q):
                b, Q = 2 * bp + par, number(bp, par, q)
                if after(bp, par, q, 1):
                    turn(after(bp, par, q, 1)[2], Q + 1)
                pe.wait_ge(x_tk, Q + 1)
                if not before(Q, 2):
                    pe.wait_ge(h_used, Q - 1)
                    pe.wait_ge(h_hi, Q - 1)
                for k in range(QT):
                    for w in (kept.w_hi, kept.w_lo):
                        mm = nc.tensor.matmul(ps_h[q % 2][:, k, :], xt[:, q % 2, k, :], w[:, 0, 0:D],
                                              start=(w is kept.w_hi), stop=(w is kept.w_lo))
                mm.then_inc(h_done, 1)
                if q == 2 and not before(Q, NQ):
                    sum_rows(b - 1)

            pe.wait_ge(ident_ready, 2)
            turn(0, 0)
            pe.wait_ge(a0_in, 16)
            for t in range(T):
                tr = nc.tensor.transpose(psum[:, 2048 + P * t:2048 + P * t + P], a0[:, P * t:P * t + P], id32[:, :])
                if t % QT == QT - 1:
                    tr.then_inc(a0T, 1)
            pe.wait_ge(w_ready, 1)
            pe.wait_ge(ones_set, 1)
            pe.wait_ge(a0_kept, NQ)
            stages(step, pe)
            sum_rows(B - 1)


def load_adj(sp, adj, stage, r, cq, sem):
    cols = slice(512 * cq, 512 * cq + 512)
    lo = 1 + 512 * r
    if r < NQ - 1:
        sp.dma_start(stage[:, r, :, :], adj[lo:lo + 512, cols].rearrange("(t p) c -> p t c", p=P)).then_inc(sem, 16)
    else:
        sp.dma_start(stage[:, r, 0:3, :], adj[lo:lo + 384, cols].rearrange("(t p) c -> p t c", p=P)).then_inc(sem, 16)
        sp.dma_start(stage[0:112, r, 3, :], adj[lo + 384:lo + 496, cols]).then_inc(sem, 16)
        sp.dma_start(stage[112:127, r, 3, :], adj[lo + 496:lo + 511, cols]).then_inc(sem, 16)


def layer_0(nc, kept, l0, sems, A, psum):
    x, maskT = kept.x, kept.maskT
    cast, turned, mask_kept, tile_used = sems("m_cast"), sems("m_turned"), sems("m_kept"), sems("m_tile_used")
    acc_done, acc_read = sems("l0_acc_done"), sems("l0_acc_read")
    row0_kept = sems("row0_kept")
    yc_ready, sq_done, var_ready, rstd_ready, x_done = (sems(n) for n in (
        "l0_yc", "l0_sq", "l0_var", "l0_rstd", "l0_x_done"))

    with ExitStack() as ctx:
        def sb(name, shape, dt):
            return ctx.enter_context(nc.sbuf_tensor(name, shape, dt))

        RING = 8
        tile = sb("mask_tiles", [P, RING, 512], BF16)
        m1 = sb("m1", [P, QT, B, D], F32)
        v = sb("v0", [P, 2, B, D], F32)
        y = sb("y0", [P, 2, B, D], F32)
        yc = sb("yc0", [P, 2, B, D], F32)
        sq = sb("sq0", [P, 2, B, D], F32)
        st = sb("st0", [P, 2, 8, B], F32)
        acc = [psum[:, 512 * i:512 * i + 512] for i in range(QT)]
        ps_m = [psum[:, 512 * i:512 * i + 256].bitcast(BF16).rearrange("p (c n) -> p c n", c=QT) for i in (4, 5)]
        ps_s = psum[:, 512 * 6:512 * 7]
        block = ctx.enter_context(nc.Block())

        @block.sync
        def _(sp):
            for cq in range(1, NQ):
                for r in range(NQ):
                    sp.wait_ge(cast, T * cq - T + QT * r + QT)
                    load_adj(sp, A["adj"], l0.stage, r, cq, l0.adj_in[r])

        @block.gpsimd
        def _(pool):
            def finish(cq, c):
                J, r = QT * cq + c, c % 2
                s = st[:, r, :, :]
                pool.wait_ge(yc_ready, J + 1)
                nc.gpsimd.tensor_tensor(sq[:, r, :, :], yc[:, r, :, :], yc[:, r, :, :], ALU.mult).then_inc(sq_done, 1)
                pool.wait_ge(var_ready, J + 1)
                nc.gpsimd.tensor_tensor(s[:, 4, :], s[:, 3, :], kept.neg_half[:, 0:B], ALU.pow).then_inc(rstd_ready, 1)
                pool.wait_ge(rstd_ready, J + 1)
                nc.gpsimd.tensor_tensor(x[:, :, bass.ds(J, 1), :].rearrange("p b o d -> p b (o d)"), yc[:, r, :, :],
                                        over(s[:, 4, :], [P, B, D], 2), ALU.mult).then_inc(x_done, 1)

            with pool.Fori(0, NQ) as cq:
                for c in range(QT):
                    finish(cq, c)

        @block.scalar
        def _(act):
            def sweep(cq, first):
                for t in range(T):
                    m = T * cq + t
                    act.wait_ge(turned, m + 1)
                    n = P if t < T - 1 else P - 1
                    nc.scalar.copy(maskT[:, bass.ds(QT * cq, QT), 1 + P * t:1 + P * t + n], ps_m[t % 2][:, :, 0:n]
                                   ).then_inc(mask_kept, 1)

            sweep(0, True)
            with act.Fori(1, NQ) as cq:
                sweep(cq, False)

        @block.tensor
        def _(pe):
            def sweep(cq, first):
                for t in range(T):
                    m = T * cq + t
                    pe.wait_ge(cast, m + 1)
                    if not (first and t < 2):
                        pe.wait_ge(mask_kept, m - 1)
                    for c in range(QT):
                        tr = nc.tensor.transpose(ps_m[t % 2][:, c, :], tile[:, t % RING, P * c:P * c + P], kept.idb[:, :])
                    tr.then_inc(turned, 1)
                    for c in range(QT):
                        if t == 0 and not first:
                            pe.wait_ge(acc_read, QT * cq - QT + c + 1)
                        for half in (l0.h_hi, l0.h_lo):
                            mm = nc.tensor.matmul(acc[c], tile[:, t % RING, P * c:P * c + P],
                                                  half[:, t, :, :].rearrange("p b d -> p (b d)"),
                                                  start=(t == 0 and half is l0.h_hi),
                                                  stop=(t == T - 1 and half is l0.h_lo))
                        if t == T - 1:
                            mm.then_inc(acc_done, 1)
                    if t < T - 1:
                        mm.then_inc(tile_used, 1)
                    else:
                        nc.tensor.matmul(ps_s[:, 0:1], l0.ones[:, 1, :], l0.ones[:, 1, 0:1], start=True, stop=True
                                         ).then_inc(tile_used, 1)

            sweep(0, True)
            with pe.Fori(1, NQ) as cq:
                sweep(cq, False)

        @block.vector
        def _(dve):
            dve.wait_ge(l0.row0_in, 16)
            nc.vector.tensor_scalar(maskT[:, :, 0], l0.row0[:, :], 0, None, ALU.is_gt).then_inc(row0_kept, 1)

            def post_read(cq):
                for c in range(QT):
                    J = QT * cq + c
                    dve.wait_ge(acc_done, J + 1)
                    a2 = l0.a12[:, bass.ds(J, 1), D:P].to_broadcast([P, B, D])
                    nc.vector.tensor_tensor(m1[:, c, :, :], acc[c].rearrange("p (b d) -> p b d", b=B), a2, ALU.mult
                                            ).then_inc(acc_read, 1)

            def post(cq, c, part):
                J, r = QT * cq + c, c % 2
                s = st[:, r, :, :]

                def lk(k, ins):
                    ins.then_inc(post_order, 1)
                    dve.wait_ge(post_order, POST * J + k)

                xj = x[:, :, bass.ds(J, 1), :].rearrange("p b o d -> p b (o d)")
                if part == 1:
                    dve.wait_ge(m1_summed, J + 1)
                    lk(1, nc.vector.scalar_tensor_tensor(out=s[:, 1, :], in0=s[:, 0, :], scalar=l0.c6[:, bass.ds(J, 1)],
                                                         in1=l0.sc1[:, :, bass.ds(J, 1)].rearrange("p b o -> p (b o)"),
                                                         op0=ALU.mult, op1=ALU.add))
                    lk(2, nc.vector.tensor_tensor(v[:, r, :, :], l0.hsum[:, :, :], over(s[:, 1, :], [P, B, D], 2), ALU.mult))
                    lk(3, nc.vector.scalar_tensor_tensor(out=y[:, r, :, :], in0=v[:, r, :, :], scalar=0.2, in1=v[:, r, :, :],
                                                         op0=ALU.mult, op1=ALU.max))
                if part == 2:
                    lk(4, nc.vector.tensor_tensor(v[:, r, :, :], y[:, r, :, :], xj, ALU.add))
                    lk(5, nc.vector.tensor_reduce(s[:, 2, :], v[:, r, :, :], X, ALU.add))
                    if not (isinstance(cq, int) and cq == 0 and c < 2):
                        dve.wait_ge(x_done, J - 1)
                    nc.vector.scalar_tensor_tensor(out=yc[:, r, :, :], in0=over(s[:, 2, :], [P, B, D], 2),
                                                   scalar=-1.0 / D, in1=v[:, r, :, :], op0=ALU.mult, op1=ALU.add
                                                   ).then_inc(yc_ready, 1)
                if part == 3:
                    dve.wait_ge(sq_done, J + 1)
                    nc.vector.tensor_reduce(s[:, 5, :], sq[:, r, :, :], X, ALU.add).then_inc(sq_summed, 1)
                    dve.wait_ge(sq_summed, J + 1)
                    nc.vector.tensor_scalar(s[:, 3, :], s[:, 5, :], 1.0 / D, EPS, ALU.mult, ALU.add).then_inc(var_ready, 1)

            def sum_m1(cq, c):
                J = QT * cq + c
                dve.wait_ge(acc_read, J + 1)
                if not (isinstance(cq, int) and cq == 0 and c < 2):
                    dve.wait_ge(post_order, POST * (J - 2) + 1)
                nc.vector.tensor_reduce(st[:, c % 2, 0, :], m1[:, c, :, :], X, ALU.add).then_inc(m1_summed, 1)

            PARTS = ((4, 0, 0), (4, 0, 1), (5, 0, 2), (7, 1, 0), (7, 1, 1), (8, 0, 3), (8, 1, 2), (10, 2, 0), (10, 2, 1),
                     (11, 1, 3), (11, 2, 2), (13, 3, 0), (13, 3, 1), (14, 2, 3), (14, 3, 2), (15, 3, 3))

            def parts(cq, at=None):
                for t, c, part in PARTS:
                    if at is None or t == at:
                        if part == 0:
                            sum_m1(cq, c)
                        else:
                            post(cq, c, part)

            POST = 5
            post_order, m1_summed, sq_summed = sems("l0_post"), sems("m1_summed"), sems("sq_summed")

            def sweep(cq, first):
                for t in range(T):
                    m = T * cq + t
                    if t % QT == 0:
                        dve.wait_ge(l0.adj_in[t // QT], (48 if t // QT == NQ - 1 else 16) * (cq + 1))
                    if not (first and t < RING):
                        dve.wait_ge(tile_used, m - RING + 1)
                    nc.vector.tensor_scalar(tile[:, t % RING, :], l0.stage[:, t // QT, t % QT, :], 0, None, ALU.is_gt
                                            ).then_inc(cast, 1)
                    if not first and t == 3:
                        post_read(cq - 1)
                    if not first:
                        parts(cq - 1, t)

            sweep(0, True)
            sweep(1, False)
            with dve.Fori(2, NQ) as cq:
                sweep(cq, False)
            post_read(NQ - 1)
            parts(NQ - 1)


def layer_1(nc, kept, sems, psum):
    x, maskT = kept.x, kept.maskT
    qk_done, exp_done, mul_done, pv_done = sems("qk_done"), sems("exp_done"), sems("mul_done"), sems("pv_done")
    hi_done, lo_done, turned, ab_ready = sems("a_hi"), sems("a_lo"), sems("a_turned"), sems("a_ready")
    xv_ready = sems("xv_ready")
    o_out, o_turned, o_rows = sems("o_out"), sems("o_turned"), sems("o_rows")
    sum_wide, mean_ps, mean_kept = sems("sum_wide"), sems("mean_ps"), sems("mean_kept")
    q_summed, mean_spread, filled = sems("q_summed"), sems("mean_spread"), sems("filled")
    yc_ready, sq_done, var_ready, rstd_ready = sems("l1_yc"), sems("l1_sq"), sems("l1_var"), sems("l1_rstd")
    post_order, x_done = sems("l1_post"), sems("l1_x_done")
    CH = 2 * T
    LAG = 4
    POST = 8

    with ExitStack() as ctx:
        def sb(name, shape, dt):
            return ctx.enter_context(nc.sbuf_tensor(name, shape, dt))

        xa = sb("xa", [P, 2, N], F16)
        xb = sb("xb", [P, 2, N], F16)
        xs = sb("xs1", [P, QT, 3, D], F16)
        xv = sb("xv", [P, 2, T, D], F32)
        e = sb("e", [P, 4, 1024], F32)
        pm = sb("pm", [P, 2 * LAG, 1024], F32)
        oT = sb("oT", [P, 1024], F32)
        o = sb("o", [P, T, D], F32)
        y = sb("y1", [P, T, D], F32)
        yc = sb("yc1", [P, T, D], F32)
        st = sb("st1", [P, 8, T], F32)
        none = sb("none1", [P, T], F32)
        fill = sb("fill1", [P, T, D], F32)
        qsum = sb("qsum1", [P, 2, NQ], F32)
        wide = sb("wide1", [P, P], F32)
        mean = sb("mean1", [P, 2, D], F32)
        S = [psum[:, 1024 * h:1024 * h + 1024] for h in (0, 1)]
        acc = [psum[:, 2048 + 512 * j:2560 + 512 * j] for j in (0, 1)]
        ps_x = psum[:, 3072:3584].bitcast(F16).rearrange("p (u t n) -> p u t n", u=2, t=QT)
        ps_o = psum[:, 3584:3840]
        ps_mean = psum[:, 3840:3840 + D]
        block = ctx.enter_context(nc.Block())

        @block.gpsimd
        def _(pool):
            nc.gpsimd.memset(xv[:, :, :, D - 1:D], 1.0).then_inc(xv_ready, 1)
            nc.gpsimd.tensor_copy(xv[:, 0, :, 0:D - 1], x[:, 0, :, 0:D - 1]).then_inc(xv_ready, 1)

            def fill_of(g, par):
                pool.wait_ge(mean_kept, g + 1)
                pool.wait_ge(post_order, POST * g + 1)
                nc.gpsimd.tensor_tensor(fill[:, :, :], over(none[:, :], [P, T, D], 2), over(mean[:, par, :], [P, T, D], 1),
                                        ALU.mult).then_inc(mean_spread, 1)
                pool.wait_ge(mean_spread, g + 1)
                nc.gpsimd.tensor_tensor(fill[:, :, :], fill[:, :, :], x[:, g, :, :], ALU.add).then_inc(filled, 1)

            def rstd(g):
                pool.wait_ge(var_ready, g + 1)
                nc.gpsimd.tensor_tensor(st[:, 5, :], st[:, 4, :], kept.neg_half[:, :], ALU.pow).then_inc(rstd_ready, 1)

            def body(b, par, first):
                if not first:
                    pool.wait_ge(pv_done, T * b)
                nc.gpsimd.tensor_copy(xv[:, 1 - par, :, 0:D - 1], x[:, after(b), :, 0:D - 1]).then_inc(xv_ready, 1)
                if not first:
                    fill_of(b - 1, 1 - par)
                    rstd(b - 1)

            def after(b):
                return b + 1

            body(0, 0, True)
            body(1, 1, False)
            with pool.Fori(1, B // 2 - 1) as bp:
                body(2 * bp, 0, False)
                body(2 * bp + 1, 1, False)
            body(B - 2, 0, False)
            fill_of(B - 2, 0)
            rstd(B - 2)
            fill_of(B - 1, 1)
            rstd(B - 1)

        @block.tensor
        def _(pe):
            def pv(b, par, mt, s):
                pe.wait_ge(mul_done, 2 * s + 2)
                if mt == 0:
                    pe.wait_ge(xv_ready, b + 2)
                for j in (0, 1):
                    for h in (0, 1):
                        mm = nc.tensor.matmul(acc[j][D * h:D * h + D, :], xv[:, par, mt, :],
                                              pm[:, 2 * (mt % LAG) + h, 512 * j:512 * j + 512],
                                              start=(mt == 0), stop=(mt == T - 1))
                mm.then_inc(pv_done, 1)

            def turn_x(par, q, Q):
                pe.wait_ge(hi_done, Q + 1)
                pe.wait_ge(lo_done, Q + 1)
                if not (isinstance(Q, int) and Q == 0):
                    pe.wait_ge(ab_ready, Q)
                for u in (0, 1):
                    for k in range(QT):
                        tr = nc.tensor.transpose(ps_x[:, u, k, :], xs[:, k, u:u + 2, :].rearrange("p u d -> p (u d)"),
                                                 kept.id16[:, :])
                tr.then_inc(turned, 1)

            def turn_o(g, i):
                pe.wait_ge(o_out, 2 * g + 2)
                if not (isinstance(g, int) and g == 0 and i == 0):
                    pe.wait_ge(o_rows, 4 * g + i)
                if i == 0 and not (isinstance(g, int) and g == 0):
                    pe.wait_ge(mean_kept, g + 1)
                for k in (0, 1):
                    tr = nc.tensor.transpose(ps_o[:, P * k:P * k + P], oT[:, P * (2 * i + k):P * (2 * i + k) + P],
                                             kept.id32[:, :])
                tr.then_inc(o_turned, 1)

            def mean_of(g):
                pe.wait_ge(sum_wide, g + 1)
                if not (isinstance(g, int) and g == 0):
                    pe.wait_ge(o_rows, 4 * g)
                nc.tensor.matmul(ps_mean, wide[:, :], kept.eye2[:, :], start=True, stop=True).then_inc(mean_ps, 1)

            def body(b, par, first, last=False):
                for mt in range(T):
                    s = T * b + mt
                    if mt == 0:
                        pe.wait_ge(ab_ready, NQ * b + NQ)
                    for h in (0, 1):
                        if not (first and mt == 0):
                            pe.wait_ge(exp_done, 2 * s + h - 1)
                        for nb in (0, 1):
                            for xm in (xa, xb):
                                mm = nc.tensor.matmul(S[h][:, 512 * nb:512 * nb + 512],
                                                      xa[:, par, P * mt:P * mt + P],
                                                      xm[:, par, 1024 * h + 512 * nb:1024 * h + 512 * nb + 512],
                                                      start=(xm is xa), stop=(xm is xb))
                        mm.then_inc(qk_done, 1)
                    if mt > 1:
                        if mt == 2 and not first:
                            pe.wait_ge(o_out, 2 * b)
                        pv(b, par, mt - 2, s - 2)
                    elif not first:
                        pv(b - 1, 1 - par, T - 2 + mt, s - 2)
                    if mt % 3 == 2 and mt < 12 and not last:
                        turn_x(1 - par, mt // 3, NQ * b + NQ + mt // 3)
                    if mt in (2, 3, 4, 5) and not first:
                        turn_o(b - 1, mt - 2)
                    if mt == 10:
                        mean_of(b)

            for q in range(NQ):
                turn_x(0, q, q)
            body(0, 0, True)
            body(1, 1, False)
            with pe.Fori(1, B // 2 - 1) as bp:
                body(2 * bp, 0, False)
                body(2 * bp + 1, 1, False)
            body(B - 2, 0, False)
            body(B - 1, 1, False, last=True)
            pv(B - 1, 1, T - 2, T * B - 2)
            pv(B - 1, 1, T - 1, T * B - 1)
            for i in range(4):
                turn_o(B - 1, i)

        @block.scalar
        def _(act):
            def split_hi(b, q, Q, first):
                if not first:
                    act.wait_ge(turned, Q)
                nc.scalar.activation(xs[:, :, 0:3:2, :], over(x[:, b, QT * q:QT * q + QT, :], [P, QT, 2, D], 2),
                                     ACT.Copy, scale=SX).then_inc(hi_done, 1)

            def keep_x(par, q, Q):
                act.wait_ge(turned, Q + 1)
                nc.scalar.activation(xa[:, par, 512 * q:512 * q + 512], ps_x[:, 0, :, :].rearrange("p t n -> p (t n)"),
                                     ACT.Copy, accum_out=qsum[:, par, q:q + 1])
                nc.scalar.copy(xb[:, par, 512 * q:512 * q + 512], ps_x[:, 1, :, :].rearrange("p t n -> p (t n)")
                               ).then_inc(ab_ready, 1)

            def keep_o(g, i):
                act.wait_ge(o_turned, 4 * g + i + 1)
                if i == 0 and not (isinstance(g, int) and g == 0):
                    act.wait_ge(x_done, g)
                nc.scalar.copy(o[:, :, :].rearrange("p (h t) d -> p t h d", h=2)[:, 2 * i:2 * i + 2, :, :],
                               ps_o.rearrange("p (t h d) -> p t h d", t=2, h=2)).then_inc(o_rows, 1)

            def out_sums(g):
                act.wait_ge(pv_done, T * g + T)
                if not (isinstance(g, int) and g == 0):
                    act.wait_ge(o_turned, 4 * g)
                nc.scalar.copy(oT[:, 0:512], psum[:, 2048:2560]).then_inc(o_out, 1)

            def square(g):
                act.wait_ge(yc_ready, g + 1)
                nc.scalar.activation(y[:, :, :], yc[:, :, :], ACT.Square).then_inc(sq_done, 1)

            def body(b, par, first, last=False):
                for mt in range(T):
                    s = T * b + mt
                    for h in (0, 1):
                        act.wait_ge(qk_done, 2 * s + h + 1)
                        if not (first and mt < 2):
                            act.wait_ge(mul_done, 2 * s + h - 3)
                        nc.scalar.activation(e[:, (2 * mt + h) % 4, :], S[h], ACT.Exp, scale=1.0 / SX / SX / 8.0
                                             ).then_inc(exp_done, 1)
                    if mt == 1 and not first:
                        out_sums(b - 1)
                    if mt % 3 == 0 and mt <= 12 and not last:
                        q = mt // 3
                        if q > 0:
                            keep_x(1 - par, q - 1, NQ * b + NQ + q - 1)
                        if q < NQ:
                            split_hi(b + 1, q, NQ * b + NQ + q, False)
                    if mt in (3, 4, 5, 6) and not first:
                        keep_o(b - 1, mt - 3)
                    if mt == 13 and not first:
                        square(b - 1)

            for q in range(NQ):
                split_hi(0, q, q, q == 0)
                keep_x(0, q, q)
            body(0, 0, True)
            body(1, 1, False)
            with act.Fori(1, B // 2 - 1) as bp:
                body(2 * bp, 0, False)
                body(2 * bp + 1, 1, False)
            body(B - 2, 0, False)
            body(B - 1, 1, False, last=True)
            out_sums(B - 1)
            for i in range(4):
                keep_o(B - 1, i)
            square(B - 1)

        @block.vector
        def _(dve):
            def split_lo(b, q, Q):
                dve.wait_ge(hi_done, Q + 1)
                nc.vector.scalar_tensor_tensor(out=xs[:, :, 1, :], in0=x[:, b, QT * q:QT * q + QT, :], scalar=SX,
                                               in1=xs[:, :, 0, :], op0=ALU.mult, op1=ALU.subtract).then_inc(lo_done, 1)

            def widen(par, g):
                dve.wait_ge(ab_ready, NQ * g + NQ)
                link1(g, nc.vector.tensor_reduce(st[:, 7, 0:1], qsum[:, par, :], X, ALU.add))
                nc.vector.tensor_scalar(wide[:, :], st[:, 7, 0:1].to_broadcast([P, P]), 1.0 / SX / N, None, ALU.mult
                                        ).then_inc(sum_wide, 1)

            def link1(g, ins):
                ins.then_inc(q_summed, 1)
                dve.wait_ge(q_summed, g + 1)

            def link(g, k, ins):
                ins.then_inc(post_order, 1)
                dve.wait_ge(post_order, POST * g + k)

            def post(par, g, part):
                xg = x[:, g, :, :]
                if part == 1:
                    dve.wait_ge(o_rows, 4 * g + 4)
                    if not (isinstance(g, int) and g == 0):
                        dve.wait_ge(filled, g)
                    link(g, 1, nc.vector.tensor_scalar(none[:, :], o[:, :, D - 1], 0.0, None, ALU.is_equal))
                    link(g, 2, nc.vector.tensor_tensor(st[:, 0, :], o[:, :, D - 1], none[:, :], ALU.add))
                    link(g, 3, nc.vector.reciprocal(st[:, 1, :], st[:, 0, :]))
                    link(g, 4, nc.vector.tensor_reduce(o[:, :, D - 1:D], o[:, :, 0:D - 1], X, ALU.add, negate=True))
                if part == 2:
                    link(g, 5, nc.vector.tensor_tensor(o[:, :, :], o[:, :, :], over(st[:, 1, :], [P, T, D], 2), ALU.mult))
                if part == 4:
                    dve.wait_ge(filled, g + 1)
                    link(g, 6, nc.vector.tensor_tensor(y[:, :, :], o[:, :, :], fill[:, :, :], ALU.add))
                if part == 5:
                    link(g, 7, nc.vector.tensor_reduce(st[:, 2, :], y[:, :, :], X, ALU.add))
                    nc.vector.scalar_tensor_tensor(out=yc[:, :, :], in0=over(st[:, 2, :], [P, T, D], 2), scalar=-1.0 / D,
                                                   in1=y[:, :, :], op0=ALU.mult, op1=ALU.add).then_inc(yc_ready, 1)
                if part == 6:
                    dve.wait_ge(sq_done, g + 1)
                    link(g, 8, nc.vector.tensor_reduce(st[:, 3, :], y[:, :, :], X, ALU.add))
                    nc.vector.tensor_scalar(st[:, 4, :], st[:, 3, :], 1.0 / D, EPS, ALU.mult, ALU.add
                                            ).then_inc(var_ready, 1)
                if part == 7:
                    dve.wait_ge(rstd_ready, g + 1)
                    nc.vector.tensor_tensor(xg, yc[:, :, :], over(st[:, 5, :], [P, T, D], 2), ALU.mult).then_inc(x_done, 1)

            def out_sums(g):
                dve.wait_ge(pv_done, T * g + T)
                if not (isinstance(g, int) and g == 0):
                    dve.wait_ge(o_turned, 4 * g)
                nc.vector.tensor_copy(oT[:, 512:1024], psum[:, 2560:3072]).then_inc(o_out, 1)

            def body(b, par, first, last=False):
                for mt in range(T):
                    s = T * b + mt
                    if mt == 2 and not first:
                        out_sums(b - 1)
                    for h in (0, 1):
                        dve.wait_ge(exp_done, 2 * s + h + 1)
                        if not (first and mt < LAG):
                            dve.wait_ge(pv_done, s - LAG + 1)
                        nc.vector.tensor_tensor(pm[:, 2 * (mt % LAG) + h, :], e[:, (2 * mt + h) % 4, :],
                                                maskT[:, mt, 1024 * h:1024 * h + 1024], ALU.mult).then_inc(mul_done, 1)
                    if mt < 12 and mt % 3 == 1 and not last:
                        split_lo(b + 1, mt // 3, NQ * b + NQ + mt // 3)
                    if mt == 0:
                        widen(par, b)
                    if mt == 11:
                        dve.wait_ge(mean_ps, b + 1)
                        nc.vector.tensor_copy(mean[:, par, :], ps_mean).then_inc(mean_kept, 1)
                    if not first and mt in PART_AT:
                        post(1 - par, b - 1, PART_AT[mt])

            for q in range(NQ):
                split_lo(0, q, q)
            PART_AT = {7: 1, 8: 2, 9: 4, 10: 5, 13: 6, 15: 7}
            body(0, 0, True)
            body(1, 1, False)
            with dve.Fori(1, B // 2 - 1) as bp:
                body(2 * bp, 0, False)
                body(2 * bp + 1, 1, False)
            body(B - 2, 0, False)
            body(B - 1, 1, False, last=True)
            out_sums(B - 1)
            for part in (1, 2, 4, 5, 6, 7):
                post(1, B - 1, part)


def layers_2_3(nc, kept, sems, psum, scratch, out):
    x, maskT = kept.x, kept.maskT
    BIG = 2.0 ** 40
    SV = 256.0
    W1 = D + 1
    LEAD = 4
    G = 2 * B
    relu_done, mp_done, av_done, evac = sems("relu_done"), sems("mp_done"), sems("av_done"), sems("uv_evac")
    hi_done, lo_done, turned, xt_ready, h_ps, h_kept = (sems(n) for n in (
        "g_hi", "g_lo", "g_turned", "g_xt", "g_h_ps", "g_h_kept"))
    top_part, top_all, args_ready, ex_ready, bias_ready = (sems(n) for n in (
        "top_part", "top_all", "args_ready", "ex_ready", "bias_ready"))
    v_done, v_hi, v_lo, v_ready = sems("v_done"), sems("v_hi"), sems("v_lo"), sems("v_ready")
    q_summed, sum_wide, mean_ps, mean_kept = sems("g_q_summed"), sems("g_wide"), sems("g_mean_ps"), sems("g_mean_kept")
    s_out, r_in = sems("s_out"), [sems("r_in0"), sems("r_in1")]
    uv_used, elu_in, elu_out = sems("uv_used"), sems("elu_in"), sems("elu_out")
    filled, mean_spread = sems("g_filled"), sems("g_mean_spread")
    yc_ready, sq_done, var_ready, rstd_ready = sems("g_yc"), sems("g_sq"), sems("g_var"), sems("g_rstd")
    post_order, sc_order, x_done, out_done, ones_set = (sems(n) for n in (
        "g_post", "g_sc", "g_x_done", "out_done", "ones_set"))
    POST, SC = 9, 2

    with ExitStack() as ctx:
        def sb(name, shape, dt):
            return ctx.enter_context(nc.sbuf_tensor(name, shape, dt))

        si = sb("si", [P, 2, N], F32)
        z = sb("z", [P, 2, N], BF16)
        mp = sb("mp", [P, LEAD, N], BF16)
        mn = sb("mn", [P, 2, N], BF16)
        v = sb("v", [P, T, 6, W1], F16)
        vf = sb("vf", [P, 2, QT, W1], F32)
        h = sb("h", [P, 2, T, D + 3], F32)
        xs = sb("xs2", [P, NQ, QT, 2, D], F16)
        xt = sb("xt2", [P, 2, QT * P], F16)
        qsum = sb("qsum", [P, 2, NQ], F32)
        wide = sb("wide", [P, P], F32)
        mean = sb("mean", [P, 2, D], F32)
        args = sb("args", [P, 4, T], F32)
        ex = sb("ex", [P, 2, 4, T], F32)
        bias = sb("bias", [P, 2, T], F32)
        tops = sb("tops", [P, 4], F32)
        tt = sb("tt", [P, T], F32)
        uv = sb("uv", [P, T, 2, W1], F32)
        n2 = sb("n2", [P, T, W1], F32)
        o = sb("o2", [P, T, W1], F32)
        y = sb("y2", [P, T, D], F32)
        yc = sb("yc2", [P, T, D], F32)
        st = sb("st2", [P, 8, T], F32)
        none = sb("none2", [P, T], F32)
        fill = sb("fill2", [P, T, D], F32)
        big = sb("big", [P, T], F32)
        ps_x = psum[:, 3072:3328].bitcast(F16)
        ps_h = psum[:, 3584:3584 + QT * (D + 2)].rearrange("p (t d) -> p t d", t=QT)
        ps_mean = psum[:, 3584 + QT * (D + 2):3584 + QT * (D + 2) + D]

        def tile_sum(it):
            c = 512 * (it // 3) + 2 * W1 * (it % 3)
            return psum[:, c:c + 2 * W1]

        block = ctx.enter_context(nc.Block())

        def drive(eng, body, pair=None):
            for lay in (0, 1):
                body(lay, 0, 0, (lay, 2))
                body(lay, 1, 1, (lay, 3))
                with eng.Fori(1, B // 2 - 1) as bp:
                    if pair is not None:
                        pair[0] = bp
                    for par in (0, 1):
                        body(lay, 2 * bp + par, par, (lay, 2 * bp + par + 2))
                for par in (0, 1):
                    body(lay, B - 2 + par, par, (1, par) if lay == 0 else None)

        def is0(g):
            return isinstance(g, int) and g == 0

        def last_of_all(lay, b):
            return lay == 1 and isinstance(b, int) and b == B - 1

        @block.sync
        def _(sp):
            def load_si(g, par):
                sp.wait_ge(h_kept, NQ * g + NQ)
                sp.dma_start(scratch[par:par + 1, :].rearrange("o (t p) -> p (o t)", p=P), h[:, par, :, D + 1],
                             allow_slow_non_contiguous=True).then_inc(s_out, 16)
                if g >= 2:
                    sp.wait_ge(relu_done, T * g - T)
                sp.wait_ge(s_out, 16 * g + 16)
                sp.dma_start(si[:, par, :], scratch[par:par + 1, :].to_broadcast([P, N])).then_inc(r_in[par], 16)

            def store(b, g):
                sp.wait_ge(x_done, g + 1)
                sp.dma_start(rows(out[b]), x[:, b, :, :]).then_inc(out_done, 16)

            load_si(0, 0)
            for g in range(G):
                if g + 1 < G:
                    load_si(g + 1, (g + 1) % 2)
                if g >= B + 1:
                    store(g - B - 1, g - 1)
            store(B - 1, G - 1)
            sp.wait_ge(out_done, 16 * B)

        @block.gpsimd
        def _(pool):
            nc.gpsimd.memset(big[:, :], BIG).then_inc(ones_set, 1)
            nc.gpsimd.memset(h[:, :, :, 0:1], 1.0).then_inc(ones_set, 1)
            pool.wait_ge(ones_set, 2)

            def top_of(g, par):
                pool.wait_ge(top_part, g + 1)
                nc.gpsimd.tensor_tensor(bias[:, par, :], h[:, par, :, D + 2], big[:, :], ALU.mult).then_inc(bias_ready, 1)
                nc.gpsimd.partition_all_reduce(tops[:, 2:3], tops[:, 0:1], P, bass.bass_isa.ReduceOp.max
                                               ).then_inc(top_all, 1)

            def fill_of(lay, g, b, par):
                pool.wait_ge(mean_kept, g + 1)
                pool.wait_ge(post_order, POST * g + 3)
                if lay == 1:
                    nc.gpsimd.tensor_tensor(fill[:, :, :], over(none[:, :], [P, T, D], 2),
                                            over(mean[:, par, :], [P, T, D], 1), ALU.mult).then_inc(filled, 1)
                    return
                nc.gpsimd.tensor_tensor(fill[:, :, :], over(none[:, :], [P, T, D], 2),
                                        over(mean[:, par, :], [P, T, D], 1), ALU.mult).then_inc(mean_spread, 1)
                pool.wait_ge(mean_spread, g + 1)
                nc.gpsimd.tensor_tensor(fill[:, :, :], fill[:, :, :], x[:, b, :, :], ALU.add).then_inc(filled, 1)

            def rstd(g):
                pool.wait_ge(var_ready, g + 1)
                nc.gpsimd.tensor_tensor(st[:, 5, :], st[:, 4, :], kept.neg_half[:, :], ALU.pow).then_inc(rstd_ready, 1)

            def body(lay, b, par, ahead):
                g = B * lay + b
                if not last_of_all(lay, b):
                    top_of(g + 1, 1 - par)
                if not is0(g):
                    if isinstance(b, int) and b == 0:
                        fill_of(lay - 1, g - 1, B - 1, 1 - par)
                    else:
                        fill_of(lay, g - 1, b - 1, 1 - par)
                    rstd(g - 1)

            top_of(0, 0)
            drive(pool, body)
            fill_of(1, G - 1, B - 1, 1)
            rstd(G - 1)

        @block.tensor
        def _(pe):
            def turn(q, Q):
                pe.wait_ge(hi_done, Q + 1)
                pe.wait_ge(lo_done, Q + 1)
                if not is0(Q):
                    pe.wait_ge(xt_ready, Q)
                for k in range(QT):
                    tr = nc.tensor.transpose(ps_x[:, P * k:P * k + P], xs[:, q, k, :, :].rearrange("p u d -> p (u d)"),
                                             kept.id16[:, :])
                tr.then_inc(turned, 1)

            def times_w(lay, q, Q, g=None):
                pe.wait_ge(xt_ready, Q + 1)
                if not is0(Q):
                    pe.wait_ge(h_kept, Q)
                if q == 0 and g is not None:
                    pe.wait_ge(mean_kept, g + 1)
                for k in range(QT):
                    for w in (kept.w_hi, kept.w_lo):
                        mm = nc.tensor.matmul(ps_h[:, k, :], xt[:, q % 2, P * k:P * k + P], w[:, 1 + lay, :],
                                              start=(w is kept.w_hi), stop=(w is kept.w_lo))
                mm.then_inc(h_ps, 1)

            def mean_of(lay, g, kept_quarters):
                pe.wait_ge(sum_wide, g + 1)
                pe.wait_ge(h_kept, kept_quarters)
                nc.tensor.matmul(ps_mean, wide[:, :], kept.w_raw[:, 1 + lay, 0:D], start=True, stop=True
                                 ).then_inc(mean_ps, 1)

            def step(g, jt):
                s = T * g + jt
                apart = jt % 4 == 0
                pe.wait_ge(mp_done, s + 1)
                if jt % QT == 0:
                    pe.wait_ge(v_ready, NQ * g + jt // QT + 1)
                w = v[:, jt, :, :]
                for it in range(T):
                    if jt == 0 and it % 3 == 0 and not is0(g):
                        pe.wait_ge(evac, 6 * g - 6 + it // 3 + 1)
                    a = mp[:, jt % LEAD, P * it:P * it + P]
                    m = mn[:, jt // 4 % 2, P * it:P * it + P] if apart else maskT[:, jt, P * it:P * it + P]
                    acc = tile_sum(it)
                    for half in (0, 1):
                        lead = w[:, 2 * half:2 * half + (1 if apart else 2), :].rearrange("p u d -> p (u d)")
                        nc.tensor.matmul(acc[:, 0:lead.shape[1]], a, lead,
                                         start=(jt == 0 and half == 0 and it % 3 == 0), stop=False,
                                         skip_group_check=True)
                    for half in (0, 1):
                        mm = nc.tensor.matmul(acc[:, W1:2 * W1], m, w[:, 4 + half, :], start=False,
                                              stop=(jt == T - 1 and half == 1 and (it % 3 == 2 or it == T - 1)),
                                              skip_group_check=True)
                mm.then_inc(av_done, 1)

            def body(lay, b, par, ahead):
                g = B * lay + b
                for jt in range(T):
                    step(g, jt)
                    if ahead:
                        Q = NQ * (g + 2)
                        if jt % 2 == 0 and jt < 8:
                            turn(jt // 2, Q + jt // 2)
                        if jt % 2 == 1 and 3 <= jt < 11:
                            times_w(ahead[0], (jt - 3) // 2, Q + (jt - 3) // 2, g)
                    if jt == 11 and not last_of_all(lay, b):
                        mean_of(1 if lay == 0 and isinstance(b, int) and b == B - 1 else lay, g + 1,
                                NQ * (g + 3) if ahead else NQ * G)

            for Q in range(2 * NQ):
                turn(Q % NQ, Q)
                times_w(0, Q % NQ, Q)
            mean_of(0, 0, 2 * NQ)
            drive(pe, body)

        @block.scalar
        def _(act):
            def split_hi(b, q, Q):
                if not (isinstance(Q, int) and Q < NQ):
                    act.wait_ge(turned, Q - NQ + 1)
                nc.scalar.activation(xs[:, q, :, 0, :], x[:, b, QT * q:QT * q + QT, :], ACT.Copy, scale=SX
                                     ).then_inc(hi_done, 1)

            def keep_x(par, q, Q):
                act.wait_ge(turned, Q + 1)
                if not (isinstance(Q, int) and Q < 2):
                    act.wait_ge(h_ps, Q - 1)
                nc.scalar.activation(xt[:, q % 2, :], ps_x, ACT.Copy, accum_out=qsum[:, par, q:q + 1]
                                     ).then_inc(xt_ready, 1)

            def exps(g, par):
                act.wait_ge(args_ready, g + 1)
                if not (isinstance(g, int) and g < 2):
                    act.wait_ge(uv_used, g - 1)
                nc.scalar.activation(ex[:, par, :, :], args[:, :, :], ACT.Exp).then_inc(ex_ready, 1)

            def values_hi(q, Q):
                act.wait_ge(v_done, Q + 1)
                nc.scalar.copy(v[:, QT * q:QT * q + QT, 0:5:4, :].rearrange("p t u d -> p u t d"), vf[:, :, :, :]
                               ).then_inc(v_hi, 1)

            def values_minus(q, Q):
                act.wait_ge(v_lo, Q + 1)
                nc.scalar.activation(v[:, QT * q:QT * q + QT, 1:4:2, :], v[:, QT * q:QT * q + QT, 4:6, :], ACT.Copy,
                                     scale=-1.0).then_inc(v_ready, 1)

            def copy_sums(g):
                act.wait_ge(av_done, T * g + T)
                if not is0(g):
                    act.wait_ge(uv_used, g)
                for k in range(6):
                    n = 3 if k < 5 else 1
                    nc.scalar.copy(uv[:, 3 * k:3 * k + n, :, :].rearrange("p t u d -> p (t u d)"),
                                   psum[:, 512 * k:512 * k + 2 * W1 * n]).then_inc(evac, 1)

            def square(g):
                act.wait_ge(yc_ready, g + 1)
                nc.scalar.activation(y[:, :, :], yc[:, :, :], ACT.Square).then_inc(sq_done, 1)

            def elu_exp(b1):
                act.wait_ge(elu_in, b1)
                nc.scalar.activation(y[:, :, :], o[:, :, 1:W1], ACT.Exp).then_inc(elu_out, 1)

            def body(lay, b, par, ahead):
                g = B * lay + b
                last = last_of_all(lay, b)
                for jt in range(T):
                    s = T * g + jt
                    if jt == 0:
                        act.wait_ge(r_in[par], 16 * count_pairs(lay, b, par))
                        act.wait_ge(bias_ready, g + 1)
                    if not (is0(g) and jt < 2):
                        act.wait_ge(mp_done, s - 1)
                    nc.scalar.activation(z[:, jt % 2, :], si[:, par, :], ACT.Relu, scale=BIG,
                                         bias=bias[:, par, jt:jt + 1]).then_inc(relu_done, 1)
                    if jt == 4 and not is0(g):
                        copy_sums(g - 1)
                    if ahead and jt % 2 == 0 and jt < 8:
                        q = jt // 2
                        if lay == 0 and ahead[0] == 1 and q == 0:
                            act.wait_ge(x_done, ahead[1] + 1)
                        split_hi(ahead[1], q, NQ * (g + 2) + q)
                    if ahead and jt % 2 == 1 and 5 <= jt < 13:
                        q = (jt - 5) // 2
                        keep_x(par, q, NQ * (g + 2) + q)
                    if jt == 7 and not last:
                        exps(g + 1, 1 - par)
                    Q = NQ * g + jt // QT + 2
                    if not (last and jt >= 8):
                        if jt % QT == 2:
                            values_hi((jt // QT + 2) % NQ, Q)
                        if jt % QT == 3:
                            values_minus((jt // QT + 2) % NQ, Q)
                    if not is0(g):
                        if jt == 9 and elu_here(lay, b):
                            elu_exp(g - B)
                        if jt == 13:
                            square(g - 1)

            def count_pairs(lay, b, par):
                if isinstance(b, int):
                    return (B * lay + b) // 2 + 1
                return B // 2 * lay + pair[0] + 1

            def elu_here(lay, b):
                return lay == 1 and not is0(b)

            pair = [None]

            for Q in range(2 * NQ):
                split_hi(Q // NQ, Q % NQ, Q)
                keep_x(Q // NQ, Q % NQ, Q)
            exps(0, 0)
            for q in (0, 1):
                values_hi(q, q)
                values_minus(q, q)
            drive(act, body, pair)
            copy_sums(G - 1)
            elu_exp(B)
            square(G - 1)

        @block.vector
        def _(dve):
            def split_lo(b, q, Q):
                dve.wait_ge(hi_done, Q + 1)
                nc.vector.scalar_tensor_tensor(out=xs[:, q, :, 1, :], in0=x[:, b, QT * q:QT * q + QT, :], scalar=SX,
                                               in1=xs[:, q, :, 0, :], op0=ALU.mult, op1=ALU.subtract).then_inc(lo_done, 1)

            def keep_h(par, q, Q, stored=None):
                dve.wait_ge(h_ps, Q + 1)
                if stored is not None:
                    dve.wait_ge(s_out, 16 * stored)
                nc.vector.tensor_scalar(h[:, par, QT * q:QT * q + QT, 1:D + 3], ps_h, 1.0 / SX / SX, None, ALU.mult
                                        ).then_inc(h_kept, 1)

            def sc(g, k, ins):
                ins.then_inc(sc_order, 1)
                dve.wait_ge(sc_order, SC * g + k)

            def tops_of(g, par):
                dve.wait_ge(h_kept, NQ * g + NQ)
                nc.vector.tensor_reduce(tops[:, 0:1], h[:, par, :, D + 2], X, ALU.max).then_inc(top_part, 1)
                dve.wait_ge(xt_ready, NQ * g + NQ)
                sc(g, 1, nc.vector.tensor_reduce(tops[:, 1:2], qsum[:, par, :], X, ALU.add))
                nc.vector.tensor_scalar(wide[:, :], tops[:, 1:2].to_broadcast([P, P]), 1.0 / SX / N, None, ALU.mult
                                        ).then_inc(sum_wide, 1)

            def args_of(g, par):
                dve.wait_ge(top_all, g + 1)
                top, s_j = tops[:, 2:3], h[:, par, :, D + 2]
                if not is0(g):
                    dve.wait_ge(ex_ready, g)
                sc(g, 2, nc.vector.tensor_scalar(tt[:, :], h[:, par, :, D + 1], top, 0.8, ALU.add, ALU.mult))
                nc.vector.tensor_scalar(args[:, 0, :], tt[:, :], 0.0, None, ALU.min)
                nc.vector.tensor_scalar(args[:, 1, :], tt[:, :], -1.0, 0.0, ALU.mult, ALU.min)
                nc.vector.tensor_scalar(args[:, 2, :], s_j, top, None, ALU.subtract)
                nc.vector.tensor_scalar(args[:, 3, :], s_j, top, 0.2, ALU.subtract, ALU.mult).then_inc(args_ready, 1)

            def keep_mean(g, par):
                dve.wait_ge(mean_ps, g + 1)
                nc.vector.tensor_copy(mean[:, par, :], ps_mean).then_inc(mean_kept, 1)

            def values(q, Q, g, par):
                dve.wait_ge(ex_ready, g + 1)
                if not is0(Q):
                    dve.wait_ge(v_lo, Q)
                hq = h[:, par, QT * q:QT * q + QT, 0:W1]
                for u in (0, 1):
                    ins = nc.vector.scalar_tensor_tensor(out=vf[:, u, :, :], in0=hq, scalar=SV,
                                                         in1=over(ex[:, par, 2 + u, QT * q:QT * q + QT], [P, QT, W1], 2),
                                                         op0=ALU.mult, op1=ALU.mult)
                ins.then_inc(v_done, 1)

            def values_lo(q, Q):
                dve.wait_ge(v_hi, Q + 1)
                for u in (0, 1):
                    ins = nc.vector.tensor_tensor(v[:, QT * q:QT * q + QT, 2 + 3 * u, :], vf[:, u, :, :],
                                                  v[:, QT * q:QT * q + QT, 4 * u, :], ALU.subtract)
                ins.then_inc(v_lo, 1)

            def post(g, b, lay, par, part):
                def lk(k, ins):
                    ins.then_inc(post_order, 1)
                    dve.wait_ge(post_order, POST * g + k)

                xg = x[:, b, :, :]
                if part == 4:
                    dve.wait_ge(evac, 6 * g + 6)
                    lk(1, nc.vector.tensor_tensor(n2[:, :, :], uv[:, :, 1, :], over(ex[:, par, 1, :], [P, T, W1], 2), ALU.mult))
                    nc.vector.tensor_tensor(o[:, :, :], uv[:, :, 0, :], over(ex[:, par, 0, :], [P, T, W1], 2), ALU.mult
                                            ).then_inc(uv_used, 1)
                if part == 5:
                    dve.wait_ge(uv_used, g + 1)
                    lk(2, nc.vector.tensor_tensor(o[:, :, :], o[:, :, :], n2[:, :, :], ALU.add))
                    if not is0(g):
                        dve.wait_ge(filled, g)
                    lk(3, nc.vector.tensor_scalar(none[:, :], o[:, :, 0], 0.0, None, ALU.is_equal))
                    lk(4, nc.vector.tensor_tensor(st[:, 0, :], o[:, :, 0], none[:, :], ALU.add))
                    lk(5, nc.vector.reciprocal(st[:, 1, :], st[:, 0, :]))
                if part == 6:
                    lk(6, nc.vector.tensor_tensor(o[:, :, 1:W1], o[:, :, 1:W1], over(st[:, 1, :], [P, T, D], 2), ALU.mult))
                if part == 7:
                    dve.wait_ge(filled, g + 1)
                    if lay == 0:
                        nc.vector.tensor_tensor(y[:, :, :], o[:, :, 1:W1], fill[:, :, :], ALU.add
                                                ).then_inc(post_order, 2)
                        dve.wait_ge(post_order, POST * g + 8)
                    else:
                        nc.vector.tensor_tensor(o[:, :, 1:W1], o[:, :, 1:W1], fill[:, :, :], ALU.add).then_inc(elu_in, 1)
                if part == 9 and lay == 1:
                    dve.wait_ge(elu_out, b + 1)
                    lk(7, nc.vector.tensor_scalar(n2[:, :, 0:D], y[:, :, :], 1.0, -1.0, ALU.min, ALU.add))
                    nc.vector.scalar_tensor_tensor(out=o[:, :, 1:W1], in0=o[:, :, 1:W1], scalar=0.0,
                                                   in1=n2[:, :, 0:D], op0=ALU.max, op1=ALU.add).then_inc(elu_sum, 1)
                    dve.wait_ge(elu_sum, b + 1)
                    lk(8, nc.vector.tensor_tensor(y[:, :, :], o[:, :, 1:W1], xg, ALU.add))
                if part == 10:
                    lk(9, nc.vector.tensor_reduce(st[:, 2, :], y[:, :, :], X, ALU.add))
                if part == 11:
                    nc.vector.scalar_tensor_tensor(out=yc[:, :, :], in0=over(st[:, 2, :], [P, T, D], 2), scalar=-1.0 / D,
                                                   in1=y[:, :, :], op0=ALU.mult, op1=ALU.add).then_inc(yc_ready, 1)
                if part == 13:
                    dve.wait_ge(sq_done, g + 1)
                    nc.vector.tensor_reduce(st[:, 3, :], y[:, :, :], X, ALU.add).then_inc(var_sum, 1)
                    dve.wait_ge(var_sum, g + 1)
                    nc.vector.tensor_scalar(st[:, 4, :], st[:, 3, :], 1.0 / D, EPS, ALU.mult, ALU.add
                                            ).then_inc(var_ready, 1)
                if part == 15:
                    dve.wait_ge(rstd_ready, g + 1)
                    nc.vector.tensor_tensor(xg, yc[:, :, :], over(st[:, 5, :], [P, T, D], 2), ALU.mult).then_inc(x_done, 1)

            elu_sum, var_sum = sems("elu_sum"), sems("var_sum")

            def body(lay, b, par, ahead):
                g = B * lay + b
                last = last_of_all(lay, b)
                if isinstance(b, int) and b == 0:
                    lay1, b1 = lay - 1, B - 1
                else:
                    lay1, b1 = lay, b - 1
                for jt in range(T):
                    s = T * g + jt
                    dve.wait_ge(relu_done, s + 1)
                    if not (is0(g) and jt < LEAD):
                        dve.wait_ge(av_done, s - LEAD + 1)
                    nc.vector.tensor_tensor(mp[:, jt % LEAD, :], z[:, jt % 2, :], maskT[:, jt, :], ALU.min
                                            ).then_inc(mp_parts if jt % 4 == 0 else mp_done, 1)
                    if jt % 4 == 0:
                        dve.wait_ge(mp_parts, NQ * g + jt // 4 + 1)
                        nc.vector.tensor_tensor(mn[:, jt // 4 % 2, :], maskT[:, jt, :], mp[:, jt % LEAD, :], ALU.subtract
                                                ).then_inc(mp_done, 1)
                    Q = NQ * g + jt // QT + 2
                    if jt % QT == 0 and not (last and jt >= 8):
                        if jt < 8:
                            values(jt // QT + 2, Q, g, par)
                        else:
                            values(jt // QT - 2, Q, g + 1, 1 - par)
                    if jt % QT == 2 and not (last and jt >= 8):
                        values_lo((jt // QT + 2) % NQ, Q)
                    if not is0(g):
                        post(g - 1, b1, lay1, 1 - par, jt)
                    if ahead and jt % 2 == 0 and jt < 8:
                        split_lo(ahead[1], jt // 2, NQ * (g + 2) + jt // 2)
                    if ahead and jt % 2 == 1 and jt >= 7 and jt < 15:
                        keep_h(par, (jt - 7) // 2, NQ * (g + 2) + (jt - 7) // 2, g + 1)
                    if not last:
                        if jt == 4:
                            tops_of(g + 1, 1 - par)
                        if jt == 5:
                            args_of(g + 1, 1 - par)
                        if jt == T - 1:
                            keep_mean(g + 1, 1 - par)

            mp_parts = sems("mp_parts")
            dve.wait_ge(ones_set, 2)
            for Q in range(2 * NQ):
                split_lo(Q // NQ, Q % NQ, Q)
                keep_h(Q // NQ, Q % NQ, Q)
            tops_of(0, 0)
            args_of(0, 0)
            keep_mean(0, 0)
            for q in (0, 1):
                values(q, q, 0, 0)
                values_lo(q, q)
            drive(dve, body)
            for part in (4, 5, 6, 7, 9, 10, 11, 13, 15):
                post(G - 1, B - 1, 1, 1, part)


class Layer0:

    def __init__(self, nc, ctx):
        def sb(name, shape, dt):
            return ctx.enter_context(nc.sbuf_tensor(name, shape, dt))

        self.a12 = sb("a12", [P, T, P], F32)
        self.h_hi = sb("h_hi", [P, T, B, D], F16)
        self.h_lo = sb("h_lo", [P, T, B, D], F16)
        self.sc1 = sb("sc1", [P, B, T], F32)
        self.c6 = sb("c6", [P, T], F32)
        self.not_last = sb("not_last", [P, 1], F32)
        self.ones = sb("ones16", [P, 2, P], F16)
        self.hsum = sb("hsum", [P, B, D], F32)
        self.stage = sb("stage", [P, NQ, QT, 512], I32)
        self.row0 = sb("row0", [P, T], I32)


def build(nc, A, out, stop_after=99):
    with ExitStack() as ctx:
        psum = ctx.enter_context(nc.psum_tensor("banks", [P, 4096], F32))
        names = {}

        def sems(name):
            assert name not in names
            names[name] = ctx.enter_context(nc.semaphore(name))
            return names[name]

        kept = Kept(nc, ctx)
        with ExitStack() as first:
            l0 = Layer0(nc, first)
            prepare(nc, kept, l0, sems, A, psum)
            layer_0(nc, kept, l0, sems, A, psum)
        if stop_after >= 1:
            layer_1(nc, kept, sems, psum)
        if stop_after >= 2:
            scratch = nc.dram_tensor("s_i_rows", (2, N), F32, kind="Internal").ap()
            layers_2_3(nc, kept, sems, psum, scratch, out)
            return
        if stop_after <= 1:
            out_done = sems("out_done")
            with nc.Block() as block:
                @block.sync
                def _(sp):
                    for b in range(B):
                        sp.dma_start(rows(out[b]), kept.x[:, b, :, :]).then_inc(out_done, 16)
                    sp.wait_ge(out_done, 16 * B)
            return


_INS = {"x": "x", "adj": "adj", "L0_gnn_W": "w0", "L0_gnn_a": "a0", "L2_gnn_W": "w2", "L2_gnn_a": "a2",
        "L3_gnn_W": "w3", "L3_gnn_a": "a3"}


def kernel(**inputs):
    import numpy as np
    import concourse.bacc as bacc
    from concourse.bass_utils import run_bass_kernel_spmd

    nc = bacc.Bacc("TRN2", target_bir_lowering=False, num_devices=1)
    arrays, A = {}, {}
    for name, short in _INS.items():
        a = np.ascontiguousarray(inputs[name])
        arrays[f"in_{short}"] = a
        A[short] = nc.dram_tensor(f"in_{short}", a.shape, mybir.dt.from_np(a.dtype), kind="ExternalInput").ap()
    out = nc.dram_tensor("out_x", (B, N, D), F32, kind="ExternalOutput").ap()
    build(nc, A, out)
    r = run_bass_kernel_spmd(nc, [arrays], core_ids=[0])
    return r.results[0]["out_x"]
```

```python
from contextlib import ExitStack

import concourse.bass as bass
from concourse import mybir

F32 = mybir.dt.float32
F16 = mybir.dt.float16
BF16 = mybir.dt.bfloat16
I32 = mybir.dt.int32
ALU = mybir.AluOpType
ACT = mybir.ActivationFunctionType
X = mybir.AxisListType.X

P = 128
B, N, D = 8, 2048, 64
T = N // P
QT = 4
NQ = T // QT
EPS = 1e-5
SX = 256.0
SH = 64.0
SM = 256.0
LO = 32


class Count:

    def __init__(self, sem):
        self.sem, self.n = sem, 0

    def inc(self, ins):
        ins.then_inc(self.sem, 1)
        self.n += 1
        return ins

    def now(self):
        return self.n


def over(ap, shape, axis):
    return ap.unsqueeze(axis).to_broadcast(shape)


def rows(ap):
    return ap.rearrange("(t p) c -> p t c", p=P)


class Kept:

    def __init__(self, nc, ctx):
        def sb(name, shape, dt):
            return ctx.enter_context(nc.sbuf_tensor(name, shape, dt))

        self.x = sb("x_rows", [P, B, T, D], F32)
        self.maskT = sb("mask_t", [P, T, N], BF16)
        self.w_raw = sb("w_raw", [P, 3, D + 2], F32)
        self.w_hi = sb("w_hi", [P, 3, D + 2], F16)
        self.w_lo = sb("w_lo", [P, 3, D + 2], F16)
        self.id16 = sb("id16", [P, P], F16)
        self.idb = sb("idb", [P, P], BF16)
        self.id32 = sb("id32", [P, P], F32)
        self.eye2 = sb("eye2", [P, D], F32)
        self.neg_half = sb("neg_half", [P, T], F32)
        self.none = sb("none", [P, N], F16)


def prepare(nc, kept, l0, sems, A, psum):
    x, id16, id32, idb = kept.x, kept.id16, kept.id32, kept.idb
    x_in, w_in, av_in, a0_in = [sems("x_in0"), sems("x_in1")], sems("w_in"), sems("av_in"), sems("a0_in")
    pool_order, vec_order = Count(sems("prep_pool")), Count(sems("prep_vec"))
    ident_ready, w_ready, a0T, a0_kept = sems("ident_ready"), sems("w_ready"), sems("a0T"), sems("a0_kept")
    x_hi, x_lo, x_t, x_tk = sems("p_x_hi"), sems("p_x_lo"), sems("p_x_t"), sems("p_x_tk")
    h_done, h_hi, h_used = sems("p_h_done"), sems("p_h_hi"), sems("p_h_used")
    stage_clear, ones_set = sems("stage_clear"), sems("ones16_set")
    adj_in = [sems(f"adj_in{r}") for r in range(NQ)]
    row0_in = sems("row0_in")
    l0.adj_in, l0.row0_in = adj_in, row0_in

    with ExitStack() as ctx:
        def sb(name, shape, dt):
            return ctx.enter_context(nc.sbuf_tensor(name, shape, dt))

        a0 = sb("a0", [P, N], F32)
        av = sb("av", [P, 2, 2, D], F32)
        wa = sb("wa", [P, 2, 2, D], F32)
        w256 = sb("w256", [P, 3, D + 2], F32)
        w_mean = sb("w_mean", [P, 1], F32)
        xs = sb("xs", [P, 2, QT, P], F16)
        xt = sb("xt", [P, 2, QT, P], F16)
        prod = sb("prod", [P, 2, QT, D], F32)
        ps_t = [psum[:, 512 * r:512 * r + 256].bitcast(F16).rearrange("p (t n) -> p t n", t=QT) for r in (0, 1)]
        ps_h = [psum[:, 512 * r:512 * r + QT * D].rearrange("p (t d) -> p t d", t=QT) for r in (2, 3)]
        ps_s = psum[:, 512 * 4:512 * 5]
        block = ctx.enter_context(nc.Block())
        sc_done, pr_done, hs_done = sems("p_sc_done"), sems("p_pr_done"), sems("p_hs_done")

        def stages(step, eng):
            def pair(bp):
                for par in (0, 1):
                    for q in range(NQ):
                        step(bp, par, q)

            pair(0)
            with eng.Fori(1, B // 2 - 1) as bp:
                pair(bp)
            pair(B // 2 - 1)

        def after(bp, par, q, n):
            k = NQ * par + q + n
            if k >= 2 * NQ and isinstance(bp, int) and bp == B // 2 - 1:
                return None
            return (bp + 1, 0, k - 2 * NQ) if k >= 2 * NQ else (bp, k // NQ, k % NQ)

        def number(bp, par, q):
            return 2 * NQ * bp + NQ * par + q

        def before(Q, n):
            return isinstance(Q, int) and Q < n

        @block.sync
        def _(sp):
            for b in range(B):
                if b >= 2:
                    sp.wait_ge(x_in[b % 2], 16 * (b // 2))
                sp.dma_start(x[:, b, :, :], rows(A["x"][b])).then_inc(x_in[b % 2], 16)
            sp.wait_ge(stage_clear, 1)
            for r in range(NQ):
                load_adj(sp, A["adj"], l0.stage, r, 0, adj_in[r])
            sp.dma_start(l0.row0[:, :], A["adj"][0:1, :].rearrange("o (t p) -> p (o t)", p=P),
                         allow_slow_non_contiguous=True).then_inc(row0_in, 16)

        @block.gpsimd
        def _(pool):
            pool_order.inc(nc.gpsimd.memset(id32[:, :], 0.0))
            pool_order.inc(nc.gpsimd.memset(kept.eye2[:, :], 0.0))
            pool_order.inc(nc.gpsimd.memset(kept.neg_half[:, :], -0.5))
            nc.gpsimd.memset(l0.stage[:, NQ - 1, QT - 1, :], 0).then_inc(stage_clear, 1)
            pool.wait_ge(pool_order.sem, pool_order.now())
            pool_order.inc(nc.gpsimd.affine_select(out=id32[:, :], in_=id32[:, :], compare_op=ALU.not_equal, fill=1.0,
                                                   base=0, pattern=[[-1, P]], channel_multiplier=1))
            pool_order.inc(nc.gpsimd.affine_select(out=kept.eye2[:, :], in_=kept.eye2[:, :], compare_op=ALU.not_equal,
                                                   fill=1.0, base=0, pattern=[[-1, D]], channel_multiplier=1))
            pool.wait_ge(pool_order.sem, pool_order.now())
            pool_order.inc(nc.gpsimd.affine_select(out=kept.eye2[:, :], in_=kept.eye2[:, :], compare_op=ALU.not_equal,
                                                   fill=1.0, base=-D, pattern=[[-1, D]], channel_multiplier=1))
            nc.gpsimd.tensor_copy(id16[:, :], id32[:, :]).then_inc(ident_ready, 1)
            nc.gpsimd.tensor_copy(idb[:, :], id32[:, :]).then_inc(ident_ready, 1)

        @block.scalar
        def _(act):
            act.dma_start(a0[:, :], A["a0"]).then_inc(a0_in, 16)
            for l, w in enumerate(("w0", "w2", "w3")):
                for half in (0, D):
                    act.dma_start(kept.w_raw[half:half + D, l, 0:D], A[w]).then_inc(w_in, 16)
            act.dma_start(av[:, 0, :, :].rearrange("p i d -> p (i d)"), A["a2"].unsqueeze(0).to_broadcast([P, 2 * D])
                          ).then_inc(av_in, 16)
            act.dma_start(av[:, 1, :, :].rearrange("p i d -> p (i d)"), A["a3"].rearrange("d o -> o d").to_broadcast([P, 2 * D])
                          ).then_inc(av_in, 16)
            def split_hi(bp, par, q):
                b, Q = 2 * bp + par, number(bp, par, q)
                if q == 0:
                    act.wait_ge(x_in[par], 16 * bp + 16)
                if not before(Q, 2):
                    act.wait_ge(x_t, Q - 1)
                nc.scalar.activation(xs[:, q % 2, :, 0:D], x[:, b, QT * q:QT * q + QT, :], ACT.Copy, scale=SX
                                     ).then_inc(x_hi, 1)

            def keep_x(q, Q):
                act.wait_ge(x_t, Q + 1)
                if not before(Q, 2):
                    act.wait_ge(h_done, Q - 1)
                nc.scalar.copy(xt[:, q % 2, :, :], ps_t[q % 2]).then_inc(x_tk, 1)

            def step(bp, par, q):
                b, Q = 2 * bp + par, number(bp, par, q)
                if after(bp, par, q, 2):
                    split_hi(*after(bp, par, q, 2))
                if after(bp, par, q, 1):
                    keep_x(after(bp, par, q, 1)[2], Q + 1)
                act.wait_ge(h_done, Q + 1)
                nc.scalar.activation(l0.h_hi[:, QT * q:QT * q + QT, b, :], ps_h[q % 2], ACT.Copy, scale=SH / SX / SX
                                     ).then_inc(h_hi, 1)

            split_hi(0, 0, 0)
            split_hi(0, 0, 1)
            keep_x(0, 0)
            for r in range(NQ):
                act.wait_ge(a0T, r + 1)
                nc.scalar.copy(l0.a12[:, QT * r:QT * r + QT, :],
                               psum[:, 2048 + 512 * r:2560 + 512 * r].rearrange("p (t d) -> p t d", t=QT)
                               ).then_inc(a0_kept, 1)
            stages(step, act)

        @block.vector
        def _(dve):
            def link(ins):
                vec_order.inc(ins)
                dve.wait_ge(vec_order.sem, vec_order.now())

            def split_lo(bp, par, q):
                b, Q = 2 * bp + par, number(bp, par, q)
                if q == 0:
                    dve.wait_ge(x_in[par], 16 * bp + 16)
                dve.wait_ge(x_hi, Q + 1)
                nc.vector.scalar_tensor_tensor(out=xs[:, q % 2, :, D:P], in0=x[:, b, QT * q:QT * q + QT, :], scalar=SX,
                                               in1=xs[:, q % 2, :, 0:D], op0=ALU.mult, op1=ALU.subtract
                                               ).then_inc(x_lo, 1)

            def step(bp, par, q):
                b, Q = 2 * bp + par, number(bp, par, q)
                if after(bp, par, q, 2):
                    split_lo(*after(bp, par, q, 2))
                dve.wait_ge(h_hi, Q + 1)
                if not before(Q, 2):
                    dve.wait_ge(sc_done, Q - 1)
                nc.vector.tensor_tensor(prod[:, q % 2, :, :], ps_h[q % 2], l0.a12[:, QT * q:QT * q + QT, 0:D], ALU.mult
                                        ).then_inc(pr_done, 1)
                nc.vector.scalar_tensor_tensor(out=l0.h_lo[:, QT * q:QT * q + QT, b, :], in0=ps_h[q % 2],
                                               scalar=SH / SX / SX, in1=l0.h_hi[:, QT * q:QT * q + QT, b, :],
                                               op0=ALU.mult, op1=ALU.subtract).then_inc(h_used, 1)
                dve.wait_ge(pr_done, Q + 1)
                nc.vector.tensor_reduce(l0.sc1[:, b, QT * q:QT * q + QT], prod[:, q % 2, :, :], X, ALU.add
                                        ).then_inc(sc_done, 1)

            split_lo(0, 0, 0)
            split_lo(0, 0, 1)
            link(nc.vector.memset(l0.ones[:, :, :], 1.0))
            nc.vector.memset(l0.ones[0:1, 0, :], 0.0).then_inc(ones_set, 1)
            link(nc.vector.memset(kept.w_raw[:, 0, D:D + 2], 0.0))
            dve.wait_ge(w_in, 96)
            dve.wait_ge(av_in, 32)
            for i in (0, 1):
                link(nc.vector.tensor_tensor(wa[:, :, i, :], kept.w_raw[:, 1:3, 0:D], av[:, :, i, :], ALU.mult))
            for l in (0, 1):
                link(nc.vector.tensor_reduce(kept.w_raw[:, 1 + l, D:D + 2], wa[:, l, :, :], X, ALU.add))
            link(nc.vector.tensor_reduce(w_mean[:, :], kept.w_raw[:, 1, 0:D], X, ALU.add))
            link(nc.vector.scalar_tensor_tensor(out=kept.w_raw[:, 1, 0:D], in0=w_mean[:, :].to_broadcast([P, D]),
                                                scalar=-1.0 / D, in1=kept.w_raw[:, 1, 0:D], op0=ALU.mult, op1=ALU.add))
            link(nc.vector.tensor_scalar(w256[:, :, :], kept.w_raw[:, :, :], SX, None, ALU.mult))
            link(nc.vector.tensor_copy(kept.w_hi[:, :, :], w256[:, :, :]))
            nc.vector.tensor_tensor(kept.w_lo[:, :, :], w256[:, :, :], kept.w_hi[:, :, :], ALU.subtract
                                    ).then_inc(w_ready, 1)
            dve.wait_ge(a0_kept, NQ)
            stages(step, dve)
            dve.wait_ge(sc_done, B * NQ)
            link(nc.vector.tensor_scalar(l0.sc1[:, :, :], l0.sc1[:, :, :], 1.0 / SX / SX, None, ALU.mult))
            link(nc.vector.memset(l0.sc1[0:1, :, 0], 0.0))
            link(nc.vector.memset(l0.c6[:, :], 1.0 / SH))
            link(nc.vector.memset(l0.c6[0:1, 0:1], 0.0))
            dve.wait_ge(ident_ready, 1)
            link(nc.vector.memset(l0.ones_b[:, :], 1.0))
            link(nc.vector.tensor_tensor(l0.pick[:, :], id32[:, 0:1], id32[:, LO:LO + 1], ALU.add))
            link(nc.vector.tensor_scalar(l0.pick[:, :], l0.pick[:, :], 1.0 / SM, None, ALU.mult))
            link(nc.vector.tensor_scalar(l0.not_last[:, :], id16[:, P - 1:P], -1.0, 1.0, ALU.mult, ALU.add))
            dve.wait_ge(hs_done, B)
            link(nc.vector.tensor_scalar(l0.hsum[:, :, :].rearrange("p b d -> p (b d)"), ps_s, 1.0 / SH, None, ALU.mult))
            for half in (l0.h_hi, l0.h_lo):
                link(nc.vector.memset(half[0:1, 0, :, :], 0.0))
                link(nc.vector.tensor_scalar(half[:, T - 1, :, :], half[:, T - 1, :, :], l0.not_last[:, :], None,
                                             ALU.mult))

        @block.tensor
        def _(pe):
            def turn(q, Q):
                pe.wait_ge(x_hi, Q + 1)
                pe.wait_ge(x_lo, Q + 1)
                if not before(Q, 2):
                    pe.wait_ge(x_tk, Q - 1)
                for k in range(QT):
                    mm = nc.tensor.transpose(ps_t[q % 2][:, k, :], xs[:, q % 2, k, :], id16[:, :])
                mm.then_inc(x_t, 1)

            def sum_rows(b):
                pe.wait_ge(h_used, NQ * b + NQ)
                for half in (l0.h_hi, l0.h_lo):
                    for t in range(T):
                        mm = nc.tensor.matmul(ps_s[:, D * b:D * b + D] if isinstance(b, int) else ps_s[:, bass.ds(D * b, D)],
                                              l0.ones[:, min(t, 1), :], half[:, t, b, :],
                                              start=(half is l0.h_hi and t == 0), stop=(half is l0.h_lo and t == T - 1))
                mm.then_inc(hs_done, 1)

            def step(bp, par, q):
                b, Q = 2 * bp + par, number(bp, par, q)
                if after(bp, par, q, 1):
                    turn(after(bp, par, q, 1)[2], Q + 1)
                pe.wait_ge(x_tk, Q + 1)
                if not before(Q, 2):
                    pe.wait_ge(h_used, Q - 1)
                    pe.wait_ge(h_hi, Q - 1)
                for k in range(QT):
                    for w in (kept.w_hi, kept.w_lo):
                        mm = nc.tensor.matmul(ps_h[q % 2][:, k, :], xt[:, q % 2, k, :], w[:, 0, 0:D],
                                              start=(w is kept.w_hi), stop=(w is kept.w_lo))
                mm.then_inc(h_done, 1)
                if q == 2 and not before(Q, NQ):
                    sum_rows(b - 1)

            pe.wait_ge(ident_ready, 2)
            turn(0, 0)
            pe.wait_ge(a0_in, 16)
            for t in range(T):
                tr = nc.tensor.transpose(psum[:, 2048 + P * t:2048 + P * t + P], a0[:, P * t:P * t + P], id32[:, :])
                if t % QT == QT - 1:
                    tr.then_inc(a0T, 1)
            pe.wait_ge(w_ready, 1)
            pe.wait_ge(ones_set, 1)
            pe.wait_ge(a0_kept, NQ)
            stages(step, pe)
            sum_rows(B - 1)


def load_adj(sp, adj, stage, r, cq, sem):
    cols = slice(512 * cq, 512 * cq + 512)
    lo = 1 + 512 * r
    if r < NQ - 1:
        sp.dma_start(stage[:, r, :, :], adj[lo:lo + 512, cols].rearrange("(t p) c -> p t c", p=P)).then_inc(sem, 16)
    else:
        sp.dma_start(stage[:, r, 0:3, :], adj[lo:lo + 384, cols].rearrange("(t p) c -> p t c", p=P)).then_inc(sem, 16)
        sp.dma_start(stage[0:112, r, 3, :], adj[lo + 384:lo + 496, cols]).then_inc(sem, 16)
        sp.dma_start(stage[112:127, r, 3, :], adj[lo + 496:lo + 511, cols]).then_inc(sem, 16)


def layer_0(nc, kept, l0, sems, A, psum):
    x, maskT = kept.x, kept.maskT
    cast, turned, mask_kept, tile_used = sems("m_cast"), sems("m_turned"), sems("m_kept"), sems("m_tile_used")
    acc_done, acc_read = sems("l0_acc_done"), sems("l0_acc_read")
    row0_kept, counted = sems("row0_kept"), sems("counted")
    yc_ready, sq_done, var_ready, rstd_ready, x_done = (sems(n) for n in (
        "l0_yc", "l0_sq", "l0_var", "l0_rstd", "l0_x_done"))

    with ExitStack() as ctx:
        def sb(name, shape, dt):
            return ctx.enter_context(nc.sbuf_tensor(name, shape, dt))

        RING = 8
        tile = sb("mask_tiles", [P, RING, 512], BF16)
        m1 = sb("m1", [P, QT, B, D], F32)
        v = sb("v0", [P, 2, B, D], F32)
        y = sb("y0", [P, 2, B, D], F32)
        yc = sb("yc0", [P, 2, B, D], F32)
        st = sb("st0", [P, 2, 8, B], F32)
        acc = [psum[:, 512 * i:512 * i + 512] for i in range(QT)]
        ps_m = [psum[:, 512 * i:512 * i + 256].bitcast(BF16).rearrange("p (c n) -> p c n", c=QT) for i in (4, 5)]
        ps_s = psum[:, 512 * 6:512 * 7]
        block = ctx.enter_context(nc.Block())

        @block.sync
        def _(sp):
            for cq in range(1, NQ):
                for r in range(NQ):
                    sp.wait_ge(cast, T * cq - T + QT * r + QT)
                    load_adj(sp, A["adj"], l0.stage, r, cq, l0.adj_in[r])

        @block.gpsimd
        def _(pool):
            def finish(cq, c):
                J, r = QT * cq + c, c % 2
                s = st[:, r, :, :]
                pool.wait_ge(yc_ready, J + 1)
                nc.gpsimd.tensor_tensor(y[:, r, :, :], yc[:, r, :, :], yc[:, r, :, :], ALU.mult).then_inc(sq_done, 1)
                pool.wait_ge(var_ready, J + 1)
                nc.gpsimd.tensor_tensor(s[:, 4, :], s[:, 3, :], kept.neg_half[:, 0:B], ALU.pow).then_inc(rstd_ready, 1)
                pool.wait_ge(rstd_ready, J + 1)
                nc.gpsimd.tensor_tensor(x[:, :, bass.ds(J, 1), :].rearrange("p b o d -> p b (o d)"), yc[:, r, :, :],
                                        over(s[:, 4, :], [P, B, D], 2), ALU.mult).then_inc(x_done, 1)

            with pool.Fori(0, NQ) as cq:
                for c in range(QT):
                    finish(cq, c)

        @block.scalar
        def _(act):
            def sweep(cq, first):
                for t in range(T):
                    m = T * cq + t
                    act.wait_ge(turned, m + 1)
                    n = P if t < T - 1 else P - 1
                    nc.scalar.copy(maskT[:, bass.ds(QT * cq, QT), 1 + P * t:1 + P * t + n], ps_m[t % 2][:, :, 0:n]
                                   ).then_inc(mask_kept, 1)

            sweep(0, True)
            with act.Fori(1, NQ) as cq:
                sweep(cq, False)

        @block.tensor
        def _(pe):
            def sweep(cq, first):
                for t in range(T):
                    m = T * cq + t
                    pe.wait_ge(cast, m + 1)
                    if not (first and t < 2):
                        pe.wait_ge(mask_kept, m - 1)
                    for c in range(QT):
                        tr = nc.tensor.transpose(ps_m[t % 2][:, c, :], tile[:, t % RING, P * c:P * c + P], kept.idb[:, :])
                    tr.then_inc(turned, 1)
                    for c in range(QT):
                        if t == 0 and not first:
                            pe.wait_ge(acc_read, QT * cq - QT + c + 1)
                        for half in (l0.h_hi, l0.h_lo):
                            mm = nc.tensor.matmul(acc[c], tile[:, t % RING, P * c:P * c + P],
                                                  half[:, t, :, :].rearrange("p b d -> p (b d)"),
                                                  start=(t == 0 and half is l0.h_hi),
                                                  stop=(t == T - 1 and half is l0.h_lo))
                        if t == T - 1:
                            mm.then_inc(acc_done, 1)
                    if t < T - 1:
                        mm.then_inc(tile_used, 1)
                    else:
                        nc.tensor.matmul(ps_s[:, 0:1], l0.ones[:, 1, :], l0.ones[:, 1, 0:1], start=True, stop=True
                                         ).then_inc(tile_used, 1)

            sweep(0, True)
            with pe.Fori(1, NQ) as cq:
                sweep(cq, False)
            pe.wait_ge(mask_kept, T * NQ)
            pe.wait_ge(row0_kept, 1)
            for t in range(T):
                for c in range(NQ):
                    mm = nc.tensor.matmul(psum[:, 2048 + 512 * c:2560 + 512 * c], l0.ones_b[:, :],
                                          maskT[:, t, 512 * c:512 * c + 512], start=(t == 0), stop=(t == T - 1))
            mm.then_inc(counted, 1)

        @block.vector
        def _(dve):
            dve.wait_ge(l0.row0_in, 16)
            nc.vector.tensor_scalar(maskT[:, :, 0], l0.row0[:, :], 0, None, ALU.is_gt).then_inc(row0_kept, 1)

            def post_read(cq):
                for c in range(QT):
                    J = QT * cq + c
                    dve.wait_ge(acc_done, J + 1)
                    a2 = l0.a12[:, bass.ds(J, 1), D:P].to_broadcast([P, B, D])
                    nc.vector.tensor_tensor(m1[:, c, :, :], acc[c].rearrange("p (b d) -> p b d", b=B), a2, ALU.mult
                                            ).then_inc(acc_read, 1)

            def post(cq, c, part):
                J, r = QT * cq + c, c % 2
                s = st[:, r, :, :]

                def lk(k, ins):
                    ins.then_inc(post_order, 1)
                    dve.wait_ge(post_order, POST * J + k)

                xj = x[:, :, bass.ds(J, 1), :].rearrange("p b o d -> p b (o d)")
                if part == 1:
                    dve.wait_ge(m1_summed, J + 1)
                    lk(1, nc.vector.scalar_tensor_tensor(out=s[:, 1, :], in0=s[:, 0, :], scalar=l0.c6[:, bass.ds(J, 1)],
                                                         in1=l0.sc1[:, :, bass.ds(J, 1)].rearrange("p b o -> p (b o)"),
                                                         op0=ALU.mult, op1=ALU.add))
                    lk(2, nc.vector.tensor_tensor(v[:, r, :, :], l0.hsum[:, :, :], over(s[:, 1, :], [P, B, D], 2), ALU.mult))
                    lk(3, nc.vector.scalar_tensor_tensor(out=y[:, r, :, :], in0=v[:, r, :, :], scalar=0.2, in1=v[:, r, :, :],
                                                         op0=ALU.mult, op1=ALU.max))
                if part == 2:
                    lk(4, nc.vector.tensor_tensor(v[:, r, :, :], y[:, r, :, :], xj, ALU.add))
                    lk(5, nc.vector.tensor_reduce(s[:, 2, :], v[:, r, :, :], X, ALU.add))
                    if not (isinstance(cq, int) and cq == 0 and c < 2):
                        dve.wait_ge(x_done, J - 1)
                    nc.vector.scalar_tensor_tensor(out=yc[:, r, :, :], in0=over(s[:, 2, :], [P, B, D], 2),
                                                   scalar=-1.0 / D, in1=v[:, r, :, :], op0=ALU.mult, op1=ALU.add
                                                   ).then_inc(yc_ready, 1)
                if part == 3:
                    dve.wait_ge(sq_done, J + 1)
                    nc.vector.tensor_reduce(s[:, 5, :], y[:, r, :, :], X, ALU.add).then_inc(sq_summed, 1)
                    dve.wait_ge(sq_summed, J + 1)
                    nc.vector.tensor_scalar(s[:, 3, :], s[:, 5, :], 1.0 / D, EPS, ALU.mult, ALU.add).then_inc(var_ready, 1)

            def sum_m1(cq, c):
                J = QT * cq + c
                dve.wait_ge(acc_read, J + 1)
                if not (isinstance(cq, int) and cq == 0 and c < 2):
                    dve.wait_ge(post_order, POST * (J - 2) + 1)
                nc.vector.tensor_reduce(st[:, c % 2, 0, :], m1[:, c, :, :], X, ALU.add).then_inc(m1_summed, 1)

            PARTS = ((4, 0, 0), (4, 0, 1), (5, 0, 2), (7, 1, 0), (7, 1, 1), (8, 0, 3), (8, 1, 2), (10, 2, 0), (10, 2, 1),
                     (11, 1, 3), (11, 2, 2), (13, 3, 0), (13, 3, 1), (14, 2, 3), (14, 3, 2), (15, 3, 3))

            def parts(cq, at=None):
                for t, c, part in PARTS:
                    if at is None or t == at:
                        if part == 0:
                            sum_m1(cq, c)
                        else:
                            post(cq, c, part)

            POST = 5
            post_order, m1_summed, sq_summed = sems("l0_post"), sems("m1_summed"), sems("sq_summed")

            def sweep(cq, first):
                for t in range(T):
                    m = T * cq + t
                    if t % QT == 0:
                        dve.wait_ge(l0.adj_in[t // QT], (48 if t // QT == NQ - 1 else 16) * (cq + 1))
                    if not (first and t < RING):
                        dve.wait_ge(tile_used, m - RING + 1)
                    nc.vector.tensor_scalar(tile[:, t % RING, :], l0.stage[:, t // QT, t % QT, :], 0, None, ALU.is_gt
                                            ).then_inc(cast, 1)
                    if not first and t == 3:
                        post_read(cq - 1)
                    if not first:
                        parts(cq - 1, t)

            sweep(0, True)
            sweep(1, False)
            with dve.Fori(2, NQ) as cq:
                sweep(cq, False)
            post_read(NQ - 1)
            parts(NQ - 1)
            dve.wait_ge(counted, 1)
            nc.vector.tensor_scalar(kept.none[:, :], psum[:, 2048:4096], 0.0, l0.pick[:, :], ALU.is_equal, ALU.mult)


def layer_1(nc, kept, sems, psum):
    x, maskT = kept.x, kept.maskT
    qk_done, exp_done, mul_done, pv_done = sems("qk_done"), sems("exp_done"), sems("mul_done"), sems("pv_done")
    hi_done, lo_done, turned, ab_ready = sems("a_hi"), sems("a_lo"), sems("a_turned"), sems("a_ready")
    xv_ready = sems("xv_ready")
    o_out, o_turned, o_rows = sems("o_out"), sems("o_turned"), sems("o_rows")
    sum_wide, mean_ps, mean_kept = sems("sum_wide"), sems("mean_ps"), sems("mean_kept")
    q_summed, mean_order = sems("q_summed"), sems("mean_order")
    yc_ready, sq_done, var_ready, rstd_ready = sems("l1_yc"), sems("l1_sq"), sems("l1_var"), sems("l1_rstd")
    post_order, x_done = sems("l1_post"), sems("l1_x_done")
    CH = 2 * T
    LAG = 4
    POST = 6

    with ExitStack() as ctx:
        def sb(name, shape, dt):
            return ctx.enter_context(nc.sbuf_tensor(name, shape, dt))

        xa = sb("xa", [P, 2, N], F16)
        xb = sb("xb", [P, 2, N], F16)
        xs = sb("xs1", [P, QT, 3, D], F16)
        xv = sb("xv", [P, 2, T, D], F32)
        e = sb("e", [P, 4, 1024], F32)
        pm = sb("pm", [P, 2 * LAG, 1024], F32)
        oT = sb("oT", [P, 1024], F32)
        o = sb("o", [P, T, D], F32)
        y = sb("y1", [P, T, D], F32)
        yc = sb("yc1", [P, T, D], F32)
        st = sb("st1", [P, 8, T], F32)
        qsum = sb("qsum1", [P, 2, NQ], F32)
        wide = sb("wide1", [P, P], F32)
        mean = sb("mean1", [P, 2, D], F16)
        S = [psum[:, 1024 * h:1024 * h + 1024] for h in (0, 1)]
        acc = [psum[:, 2048 + 512 * j:2560 + 512 * j] for j in (0, 1)]
        ps_x = psum[:, 3072:3584].bitcast(F16).rearrange("p (u t n) -> p u t n", u=2, t=QT)
        ps_o = psum[:, 3584:3840]
        ps_mean = psum[:, 3840:3840 + D]
        block = ctx.enter_context(nc.Block())

        @block.gpsimd
        def _(pool):
            nc.gpsimd.memset(xv[:, :, :, D - 1:D], 1.0).then_inc(xv_ready, 1)

            def rstd(g):
                pool.wait_ge(var_ready, g + 1)
                nc.gpsimd.tensor_tensor(st[:, 5, :], st[:, 4, :], kept.neg_half[:, :], ALU.pow).then_inc(rstd_ready, 1)

            rstd(0)
            with pool.Fori(1, B) as b:
                rstd(b)

        @block.tensor
        def _(pe):
            def pv(b, par, mt, s):
                pe.wait_ge(mul_done, 2 * s + 2)
                if mt == 0:
                    pe.wait_ge(xv_ready, b + 2)
                if mt == T - 1:
                    pe.wait_ge(mean_kept, b + 1)
                for j in (0, 1):
                    for h in (0, 1):
                        mm = nc.tensor.matmul(acc[j][D * h:D * h + D, :], xv[:, par, mt, :],
                                              pm[:, 2 * (mt % LAG) + h, 512 * j:512 * j + 512],
                                              start=(mt == 0), stop=False)
                if mt == T - 1:
                    for j in (0, 1):
                        for h in (0, 1):
                            q = 1024 * h + 512 * j
                            mm = nc.tensor.matmul(acc[j][D * h:D * h + D, :], mean[:, par, :], kept.none[:, q:q + 512],
                                                  start=False, stop=True)
                mm.then_inc(pv_done, 1)

            def turn_x(par, q, Q):
                pe.wait_ge(hi_done, Q + 1)
                pe.wait_ge(lo_done, Q + 1)
                if not (isinstance(Q, int) and Q == 0):
                    pe.wait_ge(ab_ready, Q)
                for u in (0, 1):
                    for k in range(QT):
                        tr = nc.tensor.transpose(ps_x[:, u, k, :], xs[:, k, u:u + 2, :].rearrange("p u d -> p (u d)"),
                                                 kept.id16[:, :])
                tr.then_inc(turned, 1)

            def turn_o(g, i):
                pe.wait_ge(o_out, 2 * g + 2)
                if not (isinstance(g, int) and g == 0 and i == 0):
                    pe.wait_ge(o_rows, 4 * g + i)
                if i == 0 and not (isinstance(g, int) and g == 0):
                    pe.wait_ge(mean_kept, g + 1)
                for k in (0, 1):
                    tr = nc.tensor.transpose(ps_o[:, P * k:P * k + P], oT[:, P * (2 * i + k):P * (2 * i + k) + P],
                                             kept.id32[:, :])
                tr.then_inc(o_turned, 1)

            def mean_of(g):
                pe.wait_ge(sum_wide, g + 1)
                if not (isinstance(g, int) and g == 0):
                    pe.wait_ge(o_rows, 4 * g)
                nc.tensor.matmul(ps_mean, wide[:, :], kept.eye2[:, :], start=True, stop=True).then_inc(mean_ps, 1)

            def body(b, par, first, last=False):
                for mt in range(T):
                    s = T * b + mt
                    if mt == 0:
                        pe.wait_ge(ab_ready, NQ * b + NQ)
                    for h in (0, 1):
                        if not (first and mt == 0):
                            pe.wait_ge(exp_done, 2 * s + h - 1)
                        for nb in (0, 1):
                            for xm in (xa, xb):
                                mm = nc.tensor.matmul(S[h][:, 512 * nb:512 * nb + 512],
                                                      xa[:, par, P * mt:P * mt + P],
                                                      xm[:, par, 1024 * h + 512 * nb:1024 * h + 512 * nb + 512],
                                                      start=(xm is xa), stop=(xm is xb))
                        mm.then_inc(qk_done, 1)
                    if mt > 1:
                        if mt == 2 and not first:
                            pe.wait_ge(o_out, 2 * b)
                        pv(b, par, mt - 2, s - 2)
                    elif not first:
                        pv(b - 1, 1 - par, T - 2 + mt, s - 2)
                    if mt % 3 == 2 and mt < 12 and not last:
                        turn_x(1 - par, mt // 3, NQ * b + NQ + mt // 3)
                    if mt in (2, 3, 4, 5) and not first:
                        turn_o(b - 1, mt - 2)
                    if mt == 10:
                        mean_of(b)

            for q in range(NQ):
                turn_x(0, q, q)
            body(0, 0, True)
            body(1, 1, False)
            with pe.Fori(1, B // 2 - 1) as bp:
                body(2 * bp, 0, False)
                body(2 * bp + 1, 1, False)
            body(B - 2, 0, False)
            body(B - 1, 1, False, last=True)
            pv(B - 1, 1, T - 2, T * B - 2)
            pv(B - 1, 1, T - 1, T * B - 1)
            for i in range(4):
                turn_o(B - 1, i)

        @block.scalar
        def _(act):
            def values(b, par):
                nc.scalar.activation(xv[:, par, :, 0:D - 1], x[:, b, :, 0:D - 1], ACT.Copy).then_inc(xv_ready, 1)

            def split_hi(b, q, Q, first):
                if not first:
                    act.wait_ge(turned, Q)
                nc.scalar.activation(xs[:, :, 0:3:2, :], over(x[:, b, QT * q:QT * q + QT, :], [P, QT, 2, D], 2),
                                     ACT.Copy, scale=SX).then_inc(hi_done, 1)

            def keep_x(par, q, Q):
                act.wait_ge(turned, Q + 1)
                nc.scalar.activation(xa[:, par, 512 * q:512 * q + 512], ps_x[:, 0, :, :].rearrange("p t n -> p (t n)"),
                                     ACT.Copy, accum_out=qsum[:, par, q:q + 1])
                nc.scalar.copy(xb[:, par, 512 * q:512 * q + 512], ps_x[:, 1, :, :].rearrange("p t n -> p (t n)")
                               ).then_inc(ab_ready, 1)

            def keep_o(g, i):
                act.wait_ge(o_turned, 4 * g + i + 1)
                if i == 0 and not (isinstance(g, int) and g == 0):
                    act.wait_ge(x_done, g)
                nc.scalar.copy(o[:, :, :].rearrange("p (h t) d -> p t h d", h=2)[:, 2 * i:2 * i + 2, :, :],
                               ps_o.rearrange("p (t h d) -> p t h d", t=2, h=2)).then_inc(o_rows, 1)

            def out_sums(g):
                act.wait_ge(pv_done, T * g + T)
                if not (isinstance(g, int) and g == 0):
                    act.wait_ge(o_turned, 4 * g)
                nc.scalar.copy(oT[:, 0:512], psum[:, 2048:2560]).then_inc(o_out, 1)

            def square(g):
                act.wait_ge(yc_ready, g + 1)
                nc.scalar.activation(y[:, :, :], yc[:, :, :], ACT.Square).then_inc(sq_done, 1)

            def body(b, par, first, last=False):
                for mt in range(T):
                    s = T * b + mt
                    for h in (0, 1):
                        act.wait_ge(qk_done, 2 * s + h + 1)
                        if not (first and mt < 2):
                            act.wait_ge(mul_done, 2 * s + h - 3)
                        nc.scalar.activation(e[:, (2 * mt + h) % 4, :], S[h], ACT.Exp, scale=1.0 / SX / SX / 8.0
                                             ).then_inc(exp_done, 1)
                    if mt == 1 and not first:
                        out_sums(b - 1)
                    if mt % 3 == 0 and mt <= 12 and not last:
                        q = mt // 3
                        if q > 0:
                            keep_x(1 - par, q - 1, NQ * b + NQ + q - 1)
                        if q < NQ:
                            split_hi(b + 1, q, NQ * b + NQ + q, False)
                    if mt in (3, 4, 5, 6) and not first:
                        keep_o(b - 1, mt - 3)
                    if mt == 13 and not first:
                        square(b - 1)
                    if mt == 14 and not last:
                        values(b + 1, 1 - par)

            for q in range(NQ):
                split_hi(0, q, q, q == 0)
                keep_x(0, q, q)
            values(0, 0)
            body(0, 0, True)
            body(1, 1, False)
            with act.Fori(1, B // 2 - 1) as bp:
                body(2 * bp, 0, False)
                body(2 * bp + 1, 1, False)
            body(B - 2, 0, False)
            body(B - 1, 1, False, last=True)
            out_sums(B - 1)
            for i in range(4):
                keep_o(B - 1, i)
            square(B - 1)

        @block.vector
        def _(dve):
            def split_lo(b, q, Q):
                dve.wait_ge(hi_done, Q + 1)
                nc.vector.scalar_tensor_tensor(out=xs[:, :, 1, :], in0=x[:, b, QT * q:QT * q + QT, :], scalar=SX,
                                               in1=xs[:, :, 0, :], op0=ALU.mult, op1=ALU.subtract).then_inc(lo_done, 1)

            def widen(par, g):
                dve.wait_ge(ab_ready, NQ * g + NQ)
                link1(g, nc.vector.tensor_reduce(st[:, 7, 0:1], qsum[:, par, :], X, ALU.add))
                nc.vector.tensor_scalar(wide[:, :], st[:, 7, 0:1].to_broadcast([P, P]), SM / SX / N, None, ALU.mult
                                        ).then_inc(sum_wide, 1)

            def keep_mean(par, g):
                link2(g, 1, nc.vector.tensor_copy(mean[:, par, 0:D - 1], ps_mean[:, 0:D - 1]))
                nc.vector.tensor_tensor(mean[LO:D, par, 0:D - 1], ps_mean[LO:D, 0:D - 1], mean[LO:D, par, 0:D - 1],
                                        ALU.subtract).then_inc(mean_kept, 1)

            def link2(g, k, ins):
                ins.then_inc(mean_order, 1)
                dve.wait_ge(mean_order, 2 + g + k)

            def link1(g, ins):
                ins.then_inc(q_summed, 1)
                dve.wait_ge(q_summed, g + 1)

            def link(g, k, ins):
                ins.then_inc(post_order, 1)
                dve.wait_ge(post_order, POST * g + k)

            def post(par, g, part):
                xg = x[:, g, :, :]
                if part == 1:
                    dve.wait_ge(o_rows, 4 * g + 4)
                    link(g, 1, nc.vector.reciprocal(st[:, 1, :], o[:, :, D - 1]))
                    link(g, 2, nc.vector.tensor_reduce(o[:, :, D - 1:D], o[:, :, 0:D - 1], X, ALU.add, negate=True))
                if part == 2:
                    link(g, 3, nc.vector.tensor_tensor(o[:, :, :], o[:, :, :], over(st[:, 1, :], [P, T, D], 2), ALU.mult))
                if part == 4:
                    link(g, 4, nc.vector.tensor_tensor(y[:, :, :], o[:, :, :], xg, ALU.add))
                if part == 5:
                    link(g, 5, nc.vector.tensor_reduce(st[:, 2, :], y[:, :, :], X, ALU.add))
                    nc.vector.scalar_tensor_tensor(out=yc[:, :, :], in0=over(st[:, 2, :], [P, T, D], 2), scalar=-1.0 / D,
                                                   in1=y[:, :, :], op0=ALU.mult, op1=ALU.add).then_inc(yc_ready, 1)
                if part == 6:
                    dve.wait_ge(sq_done, g + 1)
                    link(g, 6, nc.vector.tensor_reduce(st[:, 3, :], y[:, :, :], X, ALU.add))
                    nc.vector.tensor_scalar(st[:, 4, :], st[:, 3, :], 1.0 / D, EPS, ALU.mult, ALU.add
                                            ).then_inc(var_ready, 1)
                if part == 7:
                    dve.wait_ge(rstd_ready, g + 1)
                    nc.vector.tensor_tensor(xg, yc[:, :, :], over(st[:, 5, :], [P, T, D], 2), ALU.mult).then_inc(x_done, 1)

            def out_sums(g):
                dve.wait_ge(pv_done, T * g + T)
                if not (isinstance(g, int) and g == 0):
                    dve.wait_ge(o_turned, 4 * g)
                nc.vector.tensor_copy(oT[:, 512:1024], psum[:, 2560:3072]).then_inc(o_out, 1)

            def body(b, par, first, last=False):
                for mt in range(T):
                    s = T * b + mt
                    if mt == 2 and not first:
                        out_sums(b - 1)
                    for h in (0, 1):
                        dve.wait_ge(exp_done, 2 * s + h + 1)
                        if not (first and mt < LAG):
                            dve.wait_ge(pv_done, s - LAG + 1)
                        nc.vector.tensor_tensor(pm[:, 2 * (mt % LAG) + h, :], e[:, (2 * mt + h) % 4, :],
                                                maskT[:, mt, 1024 * h:1024 * h + 1024], ALU.mult).then_inc(mul_done, 1)
                    if mt < 12 and mt % 3 == 1 and not last:
                        split_lo(b + 1, mt // 3, NQ * b + NQ + mt // 3)
                    if mt == 0:
                        widen(par, b)
                    if mt == 11:
                        dve.wait_ge(mean_ps, b + 1)
                        keep_mean(par, b)
                    if not first and mt in PART_AT:
                        post(1 - par, b - 1, PART_AT[mt])

            nc.vector.memset(mean[:, :, D - 1:D], SM).then_inc(mean_order, 1)
            dve.wait_ge(mean_order, 1)
            nc.vector.memset(mean[LO:D, :, D - 1:D], 0.0).then_inc(mean_order, 1)
            for q in range(NQ):
                split_lo(0, q, q)
            PART_AT = {7: 1, 8: 2, 9: 4, 10: 5, 13: 6, 15: 7}
            body(0, 0, True)
            body(1, 1, False)
            with dve.Fori(1, B // 2 - 1) as bp:
                body(2 * bp, 0, False)
                body(2 * bp + 1, 1, False)
            body(B - 2, 0, False)
            body(B - 1, 1, False, last=True)
            out_sums(B - 1)
            for part in (1, 2, 4, 5, 6, 7):
                post(1, B - 1, part)


def layers_2_3(nc, kept, sems, psum, scratch, out):
    x, maskT = kept.x, kept.maskT
    BIG = 2.0 ** 40
    SV = 256.0
    W1 = D + 1
    ZR = 5
    ALONE = 2
    R = T - 1
    APART = ((0, 4, 8, 12), (0, 8))
    LEAD = 4
    G = 2 * B
    relu_done, mp_done, av_done, evac = sems("relu_done"), sems("mp_done"), sems("av_done"), sems("uv_evac")
    hi_done, lo_done, turned, xt_ready, h_ps, h_kept = (sems(n) for n in (
        "g_hi", "g_lo", "g_turned", "g_xt", "g_h_ps", "g_h_kept"))
    top_part, top_all, args_ready, ex_ready, bias_ready = (sems(n) for n in (
        "top_part", "top_all", "args_ready", "ex_ready", "bias_ready"))
    v_done, v_hi, v_lo, v_ready = sems("v_done"), sems("v_hi"), sems("v_lo"), sems("v_ready")
    q_summed, sum_wide, mean_ps, mean_kept = sems("g_q_summed"), sems("g_wide"), sems("g_mean_ps"), sems("g_mean_kept")
    s_out, r_in = sems("s_out"), [sems("r_in0"), sems("r_in1")]
    uv_used, elu_out = sems("uv_used"), sems("elu_out")
    mean_order, neg_ready = sems("g_mean_order"), sems("neg_ready")
    yc_ready, sq_done, var_ready, rstd_ready = sems("g_yc"), sems("g_sq"), sems("g_var"), sems("g_rstd")
    post_order, sc_order, x_done, out_done, ones_set = (sems(n) for n in (
        "g_post", "g_sc", "g_x_done", "out_done", "ones_set"))
    POST = (5, 9)

    with ExitStack() as ctx:
        def sb(name, shape, dt):
            return ctx.enter_context(nc.sbuf_tensor(name, shape, dt))

        si = sb("si", [P, 2, N], F32)
        z = sb("z", [P, ZR, N], BF16)
        mp = sb("mp", [P, LEAD, N], BF16)
        mn = sb("mn", [P, N], BF16)
        v = sb("v", [P, T, 6, W1], F16)
        vf = sb("vf", [P, 2, QT, W1], F32)
        h = sb("h", [P, 2, T, D + 3], F32)
        xs = sb("xs2", [P, NQ, QT, 2, D], F16)
        xt = sb("xt2", [P, 2, QT * P], F16)
        qsum = sb("qsum", [P, 2, NQ], F32)
        wide = sb("wide", [P, P], F32)
        mean = sb("mean", [P, 2, 2, W1], F16)
        args = sb("args", [P, 4, T], F32)
        ex = sb("ex", [P, 2, 4, T], F32)
        bias = sb("bias", [P, 2, T], F32)
        tops = sb("tops", [P, 4], F32)
        tt = sb("tt", [P, T], F32)
        uv = sb("uv", [P, T, 2, W1], F32)
        o = sb("o2", [P, T, W1], F32)
        y = sb("y2", [P, T, D], F32)
        centred, squares = (y[:, :, :], o[:, :, 1:W1]), (o[:, :, 1:W1], y[:, :, :])
        st = sb("st2", [P, 8, T], F32)
        big = sb("big", [P, T], F32)
        minus = sb("minus", [P, 1], F32)
        neg_sj = sb("neg_sj", [P, 2, 1], F32)
        ps_x = psum[:, 3072:3328].bitcast(F16)
        ps_h = psum[:, 3584:3584 + QT * (D + 2)].rearrange("p (t d) -> p t d", t=QT)
        ps_mean = psum[:, 3584 + QT * (D + 2):3584 + QT * (D + 2) + D]

        def tile_sum(it):
            c = 512 * (it // 3) + 2 * W1 * (it % 3)
            return psum[:, c:c + 2 * W1]

        block = ctx.enter_context(nc.Block())

        def drive(eng, body, pair=None):
            for lay in (0, 1):
                body(lay, 0, 0, (lay, 2))
                body(lay, 1, 1, (lay, 3))
                with eng.Fori(1, B // 2 - 1) as bp:
                    if pair is not None:
                        pair[0] = bp
                    for par in (0, 1):
                        body(lay, 2 * bp + par, par, (lay, 2 * bp + par + 2))
                for par in (0, 1):
                    body(lay, B - 2 + par, par, (1, par) if lay == 0 else None)

        def relu_no(jt):
            return jt if jt < ALONE else jt - 1

        def relu_step(k):
            return k if k < ALONE else k + 1

        def is0(g):
            return isinstance(g, int) and g == 0

        def last_of_all(lay, b):
            return lay == 1 and isinstance(b, int) and b == B - 1

        @block.sync
        def _(sp):
            def load_si(g, par):
                sp.wait_ge(h_kept, NQ * g + NQ)
                sp.dma_start(scratch[par:par + 1, :].rearrange("o (t p) -> p (o t)", p=P), h[:, par, :, D + 1],
                             allow_slow_non_contiguous=True).then_inc(s_out, 16)
                if g >= 2:
                    sp.wait_ge(relu_done, R * g - R)
                    sp.wait_ge(mp_done, T * g - 2 * T + ALONE + 1)
                sp.wait_ge(s_out, 16 * g + 16)
                sp.dma_start(si[:, par, :], scratch[par:par + 1, :].to_broadcast([P, N])).then_inc(r_in[par], 16)

            def store(b, g):
                sp.wait_ge(x_done, g + 1)
                sp.dma_start(rows(out[b]), x[:, b, :, :]).then_inc(out_done, 16)

            load_si(0, 0)
            for g in range(G):
                if g + 1 < G:
                    load_si(g + 1, (g + 1) % 2)
                if g >= B + 1:
                    store(g - B - 1, g - 1)
            store(B - 1, G - 1)
            sp.wait_ge(out_done, 16 * B)

        @block.gpsimd
        def _(pool):
            nc.gpsimd.memset(big[:, :], BIG).then_inc(ones_set, 1)
            nc.gpsimd.memset(h[:, :, :, 0:1], 1.0).then_inc(ones_set, 1)
            nc.gpsimd.memset(minus[:, :], -1.0).then_inc(ones_set, 1)
            pool.wait_ge(ones_set, 3)

            def top_of(g, par):
                pool.wait_ge(top_part, g + 1)
                nc.gpsimd.tensor_tensor(bias[:, par, :], h[:, par, :, D + 2], big[:, :], ALU.mult).then_inc(bias_ready, 1)
                nc.gpsimd.tensor_tensor(neg_sj[:, par, :], h[:, par, ALONE, D + 2:D + 3], minus[:, :], ALU.mult
                                        ).then_inc(neg_ready, 1)
                nc.gpsimd.partition_all_reduce(tops[:, 2:3], tops[:, 0:1], P, bass.bass_isa.ReduceOp.max
                                               ).then_inc(top_all, 1)

            def rstd(g):
                pool.wait_ge(var_ready, g + 1)
                nc.gpsimd.tensor_tensor(st[:, 5, :], st[:, 4, :], kept.neg_half[:, :], ALU.pow).then_inc(rstd_ready, 1)

            def body(lay, b, par, ahead):
                g = B * lay + b
                if not last_of_all(lay, b):
                    top_of(g + 1, 1 - par)
                if not is0(g):
                    rstd(g - 1)

            top_of(0, 0)
            drive(pool, body)
            rstd(G - 1)

        @block.tensor
        def _(pe):
            def turn(q, Q):
                pe.wait_ge(hi_done, Q + 1)
                pe.wait_ge(lo_done, Q + 1)
                if not is0(Q):
                    pe.wait_ge(xt_ready, Q)
                for k in range(QT):
                    tr = nc.tensor.transpose(ps_x[:, P * k:P * k + P], xs[:, q, k, :, :].rearrange("p u d -> p (u d)"),
                                             kept.id16[:, :])
                tr.then_inc(turned, 1)

            def times_w(lay, q, Q, g=None):
                pe.wait_ge(xt_ready, Q + 1)
                if not is0(Q):
                    pe.wait_ge(h_kept, Q)
                if q == 0 and g is not None:
                    pe.wait_ge(mean_kept, g + 1)
                for k in range(QT):
                    for w in (kept.w_hi, kept.w_lo):
                        mm = nc.tensor.matmul(ps_h[:, k, :], xt[:, q % 2, P * k:P * k + P], w[:, 1 + lay, :],
                                              start=(w is kept.w_hi), stop=(w is kept.w_lo))
                mm.then_inc(h_ps, 1)

            def mean_of(lay, g, kept_quarters):
                pe.wait_ge(sum_wide, g + 1)
                pe.wait_ge(h_kept, kept_quarters)
                nc.tensor.matmul(ps_mean, wide[:, :], kept.w_raw[:, 1 + lay, 0:D], start=True, stop=True
                                 ).then_inc(mean_ps, 1)

            def step(lay, g, par, jt):
                s = T * g + jt
                apart = jt in APART[lay]
                pe.wait_ge(mp_done, s + 1)
                if jt % QT == 0:
                    pe.wait_ge(v_ready, NQ * g + jt // QT + 1)
                w = v[:, jt, :, :]
                for it in range(T):
                    if jt == 0 and it % 3 == 0 and not is0(g):
                        pe.wait_ge(evac, 6 * g - 6 + it // 3 + 1)
                    a = mp[:, jt % LEAD, P * it:P * it + P]
                    m = mn[:, P * it:P * it + P] if apart else maskT[:, jt, P * it:P * it + P]
                    acc = tile_sum(it)
                    for half in (0, 1):
                        lead = w[:, 2 * half:2 * half + (1 if apart else 2), :].rearrange("p u d -> p (u d)")
                        nc.tensor.matmul(acc[:, 0:lead.shape[1]], a, lead,
                                         start=(jt == 0 and half == 0 and it % 3 == 0), stop=False,
                                         skip_group_check=True)
                    for half in (0, 1):
                        mm = nc.tensor.matmul(acc[:, W1:2 * W1], m, w[:, 4 + half, :], start=False, stop=False,
                                              skip_group_check=True)
                if jt == T - 1:
                    pe.wait_ge(mean_kept, g + 1)
                    for it in range(T):
                        mm = nc.tensor.matmul(tile_sum(it), kept.none[:, P * it:P * it + P],
                                              mean[:, par, :, :].rearrange("p u d -> p (u d)"), start=False,
                                              stop=(it % 3 == 2 or it == T - 1), skip_group_check=True)
                mm.then_inc(av_done, 1)

            def body(lay, b, par, ahead):
                g = B * lay + b
                for jt in range(T):
                    step(lay, g, par, jt)
                    if ahead:
                        Q = NQ * (g + 2)
                        if jt in (3, 6, 9, 12):
                            times_w(ahead[0], jt // 3 - 1, Q + jt // 3 - 1, g)
                        if jt in (0, 3, 6, 9):
                            turn(jt // 3, Q + jt // 3)
                    if jt == 0:
                        mean_of(lay, g, NQ * G if last_of_all(lay, b) else NQ * (g + 2))

            for Q in range(2 * NQ):
                turn(Q % NQ, Q)
                times_w(0, Q % NQ, Q)
            drive(pe, body)

        @block.scalar
        def _(act):
            def split_hi(b, q, Q):
                if not (isinstance(Q, int) and Q < NQ):
                    act.wait_ge(turned, Q - NQ + 1)
                nc.scalar.activation(xs[:, q, :, 0, :], x[:, b, QT * q:QT * q + QT, :], ACT.Copy, scale=SX
                                     ).then_inc(hi_done, 1)

            def keep_x(par, q, Q):
                act.wait_ge(turned, Q + 1)
                if not (isinstance(Q, int) and Q < 2):
                    act.wait_ge(h_ps, Q - 1)
                nc.scalar.activation(xt[:, q % 2, :], ps_x, ACT.Copy, accum_out=qsum[:, par, q:q + 1]
                                     ).then_inc(xt_ready, 1)

            def exps(g, par):
                act.wait_ge(args_ready, g + 1)
                if not (isinstance(g, int) and g < 2):
                    act.wait_ge(uv_used, g - 1)
                nc.scalar.activation(ex[:, par, :, :], args[:, :, :], ACT.Exp).then_inc(ex_ready, 1)

            def values_hi(q, Q):
                act.wait_ge(v_done, Q + 1)
                nc.scalar.copy(v[:, QT * q:QT * q + QT, 0:5:4, :].rearrange("p t u d -> p u t d"), vf[:, :, :, :]
                               ).then_inc(v_hi, 1)

            def values_minus(q, Q):
                act.wait_ge(v_lo, Q + 1)
                nc.scalar.activation(v[:, QT * q:QT * q + QT, 1:4:2, :], v[:, QT * q:QT * q + QT, 4:6, :], ACT.Copy,
                                     scale=-1.0).then_inc(v_ready, 1)

            def copy_sums(g):
                act.wait_ge(av_done, T * g + T)
                if not is0(g):
                    act.wait_ge(uv_used, g)
                for k in range(6):
                    n = 3 if k < 5 else 1
                    nc.scalar.copy(uv[:, 3 * k:3 * k + n, :, :].rearrange("p t u d -> p (t u d)"),
                                   psum[:, 512 * k:512 * k + 2 * W1 * n]).then_inc(evac, 1)

            def square(lay, g):
                act.wait_ge(yc_ready, g + 1)
                nc.scalar.activation(squares[lay], centred[lay], ACT.Square).then_inc(sq_done, 1)

            def elu_exp(g):
                act.wait_ge(uv_used, g + 1)
                nc.scalar.activation(y[:, :, :], o[:, :, 1:W1], ACT.Exp).then_inc(elu_out, 1)

            def body(lay, b, par, ahead):
                g = B * lay + b
                last = last_of_all(lay, b)
                for jt in range(T):
                    s = T * g + jt
                    if jt == 0:
                        act.wait_ge(r_in[par], 16 * count_pairs(lay, b, par))
                        act.wait_ge(bias_ready, g + 1)
                    if jt != ALONE:
                        k = relu_no(jt)
                        if k >= ZR:
                            act.wait_ge(mp_done, T * g + relu_step(k - ZR) + 1)
                        elif not is0(g):
                            act.wait_ge(mp_done, T * g - T + relu_step(R + k - ZR) + 1)
                        nc.scalar.activation(z[:, k % ZR, :], si[:, par, :], ACT.Relu, scale=BIG,
                                             bias=bias[:, par, jt:jt + 1]).then_inc(relu_done, 1)
                    if jt == 4 and not is0(g):
                        copy_sums(g - 1)
                    if ahead and jt % 2 == 0 and jt < 8:
                        q = jt // 2
                        if lay == 0 and ahead[0] == 1 and q == 0:
                            act.wait_ge(x_done, ahead[1] + 1)
                        split_hi(ahead[1], q, NQ * (g + 2) + q)
                    if ahead and jt in (4, 7, 10, 13):
                        q = jt // 3 - 1
                        keep_x(par, q, NQ * (g + 2) + q)
                    if jt == 7 and not last:
                        exps(g + 1, 1 - par)
                    Q = NQ * g + jt // QT + 2
                    if not (last and jt >= 8):
                        if jt % QT == 3:
                            values_hi((jt // QT + 2) % NQ, Q)
                    if jt % QT == 2 and jt > 2 and not (last and jt > 10):
                        values_minus((jt // QT + 1) % NQ, Q - 1)
                    if jt == 2 and not is0(g):
                        values_minus(1, Q - 1)
                    if not is0(g):
                        if jt == 8 and elu_here(lay, b):
                            elu_exp(g - 1)
                        lay1 = lay - 1 if isinstance(b, int) and b == 0 else lay
                        if jt == (10, 13)[lay1]:
                            square(lay1, g - 1)

            def count_pairs(lay, b, par):
                if isinstance(b, int):
                    return (B * lay + b) // 2 + 1
                return B // 2 * lay + pair[0] + 1

            def elu_here(lay, b):
                return lay == 1 and not is0(b)

            pair = [None]

            for Q in range(2 * NQ):
                split_hi(Q // NQ, Q % NQ, Q)
                keep_x(Q // NQ, Q % NQ, Q)
            exps(0, 0)
            for q in (0, 1):
                values_hi(q, q)
                values_minus(q, q)
            drive(act, body, pair)
            copy_sums(G - 1)
            elu_exp(G - 1)
            square(1, G - 1)

        @block.vector
        def _(dve):
            def split_lo(b, q, Q):
                dve.wait_ge(hi_done, Q + 1)
                nc.vector.scalar_tensor_tensor(out=xs[:, q, :, 1, :], in0=x[:, b, QT * q:QT * q + QT, :], scalar=SX,
                                               in1=xs[:, q, :, 0, :], op0=ALU.mult, op1=ALU.subtract).then_inc(lo_done, 1)

            def keep_h(par, q, Q, stored=None):
                dve.wait_ge(h_ps, Q + 1)
                if stored is not None:
                    dve.wait_ge(s_out, 16 * stored)
                nc.vector.tensor_scalar(h[:, par, QT * q:QT * q + QT, 1:D + 3], ps_h, 1.0 / SX / SX, None, ALU.mult
                                        ).then_inc(h_kept, 1)

            def tops_of(g, par):
                dve.wait_ge(h_kept, NQ * g + NQ)
                nc.vector.tensor_reduce(tops[:, 0:1], h[:, par, :, D + 2], X, ALU.max).then_inc(top_part, 1)

            def widen(g, par):
                dve.wait_ge(xt_ready, NQ * g + NQ)
                nc.vector.tensor_reduce(tops[:, 1:2], qsum[:, par, :], X, ALU.add).then_inc(q_summed, 1)
                dve.wait_ge(q_summed, g + 1)
                nc.vector.tensor_scalar(wide[:, :], tops[:, 1:2].to_broadcast([P, P]), SM / SX / N, None, ALU.mult
                                        ).then_inc(sum_wide, 1)

            def args_of(g, par):
                dve.wait_ge(top_all, g + 1)
                top, s_j = tops[:, 2:3], h[:, par, :, D + 2]
                if not is0(g):
                    dve.wait_ge(ex_ready, g)
                nc.vector.tensor_scalar(tt[:, :], h[:, par, :, D + 1], top, 0.8, ALU.add, ALU.mult).then_inc(sc_order, 1)
                dve.wait_ge(sc_order, g + 1)
                nc.vector.tensor_scalar(args[:, 0, :], tt[:, :], 0.0, None, ALU.min)
                nc.vector.tensor_scalar(args[:, 1, :], tt[:, :], -1.0, 0.0, ALU.mult, ALU.min)
                nc.vector.tensor_scalar(args[:, 2, :], s_j, top, None, ALU.subtract)
                nc.vector.tensor_scalar(args[:, 3, :], s_j, top, 0.2, ALU.subtract, ALU.mult).then_inc(args_ready, 1)

            def keep_mean(g, par):
                dve.wait_ge(mean_ps, g + 1)
                wide_mean = over(ps_mean, [P, 2, D], 1)
                mean_link(g, 1, nc.vector.tensor_copy(mean[:, par, :, 1:W1], wide_mean))
                nc.vector.tensor_tensor(mean[LO:D, par, :, 1:W1], wide_mean[LO:D], mean[LO:D, par, :, 1:W1], ALU.subtract
                                        ).then_inc(mean_kept, 1)

            def mean_link(g, k, ins):
                ins.then_inc(mean_order, 1)
                dve.wait_ge(mean_order, 2 + g + k)

            def values(q, Q, g, par):
                dve.wait_ge(ex_ready, g + 1)
                if not is0(Q):
                    dve.wait_ge(v_lo, Q)
                of_q = slice(QT * q, QT * q + QT)
                for u in (0, 1):
                    ins = nc.vector.scalar_tensor_tensor(out=vf[:, u, :, :], in0=h[:, par, of_q, 0:W1], scalar=SV,
                                                         in1=over(ex[:, par, 2 + u, of_q], [P, QT, W1], 2),
                                                         op0=ALU.mult, op1=ALU.mult)
                ins.then_inc(v_done, 1)

            def values_lo(q, Q):
                dve.wait_ge(v_hi, Q + 1)
                vq = v[:, QT * q:QT * q + QT, :, :].rearrange("p t u d -> p u t d")
                nc.vector.tensor_tensor(vq[:, 2:6:3, :, :], vf[:, :, :, :], vq[:, 0:5:4, :, :], ALU.subtract
                                        ).then_inc(v_lo, 1)

            def post(g, b, lay, par, part):
                def lk(k, ins):
                    ins.then_inc(post_order, 1)
                    dve.wait_ge(post_order, (POST[1] * b + POST[0] * B if lay else POST[0] * g) + k)

                xg, attn = x[:, b, :, :], squares[0] if lay else y[:, :, :]
                if part == 1:
                    dve.wait_ge(evac, 6 * g + 6)
                    gf = ex[:, par, 0:2, :]
                    lk(1, nc.vector.tensor_tensor(st[:, 0:2, :], uv[:, :, :, 0].rearrange("p t u -> p u t"), gf, ALU.mult))
                    lk(2, nc.vector.tensor_tensor(st[:, 2, :], st[:, 0, :], st[:, 1, :], ALU.add))
                    lk(3, nc.vector.reciprocal(st[:, 3, :], st[:, 2, :]))
                    lk(4, nc.vector.tensor_tensor(st[:, 0:2, :], gf, over(st[:, 3, :], [P, 2, T], 1), ALU.mult))
                    lk(5, nc.vector.tensor_tensor(uv[:, :, :, 1:W1], uv[:, :, :, 1:W1],
                                                  over(st[:, 0:2, :].rearrange("p u t -> p t u"), [P, T, 2, D], 3), ALU.mult))
                if part == 2:
                    nc.vector.tensor_tensor(attn, uv[:, :, 0, 1:W1], uv[:, :, 1, 1:W1], ALU.add).then_inc(uv_used, 1)
                if part == 3 and lay == 0:
                    dve.wait_ge(uv_used, g + 1)
                    nc.vector.tensor_tensor(y[:, :, :], attn, xg, ALU.add).then_inc(yc_ready, 1)
                if part == 4 and lay == 1:
                    dve.wait_ge(elu_out, b + 1)
                    lk(6, nc.vector.tensor_scalar(y[:, :, :], y[:, :, :], 1.0, -1.0, ALU.min, ALU.add))
                    lk(7, nc.vector.scalar_tensor_tensor(out=attn, in0=attn, scalar=0.0, in1=y[:, :, :],
                                                         op0=ALU.max, op1=ALU.add))
                    lk(8, nc.vector.tensor_tensor(y[:, :, :], attn, xg, ALU.add))
                if part == 5 and lay == 1:
                    lk(9, nc.vector.tensor_reduce(st[:, 2, :], y[:, :, :], X, ALU.add))
                    nc.vector.scalar_tensor_tensor(out=centred[1], in0=over(st[:, 2, :], [P, T, D], 2), scalar=-1.0 / D,
                                                   in1=y[:, :, :], op0=ALU.mult, op1=ALU.add).then_inc(yc_ready, 1)
                if part == 6:
                    dve.wait_ge(sq_done, g + 1)
                    nc.vector.tensor_reduce(st[:, 6, :], squares[lay], X, ALU.add).then_inc(var_sum, 1)
                    dve.wait_ge(var_sum, g + 1)
                    nc.vector.tensor_scalar(st[:, 4, :], st[:, 6, :], 1.0 / D, EPS, ALU.mult, ALU.add
                                            ).then_inc(var_ready, 1)
                if part == 7:
                    dve.wait_ge(rstd_ready, g + 1)
                    nc.vector.tensor_tensor(xg, centred[lay], over(st[:, 5, :], [P, T, D], 2), ALU.mult).then_inc(x_done, 1)

            var_sum = sems("var_sum")

            def body(lay, b, par, ahead):
                g = B * lay + b
                last = last_of_all(lay, b)
                if isinstance(b, int) and b == 0:
                    lay1, b1 = lay - 1, B - 1
                else:
                    lay1, b1 = lay, b - 1
                for jt in range(T):
                    s = T * g + jt
                    if not (is0(g) and jt < LEAD):
                        dve.wait_ge(av_done, s - LEAD + 1)
                    apart = jt in APART[lay]
                    if jt == ALONE:
                        dve.wait_ge(neg_ready, g + 1)
                        dve.wait_ge(relu_done, R * g + 1)
                        ins = nc.vector.scalar_tensor_tensor(out=mp[:, jt % LEAD, :], in0=si[:, par, :],
                                                             scalar=neg_sj[:, par, :], in1=maskT[:, jt, :],
                                                             op0=ALU.is_gt, op1=ALU.mult)
                    else:
                        k = relu_no(jt)
                        dve.wait_ge(relu_done, R * g + k + 1)
                        ins = nc.vector.tensor_tensor(mp[:, jt % LEAD, :], z[:, k % ZR, :], maskT[:, jt, :], ALU.min)
                    ins.then_inc(mp_parts if apart else mp_done, 1)
                    if apart:
                        k = APART[lay].index(jt)
                        n = (len(APART[1]) * b + len(APART[0]) * B if lay else len(APART[0]) * g) + k
                        dve.wait_ge(mp_parts, n + 1)
                        nc.vector.tensor_tensor(mn[:, :], maskT[:, jt, :], mp[:, jt % LEAD, :], ALU.subtract
                                                ).then_inc(mp_done, 1)
                    Q = NQ * g + jt // QT + 2
                    if jt % QT == 0 and not (last and jt >= 8):
                        if jt < 8:
                            values(jt // QT + 2, Q, g, par)
                        else:
                            values(jt // QT - 2, Q, g + 1, 1 - par)
                    if jt % QT == 3 and not (last and jt >= 8):
                        values_lo((jt // QT + 2) % NQ, Q)
                    if not is0(g):
                        for part, at in PART_AT[lay1]:
                            if jt == at:
                                post(g - 1, b1, lay1, 1 - par, part)
                    if ahead and jt % 2 == 0 and jt < 8:
                        split_lo(ahead[1], jt // 2, NQ * (g + 2) + jt // 2)
                    if ahead and jt in (5, 8, 11, 14):
                        keep_h(par, (jt - 5) // 3, NQ * (g + 2) + (jt - 5) // 3, g + 1)
                    if jt == 3:
                        keep_mean(g, par)
                    if not last:
                        if jt == 1:
                            tops_of(g + 1, 1 - par)
                        if jt == 3:
                            args_of(g + 1, 1 - par)
                            widen(g + 1, 1 - par)

            PART_AT = (((1, 4), (2, 5), (3, 6), (6, 10), (7, 13)),
                       ((1, 4), (2, 5), (4, 9), (5, 10), (6, 13), (7, 15)))
            mp_parts = sems("mp_parts")
            dve.wait_ge(ones_set, 3)
            nc.vector.memset(mean[:, :, :, 0:1], SM).then_inc(mean_order, 1)
            dve.wait_ge(mean_order, 1)
            nc.vector.memset(mean[LO:D, :, :, 0:1], 0.0).then_inc(mean_order, 1)
            for Q in range(2 * NQ):
                split_lo(Q // NQ, Q % NQ, Q)
                keep_h(Q // NQ, Q % NQ, Q)
            tops_of(0, 0)
            widen(0, 0)
            args_of(0, 0)
            for q in (0, 1):
                values(q, q, 0, 0)
                values_lo(q, q)
            drive(dve, body)
            for part in (1, 2, 4, 5, 6, 7):
                post(G - 1, B - 1, 1, 1, part)


class Layer0:

    def __init__(self, nc, ctx):
        def sb(name, shape, dt):
            return ctx.enter_context(nc.sbuf_tensor(name, shape, dt))

        self.a12 = sb("a12", [P, T, P], F32)
        self.h_hi = sb("h_hi", [P, T, B, D], F16)
        self.h_lo = sb("h_lo", [P, T, B, D], F16)
        self.sc1 = sb("sc1", [P, B, T], F32)
        self.c6 = sb("c6", [P, T], F32)
        self.not_last = sb("not_last", [P, 1], F32)
        self.ones = sb("ones16", [P, 2, P], F16)
        self.ones_b = sb("ones_b", [P, P], BF16)
        self.pick = sb("pick", [P, 1], F32)
        self.hsum = sb("hsum", [P, B, D], F32)
        self.stage = sb("stage", [P, NQ, QT, 512], I32)
        self.row0 = sb("row0", [P, T], I32)


def build(nc, A, out, stop_after=99):
    with ExitStack() as ctx:
        psum = ctx.enter_context(nc.psum_tensor("banks", [P, 4096], F32))
        names = {}

        def sems(name):
            assert name not in names
            names[name] = ctx.enter_context(nc.semaphore(name))
            return names[name]

        kept = Kept(nc, ctx)
        with ExitStack() as first:
            l0 = Layer0(nc, first)
            prepare(nc, kept, l0, sems, A, psum)
            layer_0(nc, kept, l0, sems, A, psum)
        if stop_after >= 1:
            layer_1(nc, kept, sems, psum)
        if stop_after >= 2:
            scratch = nc.dram_tensor("s_i_rows", (2, N), F32, kind="Internal").ap()
            layers_2_3(nc, kept, sems, psum, scratch, out)
            return
        if stop_after <= 1:
            out_done = sems("out_done")
            with nc.Block() as block:
                @block.sync
                def _(sp):
                    for b in range(B):
                        sp.dma_start(rows(out[b]), kept.x[:, b, :, :]).then_inc(out_done, 16)
                    sp.wait_ge(out_done, 16 * B)
            return


_INS = {"x": "x", "adj": "adj", "L0_gnn_W": "w0", "L0_gnn_a": "a0", "L2_gnn_W": "w2", "L2_gnn_a": "a2",
        "L3_gnn_W": "w3", "L3_gnn_a": "a3"}


def kernel(**inputs):
    import numpy as np
    import concourse.bacc as bacc
    from concourse.bass_utils import run_bass_kernel_spmd

    nc = bacc.Bacc("TRN2", target_bir_lowering=False, num_devices=1)
    arrays, A = {}, {}
    for name, short in _INS.items():
        a = np.ascontiguousarray(inputs[name])
        arrays[f"in_{short}"] = a
        A[short] = nc.dram_tensor(f"in_{short}", a.shape, mybir.dt.from_np(a.dtype), kind="ExternalInput").ap()
    out = nc.dram_tensor("out_x", (B, N, D), F32, kind="ExternalOutput").ap()
    build(nc, A, out)
    r = run_bass_kernel_spmd(nc, [arrays], core_ids=[0])
    return r.results[0]["out_x"]
```
